# Optimizing a Trainium2 kernel written in Bass

```python
import numpy as np
import jax
import jax.numpy as jnp

def _softmax(x, axis=-1):
    return jax.nn.softmax(x, axis=axis)

def _gelu(x):
    return jax.nn.gelu(x, approximate=True)

def _silu(x):
    return jax.nn.silu(x)

def _sigmoid(x):
    return jax.nn.sigmoid(x)

def _layernorm(x, axis=-1, eps=1e-05):
    m = jnp.mean(x, axis=axis, keepdims=True)
    v = jnp.var(x, axis=axis, keepdims=True)
    return (x - m) / jnp.sqrt(v + eps)

def _scatter_add(tgt, idx, src, axis=0):
    return tgt.at[idx].add(src)

def _segment_sum(src, seg, n):
    return jax.ops.segment_sum(src, seg, n)
kernel_name = 'mk_gnn_preln_d4_gnn_r8_d6638f'

def setup_inputs(seed: int=0):
    np.random.seed(seed)
    _w = jnp.asarray

    def _rec_inputs():
        import jax
        import jax.numpy as jnp
        _gk = jax.random.key(seed)
        x = 7.22e-05 + 1 * jax.random.normal(jax.random.fold_in(_gk, 1), (2048, 512), jnp.float32)
        _s = jax.random.randint(jax.random.fold_in(_gk, 2), (32768,), 0, 2048, jnp.int32)
        _d = jax.random.randint(jax.random.fold_in(_gk, 3), (32768,), 0, 2048, jnp.int32)
        _loop = jnp.arange(2048, dtype=jnp.int32)
        src = jnp.concatenate([_s, _d, _loop])
        dst = jnp.concatenate([_d, _s, _loop])
        _o = jnp.argsort(dst, stable=True)
        src = src[_o]
        dst = dst[_o]
        edge_attr_16 = -0.000585658 + 0.999949 * jax.random.normal(jax.random.fold_in(_gk, 12), (67584, 16), jnp.float32)
        edge_weight = jax.random.uniform(jax.random.fold_in(_gk, 14), (67584,), jnp.float32, 0.0, 0.999996)
        return (x, src, dst, edge_attr_16, edge_weight)
    x, src, dst, edge_attr_16, edge_weight = _rec_inputs()

    def _L0_gnn_setup():
        import jax, jax.numpy as jnp
        import numpy as np
        B = 32
        N = 512
        HID = 512
        H = 8
        E = 32768
        ED = 16
        key = jax.random.key(seed)
        ks = jax.random.split(key, 12)
        x = jax.random.normal(ks[0], (B * N, HID), jnp.float32)
        batch = jnp.repeat(jnp.arange(B, dtype=jnp.int64), N)
        g = jax.random.randint(ks[1], (E,), 0, B)
        src = g * N + jax.random.randint(ks[2], (E,), 0, N)
        dst = g * N + jax.random.randint(ks[3], (E,), 0, N)
        edge_index = jnp.stack([src, dst]).astype(jnp.int64)
        edge_attr = jax.random.normal(ks[4], (E, ED), jnp.float32)
        s = 1.0 / np.sqrt(HID).astype(np.float32)
        Wq = jax.random.normal(ks[5], (HID, HID), jnp.float32) * s
        Wk = jax.random.normal(ks[6], (HID, HID), jnp.float32) * s
        Wv = jax.random.normal(ks[7], (HID, HID), jnp.float32) * s
        Wo = jax.random.normal(ks[8], (HID, HID), jnp.float32) * s
        We = jax.random.normal(ks[9], (ED, H), jnp.float32) * (1.0 / np.sqrt(ED).astype(np.float32))
        bq = jnp.zeros((HID,), jnp.float32)
        bk = jnp.zeros((HID,), jnp.float32)
        bv = jnp.zeros((HID,), jnp.float32)
        bo = jnp.zeros((HID,), jnp.float32)
        be = jnp.zeros((H,), jnp.float32)
        return dict(x=x, batch=batch, edge_index=edge_index, edge_attr=edge_attr, Wq=Wq, bq=bq, Wk=Wk, bk=bk, Wv=Wv, bv=bv, Wo=Wo, bo=bo, We=We, be=be, num_graphs=B)
    _L0_gnn_all = _L0_gnn_setup()
    _L0_gnn_in = {k: v for k, v in _L0_gnn_all.items() if k in ('Wq', 'bq', 'Wk', 'bk', 'Wv', 'bv', 'Wo', 'bo', 'We', 'be')}
    del _L0_gnn_all

    def _L1_gnn_setup():
        import jax, jax.numpy as jnp
        import numpy as np
        N = 1250
        E = 20000
        IN = 512
        HID = 512
        OUT = 512

        def _gcn_norm(edge_index, n):
            loops = jnp.arange(n, dtype=edge_index.dtype)
            row = jnp.concatenate([edge_index[0], loops])
            col = jnp.concatenate([edge_index[1], loops])
            deg = jax.ops.segment_sum(jnp.ones_like(col, jnp.float32), col, num_segments=n)
            dis = jnp.where(deg > 0, jax.lax.rsqrt(jnp.maximum(deg, 1.0)), 0.0)
            norm = dis[row] * dis[col]
            return (row, col, norm)

        def _gcn_layer(x, row, col, norm, W, b, n):
            h = x @ W
            msg = h[row] * norm[:, None]
            out = jax.ops.segment_sum(msg, col, num_segments=n)
            return out + b
        key = jax.random.key(seed)
        ks = jax.random.split(key, 8)
        x = jax.random.normal(ks[0], (N, IN), dtype=jnp.float32)
        edge_index = jax.random.randint(ks[1], (2, E), 0, N, dtype=jnp.int64)

        def w(k, fi, fo):
            return jax.random.normal(k, (fi, fo), dtype=jnp.float32) * (1.0 / np.sqrt(fi)).astype(np.float32)
        return {'x': x, 'edge_index': edge_index, 'W1': w(ks[2], IN, HID), 'b1': jnp.zeros((HID,), jnp.float32), 'W2': w(ks[3], HID, HID), 'b2': jnp.zeros((HID,), jnp.float32), 'W3': w(ks[4], HID, OUT), 'b3': jnp.zeros((OUT,), jnp.float32)}
    _L1_gnn_all = _L1_gnn_setup()
    _L1_gnn_in = {k: v for k, v in _L1_gnn_all.items() if k in ('W1', 'b1', 'W2', 'b2', 'W3', 'b3')}
    del _L1_gnn_all

    def _L2_gnn_setup():
        import jax, jax.numpy as jnp
        import numpy as np
        N_NODES = 6250
        N_EDGES = 50000
        IN_DIM = 512
        OUT_DIM = 512
        key = jax.random.key(seed)
        k1, k2, k3, k4 = jax.random.split(key, 4)
        x = jax.random.normal(k1, (N_NODES, IN_DIM), dtype=jnp.float32)
        edge_index = jax.random.randint(k2, (2, N_EDGES), 0, N_NODES, dtype=jnp.int64)
        W = jax.random.normal(k3, (OUT_DIM, IN_DIM), dtype=jnp.float32) / np.sqrt(IN_DIM)
        b = jax.random.normal(k4, (OUT_DIM,), dtype=jnp.float32) * 0.01
        return {'x': x, 'edge_index': edge_index, 'W': W, 'b': b}
    _L2_gnn_all = _L2_gnn_setup()
    _L2_gnn_in = {k: v for k, v in _L2_gnn_all.items() if k in ('W', 'b')}
    del _L2_gnn_all

    def _L3_gnn_setup():
        import jax, jax.numpy as jnp
        import numpy as np
        N_NODES = 6250
        D_IN = 512
        D_OUT = 512
        N_EDGES = 50000
        key = jax.random.key(seed)
        k1, k2, k3, k4 = jax.random.split(key, 4)
        features = jax.random.normal(k1, (N_NODES, D_IN), dtype=jnp.float32)
        limit = float(np.sqrt(6.0 / (D_IN + D_OUT)))
        weight = jax.random.uniform(k2, (D_IN, D_OUT), dtype=jnp.float32, minval=-limit, maxval=limit)
        edge_index = jax.random.randint(k3, (2, N_EDGES), 0, N_NODES, dtype=jnp.int64)
        edge_vals = jax.random.uniform(k4, (N_EDGES,), dtype=jnp.float32)
        return {'features': features, 'weight': weight, 'edge_vals': edge_vals, 'edge_index': edge_index}
    _L3_gnn_all = _L3_gnn_setup()
    _L3_gnn_in = {k: v for k, v in _L3_gnn_all.items() if k in ('weight',)}
    del _L3_gnn_all
    return {'x': x, 'src': src, 'dst': dst, 'edge_attr_16': edge_attr_16, 'edge_weight': edge_weight, 'L0_gnn_Wq': _L0_gnn_in['Wq'], 'L0_gnn_bq': _L0_gnn_in['bq'], 'L0_gnn_Wk': _L0_gnn_in['Wk'], 'L0_gnn_bk': _L0_gnn_in['bk'], 'L0_gnn_Wv': _L0_gnn_in['Wv'], 'L0_gnn_bv': _L0_gnn_in['bv'], 'L0_gnn_Wo': _L0_gnn_in['Wo'], 'L0_gnn_bo': _L0_gnn_in['bo'], 'L0_gnn_We': _L0_gnn_in['We'], 'L0_gnn_be': _L0_gnn_in['be'], 'L1_gnn_W1': _L1_gnn_in['W1'], 'L1_gnn_b1': _L1_gnn_in['b1'], 'L1_gnn_W2': _L1_gnn_in['W2'], 'L1_gnn_b2': _L1_gnn_in['b2'], 'L1_gnn_W3': _L1_gnn_in['W3'], 'L1_gnn_b3': _L1_gnn_in['b3'], 'L2_gnn_W': _L2_gnn_in['W'], 'L2_gnn_b': _L2_gnn_in['b'], 'L3_gnn_weight': _L3_gnn_in['weight']}

def reference(x, src, dst, edge_attr_16, edge_weight, L0_gnn_Wq, L0_gnn_bq, L0_gnn_Wk, L0_gnn_bk, L0_gnn_Wv, L0_gnn_bv, L0_gnn_Wo, L0_gnn_bo, L0_gnn_We, L0_gnn_be, L1_gnn_W1, L1_gnn_b1, L1_gnn_W2, L1_gnn_b2, L1_gnn_W3, L1_gnn_b3, L2_gnn_W, L2_gnn_b, L3_gnn_weight):
    import jax
    import jax.numpy as jnp

    def _L0_gnn_ref(x, batch, edge_index, edge_attr, Wq, bq, Wk, bk, Wv, bv, Wo, bo, We, be, num_graphs):
        import jax, jax.numpy as jnp
        import numpy as np
        B = 32
        N = 512
        HID = 512
        H = 8
        E = 32768
        ED = 16
        n_total, hid = x.shape
        n = n_total // num_graphs
        hd = hid // H
        scale = 1.0 / jnp.sqrt(jnp.asarray(hd, x.dtype))
        q = (x @ Wq + bq).reshape(num_graphs, n, H, hd)
        k = (x @ Wk + bk).reshape(num_graphs, n, H, hd)
        v = (x @ Wv + bv).reshape(num_graphs, n, H, hd)
        attn = jnp.einsum('bnhd,bmhd->bnmh', q, k) * scale
        eb = edge_attr @ We + be
        b_idx = edge_index[0] // n
        loc_src = edge_index[0] % n
        loc_dst = edge_index[1] % n
        attn = attn.at[b_idx, loc_src, loc_dst].add(eb)
        attn = jax.nn.softmax(attn, axis=2)
        out = jnp.einsum('bnmh,bmhd->bnhd', attn, v).reshape(n_total, hid)
        return out @ Wo + bo

    def _L1_gnn_ref(x, edge_index, W1, b1, W2, b2, W3, b3):
        import jax, jax.numpy as jnp
        import numpy as np
        N = 1250
        E = 20000
        IN = 512
        HID = 512
        OUT = 512

        def _gcn_norm(edge_index, n):
            loops = jnp.arange(n, dtype=edge_index.dtype)
            row = jnp.concatenate([edge_index[0], loops])
            col = jnp.concatenate([edge_index[1], loops])
            deg = jax.ops.segment_sum(jnp.ones_like(col, jnp.float32), col, num_segments=n)
            dis = jnp.where(deg > 0, jax.lax.rsqrt(jnp.maximum(deg, 1.0)), 0.0)
            norm = dis[row] * dis[col]
            return (row, col, norm)

        def _gcn_layer(x, row, col, norm, W, b, n):
            h = x @ W
            msg = h[row] * norm[:, None]
            out = jax.ops.segment_sum(msg, col, num_segments=n)
            return out + b
        n = x.shape[0]
        row, col, norm = _gcn_norm(edge_index, n)
        h = _gcn_layer(x, row, col, norm, W1, b1, n)
        h = jax.nn.relu(h)
        h = _gcn_layer(h, row, col, norm, W2, b2, n)
        h = jax.nn.relu(h)
        h = _gcn_layer(h, row, col, norm, W3, b3, n)
        return h

    def _L2_gnn_ref(x, edge_index, W, b):
        import jax, jax.numpy as jnp
        import numpy as np
        N_NODES = 6250
        N_EDGES = 50000
        IN_DIM = 512
        OUT_DIM = 512
        n = x.shape[0]
        loops = jnp.arange(n, dtype=edge_index.dtype)
        row = jnp.concatenate([edge_index[0], loops])
        col = jnp.concatenate([edge_index[1], loops])
        deg = jax.ops.segment_sum(jnp.ones(row.shape[0], dtype=x.dtype), row, num_segments=n)
        dis = jax.lax.rsqrt(deg)
        norm = dis[row] * dis[col]
        h = x @ W.T + b
        out = jax.ops.segment_sum(norm[:, None] * h[row], col, num_segments=n)
        return jax.nn.relu(out)

    def _L3_gnn_ref(features, weight, edge_vals, edge_index):
        import jax, jax.numpy as jnp
        import numpy as np
        N_NODES = 6250
        D_IN = 512
        D_OUT = 512
        N_EDGES = 50000
        support = features @ weight
        row, col = (edge_index[0], edge_index[1])
        msgs = support[col] * edge_vals[:, None]
        output = jax.ops.segment_sum(msgs, row, num_segments=features.shape[0])
        return jax.nn.relu(output)
    edge_index = jnp.stack([src, dst])
    batch0 = jnp.zeros((2048,), jnp.int32)
    h = jnp.maximum(_layernorm(x, axis=-1), 0.0)
    x = x + _L0_gnn_ref(h, batch0, edge_index, edge_attr_16, L0_gnn_Wq, L0_gnn_bq, L0_gnn_Wk, L0_gnn_bk, L0_gnn_Wv, L0_gnn_bv, L0_gnn_Wo, L0_gnn_bo, L0_gnn_We, L0_gnn_be, 32)
    h = jnp.maximum(_layernorm(x, axis=-1), 0.0)
    x = x + _L1_gnn_ref(h, edge_index, L1_gnn_W1, L1_gnn_b1, L1_gnn_W2, L1_gnn_b2, L1_gnn_W3, L1_gnn_b3)
    h = jnp.maximum(_layernorm(x, axis=-1), 0.0)
    x = x + _L2_gnn_ref(h, edge_index, L2_gnn_W, L2_gnn_b)
    h = jnp.maximum(_layernorm(x, axis=-1), 0.0)
    x = x + _L3_gnn_ref(h, L3_gnn_weight, edge_weight, edge_index)
    return x

_drawn_inputs = setup_inputs


def setup_inputs(seed=0):
    import zlib

    import numpy as np

    out = dict(_drawn_inputs(seed))
    spreads = {'L0_gnn_bq': (0.0, 0.8),
     'L0_gnn_bk': (0.0, 2.0),
     'L0_gnn_bv': (0.0, 0.1),
     'L0_gnn_bo': (0.0, 0.1),
     'L0_gnn_be': (0.0, 2.0),
     'L1_gnn_b1': (0.0, 0.1),
     'L1_gnn_b2': (0.0, 0.1),
     'L1_gnn_b3': (0.0, 0.1)}
    factors = {'L0_gnn_Wq': 3.816, 'L0_gnn_Wk': 3.906, 'L2_gnn_b': 7.497}
    for name, (base, spread) in spreads.items():
        noise = np.random.default_rng([zlib.crc32(name.encode()), seed]).standard_normal(out[name].shape)
        drawn = base * np.exp(spread * noise) if base else spread * noise
        out[name] = jnp.asarray(drawn.astype(out[name].dtype))
    for name, factor in factors.items():
        out[name] = (out[name] * factor).astype(out[name].dtype)
    return out
```

```python
from contextlib import ExitStack

import numpy as np
import concourse.bass as bass
from concourse import mybir
from concourse.alu_op_type import AluOpType as ALU

F32, BF16, F16 = mybir.dt.float32, mybir.dt.bfloat16, mybir.dt.float16
I32, U32 = mybir.dt.int32, mybir.dt.uint32
ACT = mybir.ActivationFunctionType
AX = mybir.AxisListType

P = 128
N = 2048
D = 512
E = 67584
ED = 16
H = 8
HD = D // H
GN = 64
NT = N // P
KT = D // P
NGRAPH = N // GN

PARTS = 3
GROUP_DSTS = 2
PAIRS = GN // GROUP_DSTS
NGROUP = N // GROUP_DSTS
GTILES = NGROUP // P
PPT = PAIRS // GTILES
BATCH = 16
NBATCH = P // BATCH
BLK = 16
EPP = E // P
BPP = EPP // BLK
NBLK = E // BLK
FIELDS = 3 + H
REC = FIELDS * BLK
WIN = P // BLK
SB16 = 16
SHI = N // SB16
CCOLS = GROUP_DSTS * NT
BCOLS = GROUP_DSTS * SHI
ROUNDS_MAX = E // P + 1
LN_EPS = 1e-5


class Signals:

    def __init__(self, nc, name):
        self.sem, self.value, self.seen = nc.alloc_semaphore(name), 0, {}

    def of(self, instruction, by=1):
        instruction.then_inc(self.sem, by)
        self.value += by
        return self, self.value


def wait(engine, *marks):
    for mark in marks:
        if mark is None:
            continue
        if isinstance(mark, list):
            wait(engine, *mark)
            continue
        signals, value = mark
        if signals.seen.get(id(engine), 0) < value:
            engine.wait_ge(signals.sem, value)
            signals.seen[id(engine)] = value


def make_identity(nc, keep):
    made = Signals(nc, "identity")
    a = made.of(nc.gpsimd.memset(keep["ident"][:], 0.0))
    wait(nc.gpsimd, a)
    made.of(nc.gpsimd.affine_select(out=keep["ident"][:], in_=keep["ident"][:], compare_op=ALU.not_equal, fill=1.0, base=0,
                                    pattern=[[-1, P]], channel_multiplier=1))
    nc.all_engine_barrier()


def edge_prep(nc, io, keep):
    pe, dve, act, pool, sp = nc.tensor, nc.vector, nc.scalar, nc.gpsimd, nc.sync
    by_pe, by_dve, by_act, by_pool = (Signals(nc, f"prep_{x}") for x in ("pe", "dve", "act", "pool"))
    with ExitStack() as mem:
        sb = lambda *a: mem.enter_context(nc.sbuf_tensor(*a))
        ps = lambda *a: mem.enter_context(nc.psum_tensor(*a))
        attr = sb("attr", [P, EPP * ED], F32)
        rec = sb("rec", [P, EPP, FIELDS], F32)
        src_i = sb("src_i", [P, EPP], I32)
        dst_i = sb("dst_i", [P, EPP], I32)
        dst_next = sb("dst_next", [P, EPP], I32)
        step_f = sb("step_f", [P, EPP], F32)
        graph_i = sb("graph_i", [P, EPP], I32)
        pair_i = sb("pair_i", [P, EPP], I32)
        graph_key = sb("graph_key", [P, EPP], BF16)
        pair_key = sb("pair_key", [P, EPP], BF16)
        ew = sb("ew", [P, EPP], F32)
        we_diag = sb("we_diag", [P, H, 8], F32)
        be_row = sb("be_row", [P, H], F32)
        attr_t = sb("attr_t", [P, 2, 512], F32)
        iota_hist = sb("iota_hist", [P, PAIRS, 66], BF16)
        graph_hot = sb("graph_hot", [P, 2, PAIRS, 66], BF16)
        pair_hot = sb("pair_hot", [P, 2, PAIRS, 66], BF16)
        pad = sb("pad", [1, REC], F32)
        small = sb("small", [P, 640], F32)
        small_i = sb("small_i", [P, 160], I32)
        turn_ps = ps("turn_ps", [P, 2, 512], F32)
        eb_ps = ps("eb_ps", [P, 2, 512], F32)
        hist_ps = ps("hist_ps", [P, 512], F32)
        misc_ps = ps("misc_ps", [P, 512], F32)
        in_src, in_dst, in_attr, in_w, in_we = (Signals(nc, f"in_{x}") for x in ("src", "dst", "attr", "w", "we"))
        got_dst = in_dst.of(sp.dma_start(dst_i[:], io["dst"].rearrange("(p j) -> p j", p=P)), 16)
        last = P - 1
        got_src = in_src.of(sp.dma_start(src_i[:], io["src"].rearrange("(p j) -> p j", p=P)), 16)
        got_w = in_w.of(sp.dma_start(ew[:], io["edge_weight"].rearrange("(p j) -> p j", p=P)), 16)
        we_zero = by_dve.of(dve.memset(we_diag[:], 0.0))
        wait(sp, we_zero)
        with nc.allow_non_contiguous_dma(reason="a 16 x 8 matrix"):
            for e in range(8):
                got_we = in_we.of(sp.dma_start(we_diag[e * ED:(e + 1) * ED, :, e], io["L0_gnn_We"]), 16)
        got_we = in_we.of(sp.dma_start(be_row[:], io["L0_gnn_be"].unsqueeze(0).to_broadcast([P, H])), 16)
        got_attr = in_attr.of(act.dma_start(attr[:], io["edge_attr_16"].rearrange("(p j) f -> p (j f)", p=P)), 16)
        filled = by_dve.of(dve.memset(dst_next[:], N))
        wait(sp, filled)
        in_next = Signals(nc, "in_next")
        in_next.of(sp.dma_start(dst_next[0:last, :], io["dst"][1:1 + last * EPP].rearrange("(p j) -> p j", p=last)), 16)
        got_next = in_next.of(sp.dma_start(dst_next[last:P, 0:EPP - 1], io["dst"][1 + last * EPP:E].unsqueeze(0)), 16)

        made_iota = by_pool.of(pool.iota(iota_hist[:], pattern=[[1, PAIRS], [0, 66]], base=0, channel_multiplier=0, allow_small_or_imprecise_dtypes=True))
        wait(dve, made_iota, got_dst)
        g_i = by_dve.of(dve.tensor_scalar(graph_i[:], dst_i[:], 6, None, ALU.logical_shift_right))
        p_i = by_dve.of(dve.tensor_scalar(pair_i[:], dst_i[:], 1, PAIRS - 1, ALU.logical_shift_right, ALU.bitwise_and))
        wait(dve, p_i)
        by_dve.of(dve.tensor_copy(graph_key[:], graph_i[:]))
        keys = by_dve.of(dve.tensor_copy(pair_key[:], pair_i[:]))
        wait(dve, keys)
        used = [None, None]
        for c in range(EPP // 66):
            wait(dve, used[c % 2])
            cols = slice(c * 66, (c + 1) * 66)
            bc = [P, PAIRS, 66]
            by_dve.of(dve.tensor_tensor(graph_hot[:, c % 2], iota_hist[:], graph_key[:, cols].unsqueeze(1).to_broadcast(bc), ALU.is_equal))
            hots = by_dve.of(dve.tensor_tensor(pair_hot[:, c % 2], iota_hist[:], pair_key[:, cols].unsqueeze(1).to_broadcast(bc), ALU.is_equal))
            wait(pe, hots)
            for j in range(66):
                mm = pe.matmul(hist_ps[0:NGRAPH, 0:PAIRS], graph_hot[:, c % 2, :, j], pair_hot[:, c % 2, :, j],
                               start=c == 0 and j == 0, stop=c == EPP // 66 - 1 and j == 65)
            used[c % 2] = by_pe.of(mm)

        cnt, ones, base, end, first = (small[0:NGRAPH, i * PAIRS:(i + 1) * PAIRS] for i in range(5))
        row, viol, flag, rounds, span_max = (small[:, 160 + i:161 + i] for i in range(5))
        low = small[:, 176:176 + PAIRS]
        start_i, span_i = (small_i[0:NGRAPH, i * PAIRS:(i + 1) * PAIRS] for i in range(2))
        start_f = small[0:NGRAPH, 224:224 + PAIRS]
        wait(dve, used[(EPP // 66 - 1) % 2])
        a = by_dve.of(dve.tensor_copy(cnt, hist_ps[0:NGRAPH, 0:PAIRS]))
        by_dve.of(dve.memset(ones, 1.0))
        b = by_dve.of(dve.memset(low, 1.0))
        wait(dve, a, b)
        a = by_dve.of(dve.tensor_reduce(row[0:NGRAPH], cnt, axis=AX.X, op=ALU.add))
        wait(pool, b)
        lowered = by_pool.of(pool.affine_select(out=low[0:NGRAPH], in_=low[0:NGRAPH], compare_op=ALU.is_gt, fill=0.0, base=0,
                                                pattern=[[1, PAIRS]], channel_multiplier=-1))
        wait(pe, a, lowered)
        c0 = by_pe.of(pe.matmul(misc_ps[0:NGRAPH, 0:1], low[0:NGRAPH], row[0:NGRAPH], start=True, stop=True))
        wait(dve, c0)
        a = by_dve.of(dve.tensor_copy(base[:, 0:1], misc_ps[0:NGRAPH, 0:1]))
        wait(dve, a)
        a = by_dve.of(dve.tensor_tensor_scan(end, ones, cnt, base[:, 0:1], ALU.mult, ALU.add))
        wait(dve, a)
        a = by_dve.of(dve.tensor_tensor(first, end, cnt, ALU.subtract))
        wait(dve, a)
        a = by_dve.of(dve.tensor_copy(start_i, first))
        wait(dve, a)
        a = by_dve.of(dve.tensor_scalar(start_i, start_i, 4, None, ALU.logical_shift_right))
        wait(dve, a)
        a = by_dve.of(dve.tensor_copy(start_f, start_i))
        wait(dve, a)
        a = by_dve.of(dve.scalar_tensor_tensor(first, start_f, -float(BLK), end, ALU.mult, ALU.add))
        wait(dve, a)
        a = by_dve.of(dve.tensor_scalar(span_i, first, float(P - 1), None, ALU.add))
        wait(dve, a)
        a = by_dve.of(dve.tensor_scalar(span_i, span_i, 7, None, ALU.logical_shift_right))
        wait(dve, a)
        a = by_dve.of(dve.memset(span_max, 0.0))
        wait(dve, a)
        a = by_dve.of(dve.tensor_reduce(span_max[0:NGRAPH], span_i, axis=AX.X, op=ALU.max))
        wait(dve, got_next)
        b = by_dve.of(dve.tensor_tensor(step_f[:], dst_i[:], dst_next[:], ALU.subtract))
        wait(dve, b)
        b = by_dve.of(dve.tensor_reduce(viol, step_f[:], axis=AX.X, op=ALU.max))
        wait(pool, a, b)
        RMAX = bass.bass_isa.ReduceOp.max
        viol_all, span_all = small[:, 165:166], small[:, 166:167]
        by_pool.of(pool.partition_all_reduce(viol_all, viol, P, RMAX))
        alls = by_pool.of(pool.partition_all_reduce(span_all, span_max, P, RMAX))
        wait(dve, alls)
        a = by_dve.of(dve.tensor_scalar(flag, viol_all, 0.0, None, ALU.is_le))
        b = by_dve.of(dve.tensor_scalar(rounds, span_all, 1.0, -float(E // P), ALU.max, ALU.add))
        wait(dve, a, b)
        a = by_dve.of(dve.tensor_tensor(rounds, rounds, flag, ALU.mult))
        b = by_dve.of(dve.tensor_scalar(start_f, start_f, flag[0:NGRAPH], None, ALU.mult))
        wait(dve, a, b)
        keep["rounds_set"] = by_dve.of(dve.tensor_scalar(keep["rounds"][0:1, :], rounds[0:1], float(E // P), None, ALU.add))
        ident = keep["ident"]
        wait(pe, b)
        spread = start_f.rearrange("b (t q) -> b q t", q=PPT)
        for q in range(PPT):
            mm = pe.matmul(misc_ps[q * NGRAPH:(q + 1) * NGRAPH, 8:8 + GTILES], ident[0:NGRAPH, 0:NGRAPH], spread[:, q, :], start=True, stop=True)
        c0 = by_pe.of(mm)
        blk_i = small_i[:, 64:64 + WIN]
        blk_f = small[:, 256:256 + WIN]
        k0 = by_pool.of(pool.iota(blk_i, pattern=[[1, WIN]], base=0, channel_multiplier=0))
        wait(dve, k0, c0)
        a = by_dve.of(dve.tensor_copy(blk_f, blk_i))
        wait(dve, a)
        by_dve.of(dve.tensor_tensor(keep["blocks"][:], misc_ps[:, 8:8 + GTILES].unsqueeze(2).to_broadcast([P, GTILES, WIN]),
                                    blk_f.unsqueeze(1).to_broadcast([P, GTILES, WIN]), ALU.add))

        wait(dve, got_src, got_w)
        by_dve.of(dve.tensor_copy(rec[:, :, 0], src_i[:]))
        by_dve.of(dve.tensor_copy(rec[:, :, 1], dst_i[:]))
        by_dve.of(dve.tensor_copy(rec[:, :, 2], ew[:]))
        padded = by_dve.of(dve.memset(pad[:], -1.0))
        wait(sp, padded)
        out_rec = Signals(nc, "out_rec")
        out_rec.of(sp.dma_start(io["rec_dram"][NBLK:NBLK + 1, :], pad[:]), 16)
        nblk8 = EPP // 8
        per = 4
        wait(pe, got_attr, got_we)
        wait(dve, got_we)
        turned_free, eb_free, attr_t_free = [None, None], [None, None], [None, None]
        for i0 in range(0, nblk8, 8):
            n = min(8, nblk8 - i0)
            e = (i0 // 8) % 2
            for j0 in range(0, n, per):
                m = min(per, n - j0)
                s = (j0 // per) % 2
                wait(pe, turned_free[s])
                for j in range(m):
                    i = i0 + j0 + j
                    mm = pe.transpose(turn_ps[:, s, j * P:(j + 1) * P], attr[:, i * P:(i + 1) * P], ident[:])
                t = by_pe.of(mm)
                wait(act, t, attr_t_free[s])
                turned_free[s] = by_act.of(act.copy(attr_t[:, s, 0:m * P], turn_ps[:, s, 0:m * P]))
                wait(pe, turned_free[s])
                if j0 == 0:
                    wait(pe, eb_free[e])
                for j in range(m):
                    mm = pe.matmul(eb_ps[:, e, (j0 + j) * 64:(j0 + j + 1) * 64], attr_t[:, s, j * P:(j + 1) * P],
                                   we_diag[:].rearrange("p h e -> p (h e)"), start=True, stop=True)
                attr_t_free[s] = by_pe.of(mm)
            wait(dve, attr_t_free[s])
            eb = eb_ps[:, e, 0:n * 64].rearrange("p (b h e) -> p b e h", h=H, e=8)
            out = rec[:, i0 * 8:(i0 + n) * 8, 3:3 + H].rearrange("p (b e) h -> p b e h", e=8)
            eb_free[e] = by_dve.of(dve.tensor_tensor(out, eb, be_row[:].unsqueeze(1).unsqueeze(1).to_broadcast([P, n, 8, H]), ALU.add))
        wait(sp, eb_free[0], eb_free[1])
        wait(sp, eb_free[((nblk8 - 1) // 8) % 2])
        stored = out_rec.of(sp.dma_start(io["rec_dram"][0:NBLK, :].rearrange("(p b) r -> p (b r)", p=P),
                                         rec[:].rearrange("p j f -> p (j f)")), 16)
        wait(sp, stored)
        nc.all_engine_barrier()


def build_matrices(nc, io, keep):
    pe, dve, act, pool, sp = nc.tensor, nc.vector, nc.scalar, nc.gpsimd, nc.sync
    ident, count, bias, blocks = keep["ident"], keep["count"], keep["bias"], keep["blocks"]
    names = ("pe", "dve", "act", "pool", "gather", "old", "store0", "store1")
    signals = {}
    for n in names:
        signals[n] = Signals(nc, f"build_{n}")
    nums = [signals[n].sem.num for n in names]
    assert nums == list(range(nums[0], nums[0] + len(nums)))
    by_pe, by_dve, by_act, by_pool = (signals[x] for x in ("pe", "dve", "act", "pool"))
    once = Signals(nc, "build_once")

    with ExitStack() as mem:
        sb = lambda *a: mem.enter_context(nc.sbuf_tensor(*a))
        ps = lambda *a: mem.enter_context(nc.psum_tensor(*a))
        gathered = sb("gathered", [P, WIN, REC], F32)
        fields = sb("fields", [P, FIELDS, P], F32)
        d0 = sb("d0", [P, P], F32)
        ints = sb("ints", [P, 5, P], I32)
        dlocal = sb("dlocal", [P, P], F32)
        keys = sb("keys", [P, 2, 4, P], BF16)
        eb_parts = sb("eb_parts", [P, 2, PARTS, H + 1, P], BF16)
        idx_f = sb("idx_f", [P, GTILES * WIN], F32)
        idx = sb("idx", [P, GTILES * WIN], U32)
        iota_rep = sb("iota_rep", [P, BCOLS, BATCH], BF16)
        place = keep["x"][:].rearrange("p t d -> p (t d)").bitcast(BF16)
        n_src = 2 * P * BATCH
        hot_src = place[:, 0:n_src].rearrange("p (z c g) -> p z c g", z=2, g=BATCH)
        hot_eb = place[:, n_src:n_src + 2 * PARTS * H * SB16 * BATCH].rearrange("p (z h s g) -> p z h s g", z=2, s=SB16, g=BATCH)
        hot_bias = sb("hot_bias", [P, 2, BCOLS, BATCH], BF16)
        hot16 = sb("hot16", [P, 2, SB16, BATCH], BF16)
        hot_cnt = sb("hot_cnt", [P, 2, CCOLS, BATCH], BF16)
        hot_w = sb("hot_w", [P, 2, PARTS, CCOLS, BATCH], BF16)
        w_slab = sb("w_slab", [P, P, NT], F32)
        w_old = sb("w_old", [P, 512], F32)
        w_new = sb("w_new", [P, 2, 512], F32)
        turn_ps = ps("turn2_ps", [P, 2, 512], F32)
        cnt_ps = ps("cnt_ps", [P, 2, 512], F32)
        w_ps = ps("w_ps", [P, 2, 512], F32)
        bias_ps = ps("bias_ps", [P, 2, 512], F32)
        once.of(pool.iota(d0[:], pattern=[[GROUP_DSTS, PPT], [GN, NGRAPH]], base=0, channel_multiplier=0, allow_small_or_imprecise_dtypes=True))
        once.of(pool.iota(iota_rep[:], pattern=[[1, BCOLS], [0, BATCH]], base=0, channel_multiplier=0, allow_small_or_imprecise_dtypes=True))
        once.of(dve.memset(w_old[:], 0.0))
        once.of(dve.memset(count[:], 0.0))
        once.of(pool.memset(bias[:], 0.0))
        nc.all_engine_barrier()
        rounds = nc.values_load(keep["rounds"][0:1, :], min_val=1, max_val=ROUNDS_MAX)
        with nc.Fori(0, rounds) as r:
            a = by_dve.of(dve.tensor_scalar(idx_f[:], blocks[:].rearrange("p t k -> p (t k)"), float(NBLK), None, ALU.min))
            wait(dve, a)
            indexed = by_dve.of(dve.tensor_copy(idx[:], idx_f[:]))
            by_dve.of(dve.tensor_scalar(blocks[:], blocks[:], float(WIN), None, ALU.add))

            gather_read = [None]
            turned_free = [None, None]
            fields_free = None
            parts_done = [None, None]
            parts_free = [(), ()]
            got = [None]

            def gather(t):
                wait(pool, indexed, gather_read[0])
                for k in range(WIN):
                    g = pool.indirect_dma_start(gathered[:, k, :], None, io["rec_dram"],
                                                bass.IndirectOffsetOnAxis(ap=idx[:, t * WIN + k:t * WIN + k + 1], axis=0))
                    got[0] = signals["gather"].of(g, 16)

            def prep(t):
                nonlocal fields_free
                s = t % 2
                wait(pe, got[0])
                view = gathered[:].rearrange("p k (e f) -> p f (k e)", f=FIELDS)
                evacuated = None
                for f0 in range(0, FIELDS, 4):
                    n = min(4, FIELDS - f0)
                    bank = (f0 // 4) % 2
                    wait(pe, turned_free[bank])
                    for f in range(n):
                        mm = pe.transpose(turn_ps[:, bank, f * P:(f + 1) * P], view[:, f0 + f], ident[:])
                    gather_read[0] = by_pe.of(mm)
                    wait(act, gather_read[0], fields_free)
                    evacuated = turned_free[bank] = by_act.of(act.copy(
                        fields[:, f0:f0 + n, :], turn_ps[:, bank, 0:n * P].rearrange("p (f g) -> p f g", f=n)))
                wait(dve, evacuated, *parts_free[s])
                a = by_dve.of(dve.tensor_copy(ints[:, 0], fields[:, 0, :]))
                b = by_dve.of(dve.scalar_tensor_tensor(dlocal[:], fields[:, 1, :], -float(t * PPT * GROUP_DSTS), d0[:], ALU.add, ALU.subtract))
                wait(dve, a)
                by_dve.of(dve.tensor_scalar(ints[:, 1], ints[:, 0], P - 1, None, ALU.bitwise_and))
                by_dve.of(dve.tensor_scalar(ints[:, 2], ints[:, 0], 7, None, ALU.logical_shift_right))
                by_dve.of(dve.tensor_scalar(ints[:, 3], ints[:, 0], SB16 - 1, None, ALU.bitwise_and))
                a = by_dve.of(dve.tensor_scalar(ints[:, 4], ints[:, 0], 4, None, ALU.logical_shift_right))
                wait(dve, a)
                by_dve.of(dve.tensor_copy(keys[:, s, 0], ints[:, 1]))
                by_dve.of(dve.tensor_copy(keys[:, s, 1], ints[:, 3]))
                by_dve.of(dve.scalar_tensor_tensor(keys[:, s, 2], dlocal[:], float(NT), ints[:, 2], ALU.mult, ALU.add))
                last = by_dve.of(dve.scalar_tensor_tensor(keys[:, s, 3], dlocal[:], float(SHI), ints[:, 4], ALU.mult, ALU.add))
                wait(act, evacuated, *parts_free[s])
                source = fields[:, 2:FIELDS, :]
                p0 = by_act.of(act.copy(eb_parts[:, s, 0], source))
                wait(pool, p0, evacuated)
                p1 = by_pool.of(pool.tensor_tensor(source, source, eb_parts[:, s, 0], ALU.subtract))
                wait(act, p1)
                p2 = by_act.of(act.copy(eb_parts[:, s, 1], source))
                wait(pool, p2)
                p3 = by_pool.of(pool.tensor_tensor(source, source, eb_parts[:, s, 1], ALU.subtract))
                wait(act, p3)
                p4 = by_act.of(act.copy(eb_parts[:, s, 2], source))
                wait(act, last)
                parts_done[s] = (last, p4)
                fields_free = p4
                wait(act, last)

            hot_free = [None, None]
            ps_free = [(), ()]
            bias_free = [None, None]
            slab_free = [None]
            made = {}

            def hots(t, i):
                n = t * NBATCH + i
                s, ts = n % 2, t % 2
                cols = slice(i * BATCH, (i + 1) * BATCH)

                def key(k, c):
                    return keys[:, ts, k, cols].unsqueeze(1).to_broadcast([P, c, BATCH])
                wait(dve, hot_free[s], *parts_done[ts])
                a16 = by_dve.of(dve.tensor_tensor(hot16[:, s], iota_rep[:, 0:SB16], key(1, SB16), ALU.is_equal))
                acn = by_dve.of(dve.tensor_tensor(hot_cnt[:, s], iota_rep[:, 0:CCOLS], key(2, CCOLS), ALU.is_equal))
                wait(pool, hot_free[s], acn, *parts_done[ts])

                def product(eng, by, p):
                    return by.of(eng.tensor_tensor(
                        hot_eb[:, s, p * H:(p + 1) * H], hot16[:, s].unsqueeze(1).to_broadcast([P, H, SB16, BATCH]),
                        eb_parts[:, ts, p, 1:1 + H, cols].unsqueeze(2).to_broadcast([P, H, SB16, BATCH]), ALU.mult))
                w = by_pool.of(pool.tensor_tensor(
                    hot_w[:, s], hot_cnt[:, s].unsqueeze(1).to_broadcast([P, PARTS, CCOLS, BATCH]),
                    eb_parts[:, ts, :, 0, cols].unsqueeze(2).to_broadcast([P, PARTS, CCOLS, BATCH]), ALU.mult))
                e2 = product(pool, by_pool, 2)
                by_dve.of(dve.tensor_tensor(hot_src[:, s], iota_rep[:, 0:P], key(0, P), ALU.is_equal))
                by_dve.of(dve.tensor_tensor(hot_bias[:, s], iota_rep[:], key(3, BCOLS), ALU.is_equal))
                wait(dve, a16)
                product(dve, by_dve, 0)
                e1 = product(dve, by_dve, 1)
                made[n] = (e1, e2)
                parts_free[ts] = (e1, e2)

            def products(t, i):
                n = t * NBATCH + i
                s = n % 2
                pair = n // 2
                half = n % 2
                bank = pair % 2
                wait(pe, *made[n], *ps_free[s])
                if half == 0:
                    wait(pe, bias_free[bank])
                for g in range(BATCH):
                    hs = hot_src[:, s, :, g]
                    c = slice(g * CCOLS, (g + 1) * CCOLS)
                    pe.matmul(cnt_ps[:, s, c], hs, hot_cnt[:, s, :, g], start=True, stop=True)
                    for p in range(PARTS):
                        pe.matmul(w_ps[:, s, c], hs, hot_w[:, s, p, :, g], start=p == 0, stop=p == PARTS - 1)
                    for p in range(PARTS):
                        mm = pe.matmul(bias_ps[:, bank, 0:BCOLS], hot_eb[:, s, p * H:(p + 1) * H, :, g].rearrange("p h s -> p (h s)"),
                                       hot_bias[:, s, :, g], start=half == 0 and g == 0 and p == 0,
                                       stop=half == 1 and g == BATCH - 1 and p == PARTS - 1)
                hot_free[s] = by_pe.of(mm)
                done = hot_free[s]
                wait(dve, done)
                half_b = slice(half * BATCH, (half + 1) * BATCH)
                c_view = count[:].rearrange("p s (b m) -> p b m s", m=GN)[:, half_b, GROUP_DSTS * pair:GROUP_DSTS * pair + 2, :]
                ps_view = cnt_ps[:, s].rearrange("p (b m s) -> p b m s", m=GROUP_DSTS, s=NT)
                c1 = by_dve.of(dve.tensor_tensor(c_view, ps_view, c_view, ALU.add))
                wait(act, done, slab_free[0])
                w_at = (pair % 2) * GROUP_DSTS * NGRAPH + half * GROUP_DSTS * BATCH
                c2 = by_act.of(act.copy(w_slab[:, w_at:w_at + GROUP_DSTS * BATCH, :].rearrange("p d s -> p (d s)"), w_ps[:, s]))
                ps_free[s] = (c1, c2)
                if half == 1:
                    b_view = bias[:].rearrange("p i m -> p m i")[:, GROUP_DSTS * pair:GROUP_DSTS * pair + 2, :]
                    bias_free[bank] = by_dve.of(dve.tensor_tensor(
                        b_view, bias_ps[:, bank, 0:BCOLS].rearrange("p (m i) -> p m i", m=GROUP_DSTS), b_view, ALU.add))
                return c2

            new_free = [None, None]
            old_free = [None]

            def weight_rows(q, slab_done):
                wait(pe, slab_done)
                for c in range(NT // 4):
                    cols = slice(c * 512, (c + 1) * 512)
                    bank = c % 2
                    wait(pe, turned_free[bank])
                    for s1 in range(4):
                        mm = pe.transpose(turn_ps[:, bank, s1 * P:(s1 + 1) * P], w_slab[:, :, c * 4 + s1], ident[:])
                    t = by_pe.of(mm)
                    wait(sp, old_free[0])
                    old = signals["old"].of(sp.dma_start(w_old[:], io["weight_dram"][q, :, cols], cond=(r > 0)), 16)
                    wait(dve, t, old, new_free[bank])
                    turned_free[bank] = by_dve.of(dve.tensor_tensor(w_new[:, bank], turn_ps[:, bank], w_old[:], ALU.add))
                    old_free[0] = turned_free[bank]
                    wait(sp, turned_free[bank])
                    new_free[bank] = signals[f"store{bank}"].of(sp.dma_start(io["weight_dram"][q, :, cols], w_new[:, bank]), 16)
                slab_free[0] = t


            gather(0)
            prep(0)
            gather(1)
            hots(0, 0)
            for t in range(GTILES):
                for i in range(NBATCH):
                    n = t * NBATCH + i
                    if i == NBATCH - 1 and t + 1 < GTILES:
                        hots(t + 1, 0)
                    elif i + 1 < NBATCH:
                        hots(t, i + 1)
                    c2 = products(t, i)
                    if i == 3 and t + 1 < GTILES:
                        prep(t + 1)
                        if t + 2 < GTILES:
                            gather(t + 2)
                    if i % 4 == 3:
                        weight_rows(n // 4, c2)
            wait(sp, *((signals[x], signals[x].value) for x in ("old", "store0", "store1")))
            nc.all_engine_barrier()
            pool.dma_reset(range(nums[0], nums[-1] + 1))
            pool.sem_clear(range(nums[0], nums[-1] + 1))
            nc.all_engine_barrier()


def layer_norm_scales(nc, by_dve, by_act, x, x_ready, stats, rstd, shift):
    dve, act = nc.vector, nc.scalar
    moments = stats[:, 6 * NT:8 * NT].rearrange("p (t two) -> p t two", two=2)
    for t in range(NT):
        wait(dve, x_ready[t])
        mark = by_dve.of(dve.bn_stats(stats[:, 6 * t:6 * t + 6], x[:, t, :]))
    wait(dve, mark)
    for t in range(NT):
        mark = by_dve.of(dve.bn_aggr(moments[:, t, :], stats[:, 6 * t:6 * t + 6]))
    wait(dve, mark)
    mark = by_dve.of(dve.tensor_scalar(rstd[:], moments[:, :, 1], LN_EPS, None, ALU.add))
    wait(act, mark)
    mark = by_act.of(act.sqrt(rstd[:], rstd[:]))
    wait(dve, mark)
    mark = by_dve.of(dve.reciprocal(rstd[:], rstd[:]))
    wait(dve, mark)
    return by_dve.of(dve.scalar_tensor_tensor(shift[:], moments[:, :, 0], -1.0, rstd[:], ALU.mult, ALU.mult))


def weight_view(w):
    return w.rearrange("(k p) n -> p k n", p=P)


def column_view(v):
    return v.rearrange("(k p) -> p k", p=P)


def attention(nc, io, keep):
    pe, dve, act, pool, sp = nc.tensor, nc.vector, nc.scalar, nc.gpsimd, nc.sync
    ident, bias, x = keep["ident"], keep["bias"], keep["x"]
    by_pe, by_dve, by_act, by_pool = (Signals(nc, f"att_{n}") for n in ("pe", "dve", "act", "pool"))
    with ExitStack() as mem:
        sb = lambda *a: mem.enter_context(nc.sbuf_tensor(*a))
        ps = lambda *a: mem.enter_context(nc.psum_tensor(*a))
        wq, wk, wv, wo = (sb(f"w{n}_sb", [P, KT, D], F32) for n in "qkvo")
        bq_col, bk_col = (sb(f"b{n}_col", [P, KT], F32) for n in "qk")
        bv_row, bo_row = (sb(f"b{n}_row", [P, D], F32) for n in "vo")
        stats, rstd, shift = sb("stats0", [P, 8 * NT], F32), sb("rstd0", [P, NT], F32), sb("shift0", [P, NT], F32)
        h = sb("h0", [P, D], F32)
        h_t = sb("h0_t", [P, KT, 2 * P], F32)
        q_split = sb("q_split", [P, KT, 2 * P // SB16, 2, SB16], F32)
        k_t = sb("k_t", [P, KT, 2 * P], F32)
        v = sb("v", [P, 2, 2, D], F32)
        prob = sb("prob", [P, 2, D], F32)
        prob_t = sb("prob_t", [P, D], F32)
        att_t = sb("att_t", [P, KT, P], F32)
        row_max, row_sum = sb("row_max", [P, 2, 8], F32), sb("row_sum", [P, 2, 8], F32)
        turn_ps = ps("turn3_ps", [P, 512], F32)
        proj_ps = ps("proj_ps", [P, 2, 512], F32)
        s_ps = ps("s_ps", [P, 2, 512], F32)
        pt_ps = ps("pt_ps", [P, 512], F32)
        av_ps = ps("av_ps", [P, 2, 512], F32)

        in_x = [Signals(nc, f"in_x{i}") for i in range(4)]
        x_ready = [None] * NT
        x_view = io["x"].rearrange("(t p) d -> p t d", p=P)
        for i in range(4):
            got = in_x[i].of(sp.dma_start(x[:, 4 * i:4 * i + 4, :], x_view[:, 4 * i:4 * i + 4, :]), 16)
            x_ready[4 * i:4 * i + 4] = [got] * 4
        in_w = {}
        for n, w in (("q", wq), ("k", wk), ("v", wv), ("o", wo)):
            in_w[n] = Signals(nc, f"in_w{n}").of(act.dma_start(w[:], weight_view(io[f"L0_gnn_W{n}"])), 16)
        in_b = Signals(nc, "in_b")
        with nc.allow_non_contiguous_dma(reason="a bias by partitions"):
            in_b.of(sp.dma_start(bq_col[:], column_view(io["L0_gnn_bq"])), 16)
            in_b.of(sp.dma_start(bk_col[:], column_view(io["L0_gnn_bk"])), 16)
        in_b.of(sp.dma_start(bv_row[:], io["L0_gnn_bv"].unsqueeze(0).to_broadcast([P, D])), 16)
        got_b = in_b.of(sp.dma_start(bo_row[:], io["L0_gnn_bo"].unsqueeze(0).to_broadcast([P, D])), 16)

        scale = float(HD) ** -0.5
        q_zero = by_dve.of(dve.memset(q_split[:], 0.0))
        wait(dve, got_b)
        bq_scaled = by_dve.of(dve.tensor_scalar(bq_col[:], bq_col[:], scale, None, ALU.mult))
        wait(act, q_zero, bq_scaled)
        normed = layer_norm_scales(nc, by_dve, by_act, x, x_ready, stats, rstd, shift)

        turn_free = h_free = h_t_free = q_free = k_free = pt_free = None
        proj_free = [None, None]
        s_free, av_free, v_free, prob_free = [None, None], [None, None], [None, None], [None, None]
        prob_t_free = att_t_free = None
        proj_n = 0
        slab_done = {}

        def project(slab):
            nonlocal turn_free, h_free, h_t_free, proj_n
            for j in range(2):
                t = 2 * slab + j
                wait(act, normed, h_free)
                a = by_act.of(act.activation(h[:], x[:, t, :], ACT.Relu, bias=shift[:, t:t + 1], scale=rstd[:, t:t + 1]))
                wait(pe, a, turn_free)
                for k in range(KT):
                    mm = pe.transpose(turn_ps[:, k * P:(k + 1) * P], h[:, k * P:(k + 1) * P], ident[:])
                h_free = by_pe.of(mm)
                wait(act, h_free, h_t_free)
                turn_free = by_act.of(act.copy(h_t[:, :, j * P:(j + 1) * P], turn_ps[:].rearrange("p (k n) -> p k n", k=KT)))
            wait(pe, turn_free)
            for w, n in ((wq, "q"), (wk, "k")):
                wait(pe, in_w[n])
                for m in range(KT):
                    s = proj_n % 2
                    proj_n += 1
                    wait(pe, proj_free[s])
                    for k in range(KT):
                        mm = pe.matmul(proj_ps[:, s, 0:2 * P], w[:, k, m * P:(m + 1) * P], h_t[:, k, :], start=k == 0, stop=k == KT - 1)
                    a = by_pe.of(mm)
                    if n == "q":
                        wait(act, a, q_free)
                        for half in range(2):
                            rows = slice(half * HD, (half + 1) * HD)
                            q_done = by_act.of(act.activation(
                                q_split[rows, m, :, half, :], proj_ps[rows, s, 0:2 * P].rearrange("p (i s) -> p i s", s=SB16),
                                ACT.Identity, bias=bq_col[rows, m:m + 1], scale=scale))
                        proj_free[s] = q_done
                    else:
                        wait(dve, a, k_free)
                        proj_free[s] = k_done = by_dve.of(dve.tensor_scalar(k_t[:, m, :], proj_ps[:, s, 0:2 * P], bk_col[:, m:m + 1], None, ALU.add))
            wait(pe, in_w["v"])
            vs = slab % 2
            for j in range(2):
                s = proj_n % 2
                proj_n += 1
                wait(pe, proj_free[s])
                for k in range(KT):
                    mm = pe.matmul(proj_ps[:, s], h_t[:, k, j * P:(j + 1) * P], wv[:, k, :], start=k == 0, stop=k == KT - 1)
                h_t_free = by_pe.of(mm)
                wait(dve, h_t_free, v_free[vs])
                proj_free[s] = v_done = by_dve.of(dve.tensor_tensor(v[:, vs, j, :], proj_ps[:, s], bv_row[:], ALU.add))
            slab_done[slab] = (q_done, k_done, v_done)

        def scores(slab, j):
            nonlocal q_free, k_free
            t = 2 * slab + j
            s = j
            wait(pe, *slab_done[slab], s_free[s])
            for i in range(4):
                for g in range(2):
                    blk = j * 8 + g * 4 + i
                    nodes = slice(j * P + g * GN, j * P + (g + 1) * GN)
                    for k in range(KT):
                        c = (i * 2 + g) * GN
                        mm = pe.matmul(s_ps[32 * k:32 * k + 32, s, c:c + GN], q_split[:, k, blk].rearrange("p z s -> p (z s)"),
                                       k_t[:, k, nodes], start=True, stop=True)
            q_free = k_free = by_pe.of(mm)
            wait(dve, q_free, prob_free[s])
            p4 = prob[:, s].rearrange("p (i g m) -> p i g m", i=4, g=2)
            a = s_free[s] = by_dve.of(dve.tensor_tensor(
                p4, s_ps[:, s].rearrange("p (i g m) -> p i g m", i=4, g=2),
                bias[:, t * 8:t * 8 + 8, :].rearrange("p (g i) m -> p i g m", g=2), ALU.add))
            wait(dve, a)
            p3 = prob[:, s].rearrange("p (r m) -> p r m", m=GN)
            wide = [P, 8, GN]
            a = by_dve.of(dve.tensor_reduce(row_max[:, s], p3, axis=AX.X, op=ALU.max))
            wait(dve, a)
            a = by_dve.of(dve.tensor_tensor(p3, p3, row_max[:, s].unsqueeze(2).to_broadcast(wide), ALU.subtract))
            wait(act, a)
            a = by_act.of(act.activation(prob[:, s], prob[:, s], ACT.Exp))
            wait(dve, a)
            a = by_dve.of(dve.tensor_reduce(row_sum[:, s], p3, axis=AX.X, op=ALU.add))
            wait(dve, a)
            a = by_dve.of(dve.reciprocal(row_sum[:, s], row_sum[:, s]))
            wait(dve, a)
            prob_done[s] = by_dve.of(dve.tensor_tensor(p3, p3, row_sum[:, s].unsqueeze(2).to_broadcast(wide), ALU.mult))

        prob_done = [None, None]

        def mix(slab, j):
            nonlocal pt_free, prob_t_free, att_t_free, proj_n
            t, s, vs = 2 * slab + j, j, slab % 2
            wait(pe, prob_done[s], pt_free)
            for i in range(4):
                mm = pe.transpose(pt_ps[:, i * P:(i + 1) * P], prob[:, s, i * P:(i + 1) * P], ident[:])
            prob_free[s] = by_pe.of(mm)
            wait(act, prob_free[s], prob_t_free)
            pt_free = by_act.of(act.copy(prob_t[:], pt_ps[:]))
            for g in range(2):
                rows = slice(g * GN, (g + 1) * GN)
                wait(pe, pt_free, av_free[g])
                for hd in range(H):
                    mm = pe.matmul(av_ps[HD * (hd % 2):HD * (hd % 2) + HD, g, (hd // 2) * GN:(hd // 2 + 1) * GN],
                                   v[rows, vs, j, hd * HD:(hd + 1) * HD],
                                   prob_t[rows].rearrange("p (i h s) -> p i h s", h=H, s=SB16)[:, :, hd, :], start=True, stop=True)
                prob_t_free = v_free[vs] = by_pe.of(mm)
                wait(act, prob_t_free, att_t_free)
                av_free[g] = by_act.of(act.copy(att_t[:, :, g * GN:(g + 1) * GN], av_ps[:, g, 0:KT * GN].rearrange("p (k n) -> p k n", k=KT)))
            s = proj_n % 2
            proj_n += 1
            wait(pe, av_free[1], proj_free[s], in_w["o"])
            for k in range(KT):
                mm = pe.matmul(proj_ps[:, s], att_t[:, k, :], wo[:, k, :], start=k == 0, stop=k == KT - 1)
            att_t_free = by_pe.of(mm)
            wait(dve, att_t_free, x_plus[t])
            proj_free[s] = by_dve.of(dve.tensor_tensor(x[:, t, :], x[:, t, :], proj_ps[:, s], ALU.add))

        x_plus = {}

        def add_bo(slab):
            for j in range(2):
                t = 2 * slab + j
                wait(pool, h_free, got_b)
                x_plus[t] = by_pool.of(pool.tensor_tensor(x[:, t, :], x[:, t, :], bo_row[:], ALU.add))

        project(0)
        add_bo(0)
        for slab in range(NT // 2):
            scores(slab, 0)
            scores(slab, 1)
            if slab + 1 < NT // 2:
                project(slab + 1)
                add_bo(slab + 1)
            mix(slab, 0)
            mix(slab, 1)
        nc.all_engine_barrier()


def exact_parts(nc, by_act, by_dve, tile, parts_at, source, scale, tile_free):
    dve, act = nc.vector, nc.scalar
    wait(act, tile_free)
    a = by_act.of(act.activation(tile, source, ACT.Copy, scale=scale))
    wait(act, a)
    b = by_act.of(act.copy(parts_at(0), tile))
    wait(dve, b)
    c = by_dve.of(dve.tensor_tensor(tile, tile, parts_at(0), ALU.subtract))
    wait(dve, c)
    c = by_dve.of(dve.tensor_copy(parts_at(1), tile))
    wait(dve, c)
    return a, by_dve.of(dve.tensor_tensor(parts_at(2), tile, parts_at(1), ALU.subtract))


def turn_h(nc, by_pe, by_act, x, rstd, shift, normed, h, h_t, turn_ps, ident, place, h_t_free):
    pe, act = nc.tensor, nc.scalar
    h_free, turn_free = [None, None], [None, None]
    marks = []
    for t in range(NT):
        s = t % 2
        wait(act, normed, h_free[s], h_t_free)
        a = by_act.of(act.activation(h[:, s], x[:, t, :], ACT.Relu, bias=shift[:, t:t + 1], scale=rstd[:, t:t + 1]))
        wait(pe, a, turn_free[s])
        for k in range(KT):
            mm = pe.transpose(turn_ps[:, s, k * P:(k + 1) * P], h[:, s, k * P:(k + 1) * P], ident[:])
        h_free[s] = by_pe.of(mm)
        turn_free[s] = place(t, turn_ps[:, s], h_free[s])
        marks.append(turn_free[s])
    return marks


def sparse_layers(nc, io, keep):
    pe, dve, act, pool, sp = nc.tensor, nc.vector, nc.scalar, nc.gpsimd, nc.sync
    ident, count, x = keep["ident"], keep["count"], keep["x"]
    by_pe, by_dve, by_act, by_pool = (Signals(nc, f"gcn_{n}") for n in ("pe", "dve", "act", "pool"))
    with ExitStack() as mem:
        sb = lambda *a: mem.enter_context(nc.sbuf_tensor(*a))
        ps = lambda *a: mem.enter_context(nc.psum_tensor(*a))
        w = sb("w_gcn", [P, KT, D], F32)
        h = sb("h_gcn", [P, 2, D], F32)
        h_t = sb("h_gcn_t", [P, KT, N], F32)
        parts = sb("parts", [P, NT, PARTS, D], BF16)
        dis_row = sb("dis_row", [P, N], F32)
        dis1, dis2 = sb("dis1", [P, NT], F32), sb("dis2", [P, NT], F32)
        b_col = sb("b_col", [P, 2, KT], F32)
        b_row = sb("b_row", [P, D], F32)
        ones_bf, one_f = sb("ones_bf", [P, P], BF16), sb("one_f", [P, 1], F32)
        stats, rstd, shift = sb("stats1", [P, 8 * NT], F32), sb("rstd1", [P, NT], F32), sb("shift1", [P, NT], F32)
        turn_ps = ps("turn4_ps", [P, 2, 512], F32)
        prod_ps = ps("prod_ps", [P, 2, 512], F32)
        agg_ps = ps("agg_ps", [P, 4, 512], F32)

        in_w, in_b = Signals(nc, "in_gcn_w"), Signals(nc, "in_gcn_b")
        got_w = in_w.of(sp.dma_start(w[:], weight_view(io["L1_gnn_W1"])), 16)
        with nc.allow_non_contiguous_dma(reason="a bias by partitions"):
            in_b.of(sp.dma_start(b_col[:, 0, :], column_view(io["L1_gnn_b1"])), 16)
            in_b.of(sp.dma_start(b_col[:, 1, :], column_view(io["L1_gnn_b2"])), 16)
        got_b = in_b.of(sp.dma_start(b_row[:], io["L1_gnn_b3"].unsqueeze(0).to_broadcast([P, D])), 16)

        a = by_dve.of(dve.memset(ones_bf[:], 1.0))
        b = by_dve.of(dve.memset(one_f[:], 1.0))
        for t in range(NT):
            diag = count[:, t, t * P:(t + 1) * P]
            looped = by_dve.of(dve.tensor_tensor(diag, diag, ident[:], ALU.add))
        wait(pe, looped)
        agg_free = [None] * 4
        for c in range(4):
            for s in range(NT):
                mm = pe.matmul(agg_ps[:, c], ones_bf[:], count[:, s, c * 512:(c + 1) * 512], start=s == 0, stop=s == NT - 1)
            a = by_pe.of(mm)
            wait(dve, a)
            agg_free[c] = by_dve.of(dve.tensor_scalar(dis_row[:, c * 512:(c + 1) * 512], agg_ps[:, c], 1.0, None, ALU.max))
        wait(act, agg_free[3])
        a = by_act.of(act.sqrt(dis_row[:], dis_row[:]))
        wait(dve, a)
        a = by_dve.of(dve.reciprocal(dis_row[:], dis_row[:]))
        wait(pe, a)
        for t in range(NT):
            mm = pe.matmul(turn_ps[:, 0, t:t + 1], dis_row[0:1, t * P:(t + 1) * P], one_f[0:1, :], start=True, stop=True)
        a = by_pe.of(mm)
        wait(dve, a)
        dis1_done = by_dve.of(dve.tensor_copy(dis1[:], turn_ps[:, 0, 0:NT]))
        wait(pe, dis1_done)
        wait(act, dis1_done)

        def to_h_t(t, source, mark):
            wait(act, mark)
            return by_act.of(act.copy(h_t[:, :, t * P:(t + 1) * P], source.rearrange("p (k n) -> p k n", k=KT)))

        prod_free, tile_free = [None, None], [None, None]
        parts_free = h_t_free = None
        agg_n = 0

        def products(h_ready, w_ready, dis, bias_row):
            nonlocal h_t_free
            marks = []
            for t in range(NT):
                s = t % 2
                wait(pe, h_ready[t], w_ready, prod_free[s])
                for k in range(KT):
                    mm = pe.matmul(prod_ps[:, s], h_t[:, k, t * P:(t + 1) * P], w[:, k, :], start=k == 0, stop=k == KT - 1)
                h_t_free = done = by_pe.of(mm)
                source = prod_ps[:, s]
                if bias_row is not None:
                    wait(dve, done, tile_free[s])
                    prod_free[s] = a = by_dve.of(dve.tensor_tensor(h[:, s], source, bias_row, ALU.add))
                    wait(act, a)
                    source = h[:, s]
                wait(act, done, parts_free)
                freed, tile_free[s] = exact_parts(nc, by_act, by_dve, h[:, s], lambda p: parts[:, t, p, :], source, dis[:, t:t + 1], tile_free[s])
                if bias_row is None:
                    prod_free[s] = freed
                marks.append(tile_free[s])
            return marks

        def sum_rows(t, ready):
            nonlocal agg_n, parts_free
            s = agg_n % 4
            agg_n += 1
            wait(pe, agg_free[s])
            for i in range(NT):
                wait(pe, ready[i])
                for p in range(PARTS):
                    mm = pe.matmul(agg_ps[:, s], count[:, i, t * P:(t + 1) * P], parts[:, i, p, :],
                                   start=i == 0 and p == 0, stop=i == NT - 1 and p == PARTS - 1)
            parts_free = by_pe.of(mm)
            return s, parts_free

        normed = layer_norm_scales(nc, by_dve, by_act, x, [None] * NT, stats, rstd, shift)
        h_ready = turn_h(nc, by_pe, by_act, x, rstd, shift, normed, h, h_t, turn_ps, ident, to_h_t, None)
        wait(act, h_t_free)
        wait(dve, got_b)
        wait(act, got_b)
        wait(dve, h_ready[-1])
        for layer in range(2):
            ready = products(h_ready, got_w, dis1, None)
            wait(sp, h_t_free)
            got_w = in_w.of(sp.dma_start(w[:], weight_view(io[f"L1_gnn_W{layer + 2}"])), 16)
            wait(act, h_t_free)
            marks = [None] * 4
            for c in range(4):
                for k in range(KT):
                    s = agg_n % 4
                    agg_n += 1
                    wait(pe, agg_free[s])
                    cols = slice(c * 512, (c + 1) * 512)
                    for i in range(NT):
                        wait(pe, ready[i])
                        for p in range(PARTS):
                            mm = pe.matmul(agg_ps[:, s], parts[:, i, p, k * P:(k + 1) * P], count[:, i, cols],
                                           start=i == 0 and p == 0, stop=i == NT - 1 and p == PARTS - 1)
                    parts_free = by_pe.of(mm)
                    wait(dve, parts_free, h_t_free)
                    agg_free[s] = by_dve.of(dve.tensor_tensor(h_t[:, k, cols], agg_ps[:, s], dis_row[:, cols], ALU.mult))
                    wait(act, agg_free[s])
                    marks[c] = by_act.of(act.activation(h_t[:, k, cols], h_t[:, k, cols], ACT.Relu, bias=b_col[:, layer, k:k + 1]))
            h_ready = [marks[t // 4] for t in range(NT)]
            if layer == 0:
                a = by_dve.of(dve.tensor_reduce(dis2[:], count[:], axis=AX.X, op=ALU.add))
                wait(act, a)
                a = by_act.of(act.sqrt(dis2[:], dis2[:]))
                wait(dve, a)
                dis2_done = by_dve.of(dve.reciprocal(dis2[:], dis2[:]))
        ready = products(h_ready, got_w, dis1, None)
        wait(sp, h_t_free)
        wo_in = dis_row[:].rearrange("p (k d) -> p k d", k=KT)
        wait(sp, h_ready[-1])
        got_w = in_w.of(sp.dma_start(wo_in, weight_view(io["L2_gnn_W"])), 16)
        x_ready = []
        wait(dve, dis1_done)
        for t in range(NT):
            s, done = sum_rows(t, ready)
            wait(dve, done)
            agg_free[s] = a = by_dve.of(dve.scalar_tensor_tensor(x[:, t, :], agg_ps[:, s], dis1[:, t:t + 1], x[:, t, :], ALU.mult, ALU.add))
            wait(pool, a, got_b)
            x_ready.append(by_pool.of(pool.tensor_tensor(x[:, t, :], x[:, t, :], b_row[:], ALU.add)))
        wait(pe, got_w)
        turned = None
        for i in range(KT):
            wait(pe, turned)
            for o in range(KT):
                mm = pe.transpose(turn_ps[:, 0, o * P:(o + 1) * P], wo_in[:, o, i * P:(i + 1) * P], ident[:])
            a = by_pe.of(mm)
            wait(dve, a)
            turned = by_dve.of(dve.tensor_copy(w[:, i, :], turn_ps[:, 0]))
        wait(pe, turned)
        wait(sp, x_ready[-1])
        got_b = in_b.of(sp.dma_start(b_row[:], io["L2_gnn_b"].unsqueeze(0).to_broadcast([P, D])), 16)
        normed = layer_norm_scales(nc, by_dve, by_act, x, x_ready, stats, rstd, shift)
        wait(act, x_ready[-1], tile_free[0], tile_free[1])
        h_ready = turn_h(nc, by_pe, by_act, x, rstd, shift, normed, h, h_t, turn_ps, ident, to_h_t, h_t_free)
        wait(dve, got_b, h_ready[-1])
        wait(act, dis2_done)
        ready = products(h_ready, turned, dis2, b_row[:])
        for t in range(NT):
            s, done = sum_rows(t, ready)
            hs = t % 2
            wait(act, done, tile_free[hs])
            agg_free[s] = a = by_act.of(act.activation(h[:, hs], agg_ps[:, s], ACT.Relu, scale=dis2[:, t:t + 1]))
            wait(dve, a)
            tile_free[hs] = by_dve.of(dve.tensor_tensor(x[:, t, :], x[:, t, :], h[:, hs], ALU.add))
        nc.all_engine_barrier()


def weighted_layer(nc, io, keep):
    pe, dve, act, pool, sp = nc.tensor, nc.vector, nc.scalar, nc.gpsimd, nc.sync
    ident, x = keep["ident"], keep["x"]
    by_pe, by_dve, by_act = (Signals(nc, f"wl_{n}") for n in ("pe", "dve", "act"))
    RING, HALF = 6, N // 2
    with ExitStack() as mem:
        sb = lambda *a: mem.enter_context(nc.sbuf_tensor(*a))
        ps = lambda *a: mem.enter_context(nc.psum_tensor(*a))
        w = sb("w_wl", [P, KT, D], F32)
        h = sb("h_wl", [P, 2, D], F32)
        h_t = sb("h_wl_t", [P, KT, N], F32)
        support = sb("support", [P, NT, D], F32)
        ring = sb("ring", [P, RING, HALF], F32)
        y = sb("y", [P, 4, D], F32)
        stats, rstd, shift = sb("stats3", [P, 8 * NT], F32), sb("rstd3", [P, NT], F32), sb("shift3", [P, NT], F32)
        acc_ps = ps("acc_ps", [P, 8, 512], F32)
        in_w = Signals(nc, "in_wl")
        got_w = in_w.of(sp.dma_start(w[:], weight_view(io["L3_gnn_weight"])), 16)
        in_ring = [Signals(nc, f"in_ring{i}") for i in range(RING)]
        ring_got, ring_read = {}, {}

        def load(n):
            half, q = divmod(n, NT)
            wait(sp, ring_read.get(n - RING))
            ring_got[n] = in_ring[n % RING].of(
                sp.dma_start(ring[:, n % RING, :], io["weight_dram"][q, :, half * HALF:(half + 1) * HALF]), 16)
        for n in range(RING):
            load(n)
        normed = layer_norm_scales(nc, by_dve, by_act, x, [None] * NT, stats, rstd, shift)

        def place(t, source, mark):
            turned = source.rearrange("p (k b q m d) -> p k b q m d", k=KT, b=2, m=2, d=2)
            cols = h_t[:].rearrange("p k (q m b d) -> p k b q m d", m=2, b=NGRAPH, d=2)
            wait(act if t % 2 else dve, mark)
            for k in range(KT):
                for b in range(2):
                    out, source_b = cols[:, k, 2 * t + b], turned[:, k, b]
                    done = by_act.of(act.copy(out, source_b)) if t % 2 else by_dve.of(dve.tensor_copy(out, source_b))
            return done

        h_ready = turn_h(nc, by_pe, by_act, x, rstd, shift, normed, h, h_t, acc_ps[:, 0:2], ident, place, None)
        free = [None, None]
        wait(pe, h_ready[-1], h_ready[-2], got_w)
        for q in range(NT):
            s = q % 2
            wait(pe, free[s])
            for k in range(KT):
                mm = pe.matmul(acc_ps[:, 2 + s], h_t[:, k, q * P:(q + 1) * P], w[:, k, :], start=k == 0, stop=k == KT - 1)
            a = by_pe.of(mm)
            wait(act, a)
            free[s] = by_act.of(act.copy(support[:, q, :], acc_ps[:, 2 + s]))
        wait(pe, free[0], free[1])
        y_free = [None] * 4
        acc_free = [None] * 8
        outs = [Signals(nc, f"out_y{i}") for i in range(4)]
        out_view = io["out"].rearrange("(t p) d -> p t d", p=P)
        for half in range(2):
            for q in range(NT):
                n = half * NT + q
                wait(pe, ring_got[n])
                for s in range(8):
                    if q == 0:
                        wait(pe, acc_free[s])
                    mm = pe.matmul(acc_ps[:, s], ring[:, n % RING, s * P:(s + 1) * P], support[:, q, :], start=q == 0, stop=q == NT - 1)
                    if q == NT - 1 or s == 7:
                        done = by_pe.of(mm)
                    if q == NT - 1:
                        t = half * 8 + s
                        ys = t % 4
                        wait(act, done, y_free[ys])
                        acc_free[s] = a = by_act.of(act.activation(y[:, ys], acc_ps[:, s], ACT.Relu))
                        wait(dve, a)
                        b = by_dve.of(dve.tensor_tensor(y[:, ys], y[:, ys], x[:, t, :], ALU.add))
                        wait(sp, b)
                        y_free[ys] = outs[ys].of(sp.dma_start(out_view[:, t, :], y[:, ys]), 16)
                ring_read[n] = done
                if n + RING < 2 * NT:
                    load(n + RING)
        wait(sp, *y_free)


INPUTS = ("x", "src", "dst", "edge_attr_16", "edge_weight", "L0_gnn_Wq", "L0_gnn_bq", "L0_gnn_Wk", "L0_gnn_bk",
          "L0_gnn_Wv", "L0_gnn_bv", "L0_gnn_Wo", "L0_gnn_bo", "L0_gnn_We", "L0_gnn_be", "L1_gnn_W1", "L1_gnn_b1",
          "L1_gnn_W2", "L1_gnn_b2", "L1_gnn_W3", "L1_gnn_b3", "L2_gnn_W", "L2_gnn_b", "L3_gnn_weight")


def program(nc, io):
    io = dict(io)
    io["rec_dram"] = nc.dram_tensor("rec_dram", [NBLK + 1, REC], F32, kind="Internal").ap()
    io["weight_dram"] = nc.dram_tensor("weight_dram", [NT, P, N], F32, kind="Internal").ap()
    with ExitStack() as mem:
        sb = lambda *a: mem.enter_context(nc.sbuf_tensor(*a))
        keep = {
            "ident": sb("ident", [P, P], F32),
            "blocks": sb("blocks", [P, GTILES, WIN], F32),
            "rounds": sb("rounds", [P, 1], I32),
            "x": sb("x_sb", [P, NT, D], F32),
        }
        make_identity(nc, keep)
        edge_prep(nc, io, keep)
        with ExitStack() as graph:
            keep["count"] = graph.enter_context(nc.sbuf_tensor("count", [P, NT, N], BF16))
            with ExitStack() as edges:
                keep["bias"] = edges.enter_context(nc.sbuf_tensor("bias", [P, SHI, GN], F32))
                build_matrices(nc, io, keep)
                attention(nc, io, keep)
            sparse_layers(nc, io, keep)
        weighted_layer(nc, io, keep)


def kernel(**inputs):
    import concourse.bacc as bacc
    from concourse.bass_utils import run_bass_kernel_spmd

    nc = bacc.Bacc("TRN2", target_bir_lowering=False, num_devices=1)
    arrays, io = {}, {}
    for name in INPUTS:
        a = np.ascontiguousarray(inputs[name])
        arrays[f"in_{name}"] = a
        io[name] = nc.dram_tensor(f"in_{name}", a.shape, mybir.dt.from_np(a.dtype), kind="ExternalInput").ap()
    io["out"] = nc.dram_tensor("out_x", [N, D], F32, kind="ExternalOutput").ap()
    program(nc, io)
    r = run_bass_kernel_spmd(nc, [arrays], core_ids=[0])
    return r.results[0]["out_x"]
```

```python
from contextlib import ExitStack

import numpy as np
import concourse.bass as bass
from concourse import mybir
from concourse.alu_op_type import AluOpType as ALU

F32, F32R, BF16 = mybir.dt.float32, mybir.dt.float32r, mybir.dt.bfloat16
I32, U32 = mybir.dt.int32, mybir.dt.uint32
ACT = mybir.ActivationFunctionType
AX = mybir.AxisListType

P = 128
N = 2048
D = 512
E = 67584
ED = 16
H = 8
HD = D // H
GN = 64
NT = N // P
KT = D // P
NGRAPH = N // GN

PARTS = 3
GROUP_DSTS = 2
PAIRS = GN // GROUP_DSTS
NGROUP = N // GROUP_DSTS
GTILES = NGROUP // P
PPT = PAIRS // GTILES
BATCH = 16
NBATCH = P // BATCH
BLK = 16
EPP = E // P
BPP = EPP // BLK
NBLK = E // BLK
FIELDS = 3 + H
REC = FIELDS * BLK
WIN = P // BLK
SB16 = 16
SHI = N // SB16
CCOLS = GROUP_DSTS * NT
BCOLS = GROUP_DSTS * SHI
ROUNDS_MAX = E // P + 1
LN_EPS = 1e-5


class Signals:

    def __init__(self, nc, name):
        self.sem, self.value, self.seen = nc.alloc_semaphore(name), 0, {}

    def of(self, instruction, by=1):
        instruction.then_inc(self.sem, by)
        self.value += by
        return self, self.value


def wait(engine, *marks):
    for mark in marks:
        if mark is None:
            continue
        if isinstance(mark, list):
            wait(engine, *mark)
            continue
        signals, value = mark
        if signals.seen.get(id(engine), 0) < value:
            engine.wait_ge(signals.sem, value)
            signals.seen[id(engine)] = value


def make_identity(nc, keep):
    made = Signals(nc, "identity")
    a = made.of(nc.gpsimd.memset(keep["ident"][:], 0.0))
    wait(nc.gpsimd, a)
    made.of(nc.gpsimd.affine_select(out=keep["ident"][:], in_=keep["ident"][:], compare_op=ALU.not_equal, fill=1.0, base=0,
                                    pattern=[[-1, P]], channel_multiplier=1))
    nc.all_engine_barrier()


def edge_prep(nc, io, keep):
    pe, dve, act, pool, sp = nc.tensor, nc.vector, nc.scalar, nc.gpsimd, nc.sync
    by_pe, by_dve, by_act, by_pool = (Signals(nc, f"prep_{x}") for x in ("pe", "dve", "act", "pool"))
    with ExitStack() as mem:
        sb = lambda *a: mem.enter_context(nc.sbuf_tensor(*a))
        ps = lambda *a: mem.enter_context(nc.psum_tensor(*a))
        attr = sb("attr", [P, EPP * ED], F32)
        rec = sb("rec", [P, EPP, FIELDS], F32)
        src_i = sb("src_i", [P, EPP], I32)
        dst_i = sb("dst_i", [P, EPP], I32)
        dst_next = sb("dst_next", [P, EPP], I32)
        step_f = sb("step_f", [P, EPP], F32)
        graph_i = sb("graph_i", [P, EPP], I32)
        pair_i = sb("pair_i", [P, EPP], I32)
        graph_key = sb("graph_key", [P, EPP], BF16)
        pair_key = sb("pair_key", [P, EPP], BF16)
        ew = sb("ew", [P, EPP], F32)
        we_diag = sb("we_diag", [P, H, 8], F32)
        be_row = sb("be_row", [P, H], F32)
        attr_t = sb("attr_t", [P, 2, 512], F32)
        iota_hist = sb("iota_hist", [P, PAIRS, 66], BF16)
        graph_hot = sb("graph_hot", [P, 2, PAIRS, 66], BF16)
        pair_hot = sb("pair_hot", [P, 2, PAIRS, 66], BF16)
        pad = sb("pad", [1, REC], F32)
        small = sb("small", [P, 640], F32)
        small_i = sb("small_i", [P, 160], I32)
        turn_ps = ps("turn_ps", [P, 2, 512], F32)
        eb_ps = ps("eb_ps", [P, 2, 512], F32)
        hist_ps = ps("hist_ps", [P, 512], F32)
        misc_ps = ps("misc_ps", [P, 512], F32)
        in_src, in_dst, in_attr, in_w, in_we = (Signals(nc, f"in_{x}") for x in ("src", "dst", "attr", "w", "we"))
        got_dst = in_dst.of(sp.dma_start(dst_i[:], io["dst"].rearrange("(p j) -> p j", p=P)), 16)
        last = P - 1
        got_src = in_src.of(sp.dma_start(src_i[:], io["src"].rearrange("(p j) -> p j", p=P)), 16)
        got_w = in_w.of(sp.dma_start(ew[:], io["edge_weight"].rearrange("(p j) -> p j", p=P)), 16)
        we_zero = by_dve.of(dve.memset(we_diag[:], 0.0))
        wait(sp, we_zero)
        with nc.allow_non_contiguous_dma(reason="a 16 x 8 matrix"):
            for e in range(8):
                got_we = in_we.of(sp.dma_start(we_diag[e * ED:(e + 1) * ED, :, e], io["L0_gnn_We"]), 16)
        got_we = in_we.of(sp.dma_start(be_row[:], io["L0_gnn_be"].unsqueeze(0).to_broadcast([P, H])), 16)
        got_attr = in_attr.of(act.dma_start(attr[:], io["edge_attr_16"].rearrange("(p j) f -> p (j f)", p=P)), 16)
        filled = by_dve.of(dve.memset(dst_next[:], N))
        wait(sp, filled)
        in_next = Signals(nc, "in_next")
        in_next.of(sp.dma_start(dst_next[0:last, :], io["dst"][1:1 + last * EPP].rearrange("(p j) -> p j", p=last)), 16)
        got_next = in_next.of(sp.dma_start(dst_next[last:P, 0:EPP - 1], io["dst"][1 + last * EPP:E].unsqueeze(0)), 16)

        made_iota = by_pool.of(pool.iota(iota_hist[:], pattern=[[1, PAIRS], [0, 66]], base=0, channel_multiplier=0, allow_small_or_imprecise_dtypes=True))
        wait(dve, made_iota, got_dst)
        g_i = by_dve.of(dve.tensor_scalar(graph_i[:], dst_i[:], 6, None, ALU.logical_shift_right))
        p_i = by_dve.of(dve.tensor_scalar(pair_i[:], dst_i[:], 1, PAIRS - 1, ALU.logical_shift_right, ALU.bitwise_and))
        wait(dve, p_i)
        by_dve.of(dve.tensor_copy(graph_key[:], graph_i[:]))
        keys = by_dve.of(dve.tensor_copy(pair_key[:], pair_i[:]))
        wait(dve, keys)
        used = [None, None]
        for c in range(EPP // 66):
            wait(dve, used[c % 2])
            cols = slice(c * 66, (c + 1) * 66)
            bc = [P, PAIRS, 66]
            by_dve.of(dve.tensor_tensor(graph_hot[:, c % 2], iota_hist[:], graph_key[:, cols].unsqueeze(1).to_broadcast(bc), ALU.is_equal))
            hots = by_dve.of(dve.tensor_tensor(pair_hot[:, c % 2], iota_hist[:], pair_key[:, cols].unsqueeze(1).to_broadcast(bc), ALU.is_equal))
            wait(pe, hots)
            for j in range(66):
                mm = pe.matmul(hist_ps[0:NGRAPH, 0:PAIRS], graph_hot[:, c % 2, :, j], pair_hot[:, c % 2, :, j],
                               start=c == 0 and j == 0, stop=c == EPP // 66 - 1 and j == 65)
            used[c % 2] = by_pe.of(mm)

        cnt, ones, base, end, first = (small[0:NGRAPH, i * PAIRS:(i + 1) * PAIRS] for i in range(5))
        row, viol, flag, rounds, span_max = (small[:, 160 + i:161 + i] for i in range(5))
        low = small[:, 176:176 + PAIRS]
        start_i, span_i = (small_i[0:NGRAPH, i * PAIRS:(i + 1) * PAIRS] for i in range(2))
        start_f = small[0:NGRAPH, 224:224 + PAIRS]
        wait(dve, used[(EPP // 66 - 1) % 2])
        a = by_dve.of(dve.tensor_copy(cnt, hist_ps[0:NGRAPH, 0:PAIRS]))
        by_dve.of(dve.memset(ones, 1.0))
        b = by_dve.of(dve.memset(low, 1.0))
        wait(dve, a, b)
        a = by_dve.of(dve.tensor_reduce(row[0:NGRAPH], cnt, axis=AX.X, op=ALU.add))
        wait(pool, b)
        lowered = by_pool.of(pool.affine_select(out=low[0:NGRAPH], in_=low[0:NGRAPH], compare_op=ALU.is_gt, fill=0.0, base=0,
                                                pattern=[[1, PAIRS]], channel_multiplier=-1))
        wait(pe, a, lowered)
        c0 = by_pe.of(pe.matmul(misc_ps[0:NGRAPH, 0:1], low[0:NGRAPH], row[0:NGRAPH], start=True, stop=True))
        wait(dve, c0)
        a = by_dve.of(dve.tensor_copy(base[:, 0:1], misc_ps[0:NGRAPH, 0:1]))
        wait(dve, a)
        a = by_dve.of(dve.tensor_tensor_scan(end, ones, cnt, base[:, 0:1], ALU.mult, ALU.add))
        wait(dve, a)
        a = by_dve.of(dve.tensor_tensor(first, end, cnt, ALU.subtract))
        wait(dve, a)
        a = by_dve.of(dve.tensor_copy(start_i, first))
        wait(dve, a)
        a = by_dve.of(dve.tensor_scalar(start_i, start_i, 4, None, ALU.logical_shift_right))
        wait(dve, a)
        a = by_dve.of(dve.tensor_copy(start_f, start_i))
        wait(dve, a)
        a = by_dve.of(dve.scalar_tensor_tensor(first, start_f, -float(BLK), end, ALU.mult, ALU.add))
        wait(dve, a)
        a = by_dve.of(dve.tensor_scalar(span_i, first, float(P - 1), None, ALU.add))
        wait(dve, a)
        a = by_dve.of(dve.tensor_scalar(span_i, span_i, 7, None, ALU.logical_shift_right))
        wait(dve, a)
        a = by_dve.of(dve.memset(span_max, 0.0))
        wait(dve, a)
        a = by_dve.of(dve.tensor_reduce(span_max[0:NGRAPH], span_i, axis=AX.X, op=ALU.max))
        wait(dve, got_next)
        b = by_dve.of(dve.tensor_tensor(step_f[:], dst_i[:], dst_next[:], ALU.subtract))
        wait(dve, b)
        b = by_dve.of(dve.tensor_reduce(viol, step_f[:], axis=AX.X, op=ALU.max))
        wait(pool, a, b)
        RMAX = bass.bass_isa.ReduceOp.max
        viol_all, span_all = small[:, 165:166], small[:, 166:167]
        by_pool.of(pool.partition_all_reduce(viol_all, viol, P, RMAX))
        alls = by_pool.of(pool.partition_all_reduce(span_all, span_max, P, RMAX))
        wait(dve, alls)
        a = by_dve.of(dve.tensor_scalar(flag, viol_all, 0.0, None, ALU.is_le))
        b = by_dve.of(dve.tensor_scalar(rounds, span_all, 1.0, -float(E // P), ALU.max, ALU.add))
        wait(dve, a, b)
        a = by_dve.of(dve.tensor_tensor(rounds, rounds, flag, ALU.mult))
        b = by_dve.of(dve.tensor_scalar(start_f, start_f, flag[0:NGRAPH], None, ALU.mult))
        wait(dve, a, b)
        keep["rounds_set"] = by_dve.of(dve.tensor_scalar(keep["rounds"][0:1, :], rounds[0:1], float(E // P), None, ALU.add))
        ident = keep["ident"]
        wait(pe, b)
        spread = start_f.rearrange("b (t q) -> b q t", q=PPT)
        for q in range(PPT):
            mm = pe.matmul(misc_ps[q * NGRAPH:(q + 1) * NGRAPH, 8:8 + GTILES], ident[0:NGRAPH, 0:NGRAPH], spread[:, q, :], start=True, stop=True)
        c0 = by_pe.of(mm)
        blk_i = small_i[:, 64:64 + WIN]
        blk_f = small[:, 256:256 + WIN]
        k0 = by_pool.of(pool.iota(blk_i, pattern=[[1, WIN]], base=0, channel_multiplier=0))
        wait(dve, k0, c0)
        a = by_dve.of(dve.tensor_copy(blk_f, blk_i))
        wait(dve, a)
        by_dve.of(dve.tensor_tensor(keep["blocks"][:], misc_ps[:, 8:8 + GTILES].unsqueeze(2).to_broadcast([P, GTILES, WIN]),
                                    blk_f.unsqueeze(1).to_broadcast([P, GTILES, WIN]), ALU.add))

        wait(dve, got_src, got_w)
        by_dve.of(dve.tensor_copy(rec[:, :, 0], src_i[:]))
        by_dve.of(dve.tensor_copy(rec[:, :, 1], dst_i[:]))
        by_dve.of(dve.tensor_copy(rec[:, :, 2], ew[:]))
        padded = by_dve.of(dve.memset(pad[:], -1.0))
        wait(sp, padded)
        out_rec = Signals(nc, "out_rec")
        out_rec.of(sp.dma_start(io["rec_dram"][NBLK:NBLK + 1, :], pad[:]), 16)
        nblk8 = EPP // 8
        per = 4
        wait(pe, got_attr, got_we)
        wait(dve, got_we)
        turned_free, eb_free, attr_t_free = [None, None], [None, None], [None, None]
        for i0 in range(0, nblk8, 8):
            n = min(8, nblk8 - i0)
            e = (i0 // 8) % 2
            for j0 in range(0, n, per):
                m = min(per, n - j0)
                s = (j0 // per) % 2
                wait(pe, turned_free[s])
                for j in range(m):
                    i = i0 + j0 + j
                    mm = pe.transpose(turn_ps[:, s, j * P:(j + 1) * P], attr[:, i * P:(i + 1) * P], ident[:])
                t = by_pe.of(mm)
                wait(act, t, attr_t_free[s])
                turned_free[s] = by_act.of(act.copy(attr_t[:, s, 0:m * P], turn_ps[:, s, 0:m * P]))
                wait(pe, turned_free[s])
                if j0 == 0:
                    wait(pe, eb_free[e])
                for j in range(m):
                    mm = pe.matmul(eb_ps[:, e, (j0 + j) * 64:(j0 + j + 1) * 64], attr_t[:, s, j * P:(j + 1) * P],
                                   we_diag[:].rearrange("p h e -> p (h e)"), start=True, stop=True)
                attr_t_free[s] = by_pe.of(mm)
            wait(dve, attr_t_free[s])
            eb = eb_ps[:, e, 0:n * 64].rearrange("p (b h e) -> p b e h", h=H, e=8)
            out = rec[:, i0 * 8:(i0 + n) * 8, 3:3 + H].rearrange("p (b e) h -> p b e h", e=8)
            eb_free[e] = by_dve.of(dve.tensor_tensor(out, eb, be_row[:].unsqueeze(1).unsqueeze(1).to_broadcast([P, n, 8, H]), ALU.add))
        wait(sp, eb_free[0], eb_free[1])
        wait(sp, eb_free[((nblk8 - 1) // 8) % 2])
        stored = out_rec.of(sp.dma_start(io["rec_dram"][0:NBLK, :].rearrange("(p b) r -> p (b r)", p=P),
                                         rec[:].rearrange("p j f -> p (j f)")), 16)
        wait(sp, stored)
        nc.all_engine_barrier()


def build_matrices(nc, io, keep):
    pe, dve, act, pool, sp = nc.tensor, nc.vector, nc.scalar, nc.gpsimd, nc.sync
    ident, count, bias, blocks = keep["ident"], keep["count"], keep["bias"], keep["blocks"]
    names = ("pe", "dve", "act", "pool", "gather", "old0", "old1", "store0", "store1")
    signals = {}
    for n in names:
        signals[n] = Signals(nc, f"build_{n}")
    nums = [signals[n].sem.num for n in names]
    assert nums == list(range(nums[0], nums[0] + len(nums)))
    by_pe, by_dve, by_act, by_pool = (signals[x] for x in ("pe", "dve", "act", "pool"))
    once = Signals(nc, "build_once")

    with ExitStack() as mem:
        sb = lambda *a: mem.enter_context(nc.sbuf_tensor(*a))
        ps = lambda *a: mem.enter_context(nc.psum_tensor(*a))
        gathered = sb("gathered", [P, WIN, REC], F32)
        fields = sb("fields", [P, FIELDS, P], F32)
        d0 = sb("d0", [P, P], F32)
        ints = sb("ints", [P, 5, P], I32)
        dlocal = fields[:, 1, :]
        keys = sb("keys", [P, 2, 4, P], BF16)
        eb_parts = sb("eb_parts", [P, 2, PARTS, H + 1, P], BF16)
        idx_f = sb("idx_f", [P, GTILES * WIN], F32)
        idx = sb("idx", [P, GTILES * WIN], U32)
        iota_rep = sb("iota_rep", [P, BCOLS, BATCH], BF16)
        place = keep["x"][:].rearrange("p t d -> p (t d)").bitcast(BF16)
        n_src = 2 * P * BATCH
        hot_src = place[:, 0:n_src].rearrange("p (z c g) -> p z c g", z=2, g=BATCH)
        hot_eb = place[:, n_src:n_src + 2 * PARTS * H * SB16 * BATCH].rearrange("p (z h s g) -> p z h s g", z=2, s=SB16, g=BATCH)
        hot_bias = sb("hot_bias", [P, 2, BCOLS, BATCH], BF16)
        hot16 = sb("hot16", [P, 2, SB16, BATCH], BF16)
        hot_cnt = sb("hot_cnt", [P, 2, CCOLS, BATCH], BF16)
        hot_w = sb("hot_w", [P, 2, PARTS, CCOLS, BATCH], BF16)
        w_slab = sb("w_slab", [P, P, NT], F32)
        w_old = sb("w_old", [P, 2, 512], F32)
        w_new = sb("w_new", [P, 2, 512], F32)
        turn_ps = ps("turn2_ps", [P, 2, 512], F32)
        cnt_ps = ps("cnt_ps", [P, 2, 512], F32)
        w_ps = ps("w_ps", [P, 2, 512], F32)
        bias_ps = ps("bias_ps", [P, 2, 512], F32)
        once.of(pool.iota(d0[:], pattern=[[GROUP_DSTS, PPT], [GN, NGRAPH]], base=0, channel_multiplier=0, allow_small_or_imprecise_dtypes=True))
        once.of(pool.iota(iota_rep[:], pattern=[[1, BCOLS], [0, BATCH]], base=0, channel_multiplier=0, allow_small_or_imprecise_dtypes=True))
        once.of(dve.memset(w_old[:], 0.0))
        once.of(dve.memset(count[:], 0.0))
        once.of(pool.memset(bias[:], 0.0))
        nc.all_engine_barrier()
        rounds = nc.values_load(keep["rounds"][0:1, :], min_val=1, max_val=ROUNDS_MAX)
        with nc.Fori(0, rounds) as r:
            a = by_dve.of(dve.tensor_scalar(idx_f[:], blocks[:].rearrange("p t k -> p (t k)"), float(NBLK), None, ALU.min))
            wait(dve, a)
            indexed = by_dve.of(dve.tensor_copy(idx[:], idx_f[:]))
            by_dve.of(dve.tensor_scalar(blocks[:], blocks[:], float(WIN), None, ALU.add))

            gather_read = [None]
            turned_free = [None, None]
            fields_free = None
            parts_done = [None, None]
            parts_free = [(), ()]
            got = [None]

            def gather(t):
                wait(pool, indexed, gather_read[0])
                for k in range(WIN):
                    g = pool.indirect_dma_start(gathered[:, k, :], None, io["rec_dram"],
                                                bass.IndirectOffsetOnAxis(ap=idx[:, t * WIN + k:t * WIN + k + 1], axis=0))
                    got[0] = signals["gather"].of(g, 16)

            def prep(t):
                nonlocal fields_free
                s = t % 2
                wait(pe, got[0])
                view = gathered[:].rearrange("p k (e f) -> p f (k e)", f=FIELDS)
                evacuated = None
                for f0 in range(0, FIELDS, 4):
                    n = min(4, FIELDS - f0)
                    bank = (f0 // 4) % 2
                    wait(pe, turned_free[bank])
                    for f in range(n):
                        mm = pe.transpose(turn_ps[:, bank, f * P:(f + 1) * P], view[:, f0 + f], ident[:])
                    gather_read[0] = by_pe.of(mm)
                    wait(act, gather_read[0], fields_free)
                    evacuated = turned_free[bank] = by_act.of(act.copy(
                        fields[:, f0:f0 + n, :], turn_ps[:, bank, 0:n * P].rearrange("p (f g) -> p f g", f=n)))
                wait(dve, evacuated, *parts_free[s])
                a = by_dve.of(dve.tensor_copy(ints[:, 0], fields[:, 0, :]))
                b = by_dve.of(dve.scalar_tensor_tensor(dlocal, fields[:, 1, :], -float(t * PPT * GROUP_DSTS), d0[:], ALU.add, ALU.subtract))
                wait(dve, a)
                by_dve.of(dve.tensor_scalar(ints[:, 1], ints[:, 0], P - 1, None, ALU.bitwise_and))
                by_dve.of(dve.tensor_scalar(ints[:, 2], ints[:, 0], 7, None, ALU.logical_shift_right))
                by_dve.of(dve.tensor_scalar(ints[:, 3], ints[:, 0], SB16 - 1, None, ALU.bitwise_and))
                a = by_dve.of(dve.tensor_scalar(ints[:, 4], ints[:, 0], 4, None, ALU.logical_shift_right))
                wait(dve, a)
                by_dve.of(dve.tensor_copy(keys[:, s, 0], ints[:, 1]))
                by_dve.of(dve.tensor_copy(keys[:, s, 1], ints[:, 3]))
                by_dve.of(dve.scalar_tensor_tensor(keys[:, s, 2], dlocal, float(NT), ints[:, 2], ALU.mult, ALU.add))
                last = by_dve.of(dve.scalar_tensor_tensor(keys[:, s, 3], dlocal, float(SHI), ints[:, 4], ALU.mult, ALU.add))
                wait(act, evacuated, *parts_free[s])
                source = fields[:, 2:FIELDS, :]
                p0 = by_act.of(act.copy(eb_parts[:, s, 0], source))
                wait(dve, p0)
                p1 = by_dve.of(dve.tensor_tensor(source, source, eb_parts[:, s, 0], ALU.subtract))
                wait(act, p1)
                p2 = by_act.of(act.copy(eb_parts[:, s, 1], source))
                wait(dve, p2)
                fields_free = by_dve.of(dve.tensor_tensor(eb_parts[:, s, 2], source, eb_parts[:, s, 1], ALU.subtract))
                parts_done[s] = (last, p2, fields_free)

            hot_free = [None, None]
            ps_free = [(), ()]
            bias_free = [None, None]
            slab_free, slab_done = [None], [None]
            made = {}

            def hots(t, i):
                n = t * NBATCH + i
                s, ts = n % 2, t % 2
                cols = slice(i * BATCH, (i + 1) * BATCH)

                def key(k, c):
                    return keys[:, ts, k, cols].unsqueeze(1).to_broadcast([P, c, BATCH])
                wait(dve, hot_free[s], *parts_done[ts])
                a16 = by_dve.of(dve.tensor_tensor(hot16[:, s], iota_rep[:, 0:SB16], key(1, SB16), ALU.is_equal))
                acn = by_dve.of(dve.tensor_tensor(hot_cnt[:, s], iota_rep[:, 0:CCOLS], key(2, CCOLS), ALU.is_equal))
                wait(pool, hot_free[s], acn, *parts_done[ts])

                def product(eng, by, p):
                    return by.of(eng.tensor_tensor(
                        hot_eb[:, s, p * H:(p + 1) * H], hot16[:, s].unsqueeze(1).to_broadcast([P, H, SB16, BATCH]),
                        eb_parts[:, ts, p, 1:1 + H, cols].unsqueeze(2).to_broadcast([P, H, SB16, BATCH]), ALU.mult))
                w = by_pool.of(pool.tensor_tensor(
                    hot_w[:, s], hot_cnt[:, s].unsqueeze(1).to_broadcast([P, PARTS, CCOLS, BATCH]),
                    eb_parts[:, ts, :, 0, cols].unsqueeze(2).to_broadcast([P, PARTS, CCOLS, BATCH]), ALU.mult))
                e2 = product(pool, by_pool, 2)
                by_dve.of(dve.tensor_tensor(hot_src[:, s], iota_rep[:, 0:P], key(0, P), ALU.is_equal))
                by_dve.of(dve.tensor_tensor(hot_bias[:, s], iota_rep[:], key(3, BCOLS), ALU.is_equal))
                wait(dve, a16)
                product(dve, by_dve, 0)
                e1 = product(dve, by_dve, 1)
                made[n] = (e1, e2)
                parts_free[ts] = (e1, e2)

            def products(n, groups):
                s, bank = n % 2, n // 2 % 2
                half = n % 2
                wait(pe, *made[n], *ps_free[s])
                if half == 0:
                    wait(pe, bias_free[bank])
                for g in groups:
                    hs = hot_src[:, s, :, g]
                    c = slice(g * CCOLS, (g + 1) * CCOLS)
                    pe.matmul(cnt_ps[:, s, c], hs, hot_cnt[:, s, :, g], start=True, stop=True)
                    for p in range(PARTS):
                        pe.matmul(w_ps[:, s, c], hs, hot_w[:, s, p, :, g], start=p == 0, stop=p == PARTS - 1)
                    for p in range(PARTS):
                        mm = pe.matmul(bias_ps[:, bank, 0:BCOLS], hot_eb[:, s, p * H:(p + 1) * H, :, g].rearrange("p h s -> p (h s)"),
                                       hot_bias[:, s, :, g], start=half == 0 and g == 0 and p == 0,
                                       stop=half == 1 and g == BATCH - 1 and p == PARTS - 1)
                hot_free[s] = by_pe.of(mm)

            def evacuate(n):
                s, half = n % 2, n % 2
                pair = n // 2
                bank = pair % 2
                done = hot_free[s]
                wait(dve, done)
                half_b = slice(half * BATCH, (half + 1) * BATCH)
                c_view = count[:].rearrange("p s (b m) -> p b m s", m=GN)[:, half_b, GROUP_DSTS * pair:GROUP_DSTS * pair + 2, :]
                ps_view = cnt_ps[:, s].rearrange("p (b m s) -> p b m s", m=GROUP_DSTS, s=NT)
                c1 = by_dve.of(dve.tensor_tensor(c_view, ps_view, c_view, ALU.add))
                wait(act, done, slab_free[0])
                w_at = (pair % 2) * GROUP_DSTS * NGRAPH + half * GROUP_DSTS * BATCH
                c2 = by_act.of(act.copy(w_slab[:, w_at:w_at + GROUP_DSTS * BATCH, :].rearrange("p d s -> p (d s)"), w_ps[:, s]))
                ps_free[s] = (c1, c2)
                if half == 1:
                    b_view = bias[:].rearrange("p i m -> p m i")[:, GROUP_DSTS * pair:GROUP_DSTS * pair + 2, :]
                    bias_free[bank] = by_dve.of(dve.tensor_tensor(
                        b_view, bias_ps[:, bank, 0:BCOLS].rearrange("p (m i) -> p m i", m=GROUP_DSTS), b_view, ALU.add))
                slab_done[0] = c2

            new_free, old_free, old_got = [None, None], [None, None], [None, None]

            def load_old(m):
                if m < NT * 4:
                    wait(sp, old_free[m % 2])
                    old_got[m % 2] = signals[f"old{m % 2}"].of(
                        sp.dma_start(w_old[:, m % 2], io["weight_dram"][m // 4, :, m % 4 * 512:(m % 4 + 1) * 512], cond=(r > 0)), 16)

            def weight_chunk(m):
                q, c = divmod(m, 4)
                bank = m % 2
                wait(pe, slab_done[0], turned_free[bank])
                for s1 in range(4):
                    mm = pe.transpose(turn_ps[:, bank, s1 * P:(s1 + 1) * P], w_slab[:, :, c * 4 + s1], ident[:])
                slab_free[0] = by_pe.of(mm)
                wait(dve, slab_free[0], old_got[bank], new_free[bank])
                old_free[bank] = turned_free[bank] = by_dve.of(dve.tensor_tensor(w_new[:, bank], turn_ps[:, bank], w_old[:, bank], ALU.add))
                load_old(m + 2)
                wait(sp, turned_free[bank])
                new_free[bank] = signals[f"store{bank}"].of(sp.dma_start(io["weight_dram"][q, :, c * 512:(c + 1) * 512], w_new[:, bank]), 16)

            load_old(0)
            load_old(1)
            gather(0)
            prep(0)
            gather(1)
            hots(0, 0)
            last = GTILES * NBATCH - 1
            for n in range(last + 1):
                if n < last:
                    hots(*divmod(n + 1, NBATCH))
                slab = n // 4 - 1 if n % 4 == 0 and n else None
                for half in range(2):
                    products(n, range(half * BATCH // 2, (half + 1) * BATCH // 2))
                    if slab is not None:
                        weight_chunk(4 * slab + 2 * half)
                        weight_chunk(4 * slab + 2 * half + 1)
                evacuate(n)
                t, i = divmod(n, NBATCH)
                if i == 3 and t + 1 < GTILES:
                    prep(t + 1)
                    if t + 2 < GTILES:
                        gather(t + 2)
            for m in range(NT * 4 - 4, NT * 4):
                weight_chunk(m)
            wait(sp, *((signals[x], signals[x].value) for x in ("old0", "old1", "store0", "store1")))
            nc.all_engine_barrier()
            pool.dma_reset(range(nums[0], nums[-1] + 1))
            pool.sem_clear(range(nums[0], nums[-1] + 1))
            nc.all_engine_barrier()


def layer_norm_scales(nc, by_dve, by_act, x, x_ready, stats, rstd, shift):
    dve, act = nc.vector, nc.scalar
    moments = stats[:, 6 * NT:8 * NT].rearrange("p (t two) -> p t two", two=2)
    for t in range(NT):
        wait(dve, x_ready[t])
        mark = by_dve.of(dve.bn_stats(stats[:, 6 * t:6 * t + 6], x[:, t, :]))
    wait(dve, mark)
    for t in range(NT):
        mark = by_dve.of(dve.bn_aggr(moments[:, t, :], stats[:, 6 * t:6 * t + 6]))
    wait(dve, mark)
    mark = by_dve.of(dve.tensor_scalar(rstd[:], moments[:, :, 1], LN_EPS, None, ALU.add))
    wait(act, mark)
    mark = by_act.of(act.sqrt(rstd[:], rstd[:]))
    wait(dve, mark)
    mark = by_dve.of(dve.reciprocal(rstd[:], rstd[:]))
    wait(dve, mark)
    return by_dve.of(dve.scalar_tensor_tensor(shift[:], moments[:, :, 0], -1.0, rstd[:], ALU.mult, ALU.mult))


def weight_view(w):
    return w.rearrange("(k p) n -> p k n", p=P)


def column_view(v):
    return v.rearrange("(k p) -> p k", p=P)


def attention(nc, io, keep):
    pe, dve, act, pool, sp = nc.tensor, nc.vector, nc.scalar, nc.gpsimd, nc.sync
    ident, bias, x = keep["ident"], keep["bias"], keep["x"]
    by_pe, by_dve, by_act, by_pool = (Signals(nc, f"att_{n}") for n in ("pe", "dve", "act", "pool"))
    with ExitStack() as mem:
        sb = lambda *a: mem.enter_context(nc.sbuf_tensor(*a))
        ps = lambda *a: mem.enter_context(nc.psum_tensor(*a))
        wq, wk, wv, wo = (sb(f"w{n}_sb", [P, KT, D], F32) for n in "qkvo")
        bq_col, bk_col = (sb(f"b{n}_col", [P, KT], F32) for n in "qk")
        bv_row, bo_row = (sb(f"b{n}_row", [P, D], F32) for n in "vo")
        stats, rstd, shift = sb("stats0", [P, 8 * NT], F32), sb("rstd0", [P, NT], F32), sb("shift0", [P, NT], F32)
        h = sb("h0", [P, D], F32)
        h_t = sb("h0_t", [P, KT, 2 * P], F32)
        q_split = sb("q_split", [P, KT, 2 * P // SB16, 2, SB16], F32)
        k_t = sb("k_t", [P, KT, 2 * P], F32)
        v = sb("v", [P, 2, 2, D], F32)
        prob = sb("prob", [P, 2, D], F32)
        prob_t = sb("prob_t", [P, D], F32)
        att_t = sb("att_t", [P, KT, P], F32)
        row_max, row_sum = sb("row_max", [P, 2, 8], F32), sb("row_sum", [P, 2, 8], F32)
        turn_ps = ps("turn3_ps", [P, 512], F32)
        proj_ps = ps("proj_ps", [P, 2, 512], F32)
        s_ps = ps("s_ps", [P, 2, 512], F32)
        pt_ps = ps("pt_ps", [P, 512], F32)
        av_ps = ps("av_ps", [P, 2, 512], F32)

        in_x = [Signals(nc, f"in_x{i}") for i in range(4)]
        x_ready = [None] * NT
        x_view = io["x"].rearrange("(t p) d -> p t d", p=P)
        for i in range(4):
            got = in_x[i].of(sp.dma_start(x[:, 4 * i:4 * i + 4, :], x_view[:, 4 * i:4 * i + 4, :]), 16)
            x_ready[4 * i:4 * i + 4] = [got] * 4
        in_w = {}
        for n, w in (("q", wq), ("k", wk), ("v", wv), ("o", wo)):
            in_w[n] = Signals(nc, f"in_w{n}").of(act.dma_start(w[:], weight_view(io[f"L0_gnn_W{n}"])), 16)
        in_b = Signals(nc, "in_b")
        with nc.allow_non_contiguous_dma(reason="a bias by partitions"):
            in_b.of(sp.dma_start(bq_col[:], column_view(io["L0_gnn_bq"])), 16)
            in_b.of(sp.dma_start(bk_col[:], column_view(io["L0_gnn_bk"])), 16)
        in_b.of(sp.dma_start(bv_row[:], io["L0_gnn_bv"].unsqueeze(0).to_broadcast([P, D])), 16)
        got_b = in_b.of(sp.dma_start(bo_row[:], io["L0_gnn_bo"].unsqueeze(0).to_broadcast([P, D])), 16)

        scale = float(HD) ** -0.5
        q_zero = by_dve.of(dve.memset(q_split[:], 0.0))
        wait(dve, got_b)
        bq_scaled = by_dve.of(dve.tensor_scalar(bq_col[:], bq_col[:], scale, None, ALU.mult))
        wait(act, q_zero, bq_scaled)
        normed = layer_norm_scales(nc, by_dve, by_act, x, x_ready, stats, rstd, shift)

        turn_free = h_free = h_t_free = q_free = k_free = pt_free = None
        proj_free = [None, None]
        s_free, av_free, v_free, prob_free = [None, None], [None, None], [None, None], [None, None]
        prob_t_free = att_t_free = None
        proj_n = 0
        slab_done = {}

        def project(slab):
            nonlocal turn_free, h_free, h_t_free, proj_n
            for j in range(2):
                t = 2 * slab + j
                wait(act, normed, h_free)
                a = by_act.of(act.activation(h[:], x[:, t, :], ACT.Relu, bias=shift[:, t:t + 1], scale=rstd[:, t:t + 1]))
                wait(pe, a, turn_free)
                for k in range(KT):
                    mm = pe.transpose(turn_ps[:, k * P:(k + 1) * P], h[:, k * P:(k + 1) * P], ident[:])
                h_free = by_pe.of(mm)
                wait(act, h_free, h_t_free)
                turn_free = by_act.of(act.copy(h_t[:, :, j * P:(j + 1) * P], turn_ps[:].rearrange("p (k n) -> p k n", k=KT)))
            wait(pe, turn_free)
            for w, n in ((wq, "q"), (wk, "k")):
                wait(pe, in_w[n])
                for m in range(KT):
                    s = proj_n % 2
                    proj_n += 1
                    wait(pe, proj_free[s])
                    for k in range(KT):
                        mm = pe.matmul(proj_ps[:, s, 0:2 * P], w[:, k, m * P:(m + 1) * P], h_t[:, k, :], start=k == 0, stop=k == KT - 1)
                    a = by_pe.of(mm)
                    if n == "q":
                        wait(act, a, q_free)
                        for half in range(2):
                            rows = slice(half * HD, (half + 1) * HD)
                            q_done = by_act.of(act.activation(
                                q_split[rows, m, :, half, :], proj_ps[rows, s, 0:2 * P].rearrange("p (i s) -> p i s", s=SB16),
                                ACT.Identity, bias=bq_col[rows, m:m + 1], scale=scale))
                        proj_free[s] = q_done
                    else:
                        wait(dve, a, k_free)
                        proj_free[s] = k_done = by_dve.of(dve.tensor_scalar(k_t[:, m, :], proj_ps[:, s, 0:2 * P], bk_col[:, m:m + 1], None, ALU.add))
            wait(pe, in_w["v"])
            vs = slab % 2
            for j in range(2):
                s = proj_n % 2
                proj_n += 1
                wait(pe, proj_free[s])
                for k in range(KT):
                    mm = pe.matmul(proj_ps[:, s], h_t[:, k, j * P:(j + 1) * P], wv[:, k, :], start=k == 0, stop=k == KT - 1)
                h_t_free = by_pe.of(mm)
                wait(dve, h_t_free, v_free[vs])
                proj_free[s] = v_done = by_dve.of(dve.tensor_tensor(v[:, vs, j, :], proj_ps[:, s], bv_row[:], ALU.add))
            slab_done[slab] = (q_done, k_done, v_done)

        def scores(slab, j):
            nonlocal q_free, k_free
            t = 2 * slab + j
            s = j
            wait(pe, *slab_done[slab], s_free[s])
            for i in range(4):
                for g in range(2):
                    blk = j * 8 + g * 4 + i
                    nodes = slice(j * P + g * GN, j * P + (g + 1) * GN)
                    for k in range(KT):
                        c = (i * 2 + g) * GN
                        mm = pe.matmul(s_ps[32 * k:32 * k + 32, s, c:c + GN], q_split[:, k, blk].rearrange("p z s -> p (z s)"),
                                       k_t[:, k, nodes], start=True, stop=True)
            q_free = k_free = by_pe.of(mm)
            wait(dve, q_free, prob_free[s])
            p4 = prob[:, s].rearrange("p (i g m) -> p i g m", i=4, g=2)
            a = s_free[s] = by_dve.of(dve.tensor_tensor(
                p4, s_ps[:, s].rearrange("p (i g m) -> p i g m", i=4, g=2),
                bias[:, t * 8:t * 8 + 8, :].rearrange("p (g i) m -> p i g m", g=2), ALU.add))
            wait(dve, a)
            p3 = prob[:, s].rearrange("p (r m) -> p r m", m=GN)
            wide = [P, 8, GN]
            a = by_dve.of(dve.tensor_reduce(row_max[:, s], p3, axis=AX.X, op=ALU.max))
            wait(dve, a)
            a = by_dve.of(dve.tensor_tensor(p3, p3, row_max[:, s].unsqueeze(2).to_broadcast(wide), ALU.subtract))
            wait(act, a)
            a = by_act.of(act.activation(prob[:, s], prob[:, s], ACT.Exp))
            wait(dve, a)
            a = by_dve.of(dve.tensor_reduce(row_sum[:, s], p3, axis=AX.X, op=ALU.add))
            wait(dve, a)
            a = by_dve.of(dve.reciprocal(row_sum[:, s], row_sum[:, s]))
            wait(dve, a)
            prob_done[s] = by_dve.of(dve.tensor_tensor(p3, p3, row_sum[:, s].unsqueeze(2).to_broadcast(wide), ALU.mult))

        prob_done = [None, None]

        def mix(slab, j):
            nonlocal pt_free, prob_t_free, att_t_free, proj_n
            t, s, vs = 2 * slab + j, j, slab % 2
            wait(pe, prob_done[s], pt_free)
            for i in range(4):
                mm = pe.transpose(pt_ps[:, i * P:(i + 1) * P], prob[:, s, i * P:(i + 1) * P], ident[:])
            prob_free[s] = by_pe.of(mm)
            wait(act, prob_free[s], prob_t_free)
            pt_free = by_act.of(act.copy(prob_t[:], pt_ps[:]))
            for g in range(2):
                rows = slice(g * GN, (g + 1) * GN)
                wait(pe, pt_free, av_free[g])
                for hd in range(H):
                    mm = pe.matmul(av_ps[HD * (hd % 2):HD * (hd % 2) + HD, g, (hd // 2) * GN:(hd // 2 + 1) * GN],
                                   v[rows, vs, j, hd * HD:(hd + 1) * HD],
                                   prob_t[rows].rearrange("p (i h s) -> p i h s", h=H, s=SB16)[:, :, hd, :], start=True, stop=True)
                prob_t_free = v_free[vs] = by_pe.of(mm)
                wait(act, prob_t_free, att_t_free)
                av_free[g] = by_act.of(act.copy(att_t[:, :, g * GN:(g + 1) * GN], av_ps[:, g, 0:KT * GN].rearrange("p (k n) -> p k n", k=KT)))
            s = proj_n % 2
            proj_n += 1
            wait(pe, av_free[1], proj_free[s], in_w["o"])
            for k in range(KT):
                mm = pe.matmul(proj_ps[:, s], att_t[:, k, :], wo[:, k, :], start=k == 0, stop=k == KT - 1)
            att_t_free = by_pe.of(mm)
            wait(dve, att_t_free, x_plus[t])
            proj_free[s] = by_dve.of(dve.tensor_tensor(x[:, t, :], x[:, t, :], proj_ps[:, s], ALU.add))
            wait(sp, proj_free[s])
            stored[0] = out_x.of(sp.dma_start(io["x_dram"][t * P:(t + 1) * P, :], x[:, t, :]), 16)

        out_x, stored = Signals(nc, "out_x0"), [None]
        x_plus = {}

        def add_bo(slab):
            for j in range(2):
                t = 2 * slab + j
                wait(pool, h_free, got_b)
                x_plus[t] = by_pool.of(pool.tensor_tensor(x[:, t, :], x[:, t, :], bo_row[:], ALU.add))

        project(0)
        add_bo(0)
        for slab in range(NT // 2):
            scores(slab, 0)
            scores(slab, 1)
            if slab + 1 < NT // 2:
                project(slab + 1)
                add_bo(slab + 1)
            mix(slab, 0)
            mix(slab, 1)
        wait(sp, stored[0])
        nc.all_engine_barrier()


def graph_layers(nc, io, keep):
    pe, dve, act, pool, sp = nc.tensor, nc.vector, nc.scalar, nc.gpsimd, nc.sync
    ident, count = keep["ident"], keep["count"]
    by_pe, by_dve, by_act, by_pool = (Signals(nc, f"gcn_{n}") for n in ("pe", "dve", "act", "pool"))
    GROUPS, PER = 4, NT // 4
    COLS = PER * P
    with ExitStack() as mem:
        sb = lambda *a: mem.enter_context(nc.sbuf_tensor(*a))
        ps = lambda *a: mem.enter_context(nc.psum_tensor(*a))
        g = sb("g", [P, NT, 2, D], F32R)
        h_t = sb("h_gcn_t", [P, KT, N], F32)
        split = sb("split", [P, 3, KT * D], F32R)
        dis_row = sb("dis_row", [P, N], F32)
        tiles = sb("tiles", [P, PER, D], F32)
        h = sb("h_gcn", [P, D], F32)
        dis1, dis2 = sb("dis1", [P, NT], F32), sb("dis2", [P, NT], F32)
        b_col = sb("b_col", [P, 2, KT], F32)
        b_row = sb("b_row", [P, D], F32)
        ones_bf, one_f = sb("ones_bf", [P, P], BF16), sb("one_f", [P, 1], F32)
        stats = sb("stats1", [P, 8 * PER], F32)
        rstd, shift = sb("rstd1", [P, PER], F32), sb("shift1", [P, PER], F32)
        banks = ps("banks", [P, 8, 512], F32)
        turn_ps, prod_ps, agg_ps = banks[:, 0:2], banks[:, 2:4], banks[:, 4:8]
        chunk = split[:, 0].rearrange("p (r c) -> p r c", r=4)
        h_parts = split[:, 0].rearrange("p (r z k n) -> p r z k n", r=2, z=2, k=KT)
        w_parts = split[:, 1:3].rearrange("p z (k d) -> p z k d", k=KT)
        x_view = io["x_dram"].rearrange("(t p) d -> p t d", p=P)

        in_w, in_b = Signals(nc, "in_gcn_w"), Signals(nc, "in_gcn_b")
        in_x, out_x = ([Signals(nc, f"{n}_x1_{i}") for i in range(PER)] for n in ("in", "out"))
        turn_free, prod_free, agg_free = [None] * 2, [None] * 2, [None] * PER
        chunk_free = [None] * 4
        tile_free = [[] for _ in range(PER)]
        w_free = h_free = h_t_free = g_free = scales_free = None
        stored = [None] * NT
        x_got = [None] * PER

        def load_weights(name):
            for b in range(PER):
                wait(sp, *tile_free[b])
            return in_w.of(sp.dma_start(tiles[:], weight_view(io[name])), 16)

        def split_weights(k, got):
            wait(act, got, w_free)
            a = by_act.of(act.copy(w_parts[:, 0, k], tiles[:, k]))
            wait(dve, a)
            b = by_dve.of(dve.tensor_tensor(w_parts[:, 1, k], tiles[:, k], w_parts[:, 0, k].bitcast(F32), ALU.subtract))
            tile_free[k] = [b]
            return b

        def split_turned_weights(o, got):
            bank = o % 2
            wait(pe, got, turn_free[bank])
            for i in range(KT):
                mm = pe.transpose(turn_ps[:, bank, i * P:(i + 1) * P], tiles[:, o, i * P:(i + 1) * P], ident[:])
            turned = by_pe.of(mm)
            source = turn_ps[:, bank].rearrange("p (i o) -> p i o", i=KT)
            hi, lo = (w_parts[:, z, :, o * P:(o + 1) * P] for z in range(2))
            wait(act, turned, w_free)
            a = by_act.of(act.copy(hi, source))
            wait(dve, a)
            turn_free[bank] = by_dve.of(dve.tensor_tensor(lo, source, hi.bitcast(F32), ALU.subtract))
            tile_free[o] = [turned]
            return turn_free[bank]

        def load_x(t, b):
            wait(sp, stored[t], *tile_free[b])
            x_got[b] = in_x[b].of(sp.dma_start(tiles[:, b], x_view[:, t, :]), 16)

        def norm_scales(first, ready):
            slots = slice(first, first + len(ready))
            moments = stats[:, 6 * PER:].rearrange("p (t two) -> p t two", two=2)
            for b, mark in zip(range(first, PER), ready):
                wait(dve, mark)
                a = by_dve.of(dve.bn_stats(stats[:, 6 * b:6 * b + 6], tiles[:, b]))
            wait(dve, a)
            for b in range(slots.start, slots.stop):
                a = by_dve.of(dve.bn_aggr(moments[:, b], stats[:, 6 * b:6 * b + 6]))
            wait(dve, a, scales_free)
            a = by_dve.of(dve.tensor_scalar(rstd[:, slots], moments[:, slots, 1], LN_EPS, None, ALU.add))
            wait(act, a)
            a = by_act.of(act.sqrt(rstd[:, slots], rstd[:, slots]))
            wait(dve, a)
            a = by_dve.of(dve.reciprocal(rstd[:, slots], rstd[:, slots]))
            wait(dve, a)
            return by_dve.of(dve.scalar_tensor_tensor(shift[:, slots], moments[:, slots, 0], -1.0, rstd[:, slots], ALU.mult, ALU.mult))

        def relu_tile(b, normed):
            nonlocal scales_free
            wait(act, normed, h_free)
            a = scales_free = by_act.of(act.activation(h[:], tiles[:, b], ACT.Relu, bias=shift[:, b:b + 1], scale=rstd[:, b:b + 1]))
            tile_free[b] = tile_free[b] + [a]
            return a

        def turn_tile(t, relued, by_graph):
            nonlocal h_free
            bank = t % 2
            wait(pe, relued, turn_free[bank])
            for k in range(KT):
                mm = pe.transpose(turn_ps[:, bank, k * P:(k + 1) * P], h[:, k * P:(k + 1) * P], ident[:])
            h_free = by_pe.of(mm)
            wait(act, h_free, h_t_free)
            source = turn_ps[:, bank].rearrange("p (k n) -> p k n", k=KT)
            if by_graph:
                for k in range(KT):
                    out = h_t[:, k].rearrange("p (v b d) -> p v b d", b=NGRAPH, d=2)[:, :, 2 * t:2 * t + 2]
                    a = by_act.of(act.copy(out, source[:, k].rearrange("p (b v d) -> p v b d", b=2, d=2)))
            else:
                a = by_act.of(act.copy(h_t[:, :, t * P:(t + 1) * P], source))
            turn_free[bank] = a
            return a

        split_n = 0

        def split_h(t, h_ready):
            nonlocal split_n, h_t_free
            s = split_n % 2
            split_n += 1
            hi, lo = h_parts[:, s, 0], h_parts[:, s, 1]
            source = h_t[:, :, t * P:(t + 1) * P]
            wait(act, h_ready, chunk_free[2 * s], chunk_free[2 * s + 1])
            a = by_act.of(act.copy(hi, source))
            wait(dve, a)
            h_t_free = by_dve.of(dve.tensor_tensor(lo, source, hi.bitcast(F32), ALU.subtract))
            return s, h_t_free

        def product(t, h_split, w_ready, scale, bias_row):
            nonlocal w_free
            s, split_done = h_split
            hi, lo = h_parts[:, s, 0], h_parts[:, s, 1]
            wait(pe, split_done, w_ready, prod_free[s])
            passes = [(hi, k, 0) for k in range(KT)] + [(hi, k, 1) for k in range(KT)] + [(lo, k, 0) for k in range(KT)]
            for n, (part, k, z) in enumerate(passes):
                mm = pe.matmul(prod_ps[:, s], part[:, k], w_parts[:, z, k], start=n == 0, stop=n == len(passes) - 1)
            done = by_pe.of(mm)
            w_free = chunk_free[2 * s] = chunk_free[2 * s + 1] = done
            result = prod_ps[:, s]
            if bias_row is not None:
                wait(dve, done)
                done = by_dve.of(dve.tensor_tensor(result, result, bias_row, ALU.add))
            wait(act, done, g_free)
            hi, lo = g[:, t, 0], g[:, t, 1]
            if scale is None:
                a = by_act.of(act.copy(hi, result))
                wait(dve, a)
                b = by_dve.of(dve.tensor_tensor(lo, result, hi.bitcast(F32), ALU.subtract))
            else:
                a = by_act.of(act.activation(hi, result, ACT.Copy, scale=scale[:, t:t + 1]))
                wait(dve, a)
                b = by_dve.of(dve.scalar_tensor_tensor(lo, result, scale[:, t:t + 1], hi.bitcast(F32), ALU.mult, ALU.subtract))
            prod_free[s] = b
            return b

        def products(h_ready, w_ready, scale, bias_row, before=lambda t: None):
            ready, ahead = [], None
            for t in range(NT + 1):
                if t < NT:
                    before(t)
                    following = split_h(t, h_ready[t])
                if t > 0:
                    ready.append(product(t - 1, ahead, w_ready, scale, bias_row))
                ahead = following
            return ready

        chunk_read = [None] * NT

        def sums(g_ready, turned, finish, aside):
            nonlocal g_free
            steps = [(c, i) for c in range(GROUPS) for i in range(NT)]
            copied = {}

            def copy_chunk(n):
                if n < len(steps):
                    c, i = steps[n]
                    wait(dve, chunk_free[n % 4])
                    copied[n] = chunk_read[i] = by_dve.of(dve.tensor_copy(chunk[:, n % 4], count[:, i, c * COLS:(c + 1) * COLS]))
            for n in range(3):
                copy_chunk(n)
            for n, (c, i) in enumerate(steps):
                copy_chunk(n + 3)
                wait(pe, copied[n], g_ready[i])
                done = []
                for b in range(4):
                    if i == 0:
                        wait(pe, agg_free[b])
                    block = slice(b * P, (b + 1) * P)
                    for z in range(2):
                        lhs, rhs = (g[:, i, z, block], chunk[:, n % 4]) if turned else (chunk[:, n % 4, block], g[:, i, z])
                        mm = pe.matmul(agg_ps[:, b], lhs, rhs, start=i == 0 and z == 0, stop=i == NT - 1 and z == 1)
                    if i == NT - 1 or b == 3:
                        done.append(by_pe.of(mm))
                chunk_free[n % 4] = g_free = done[-1]
                if i == NT - 1:
                    finish(c, done)
                for f in aside.get((c, i), ()):
                    f()

        got = in_w.of(sp.dma_start(tiles[:], weight_view(io["L1_gnn_W1"])), 16)
        a = by_dve.of(dve.memset(ones_bf[:], 1.0))
        b = by_dve.of(dve.memset(one_f[:], 1.0))
        for t in range(NT):
            diag = count[:, t, t * P:(t + 1) * P]
            looped = by_dve.of(dve.tensor_tensor(diag, diag, ident[:], ALU.add))
        w_ready = [split_weights(k, got) for k in range(KT)]
        for b in range(PER):
            load_x(b, b)
        with nc.allow_non_contiguous_dma(reason="a bias by partitions"):
            in_b.of(sp.dma_start(b_col[:, 0, :], column_view(io["L1_gnn_b1"])), 16)
            in_b.of(sp.dma_start(b_col[:, 1, :], column_view(io["L1_gnn_b2"])), 16)
        got_b = in_b.of(sp.dma_start(b_row[:], io["L1_gnn_b3"].unsqueeze(0).to_broadcast([P, D])), 16)
        wait(act, got_b)
        wait(pool, got_b)
        wait(pe, looped)
        for c in range(4):
            for s in range(NT):
                mm = pe.matmul(agg_ps[:, c], ones_bf[:], count[:, s, c * 512:(c + 1) * 512], start=s == 0, stop=s == NT - 1)
            agg_free[c] = by_pe.of(mm)

        def start_pair(pair):
            first = pair % 2 * 2
            normed = norm_scales(first, [x_got[first], x_got[first + 1]])
            marks = []
            for b in range(first, first + 2):
                tile_free[b] = []
                relued = relu_tile(b, normed)
                t = 2 * pair + b - first
                marks.append(turn_tile(t, relued, False))
                if t + 4 < NT:
                    load_x(t + 4, b)
            return marks
        h_ready = start_pair(0)
        for c in range(4):
            wait(dve, agg_free[c])
            agg_free[c] = by_dve.of(dve.tensor_scalar(dis_row[:, c * 512:(c + 1) * 512], agg_ps[:, c], 1.0, None, ALU.max))
        wait(act, agg_free[3])
        a = by_act.of(act.sqrt(dis_row[:], dis_row[:]))
        wait(dve, a)
        a = by_dve.of(dve.reciprocal(dis_row[:], dis_row[:]))
        wait(pe, a, turn_free[0])
        for t in range(NT):
            mm = pe.matmul(turn_ps[:, 0, t:t + 1], dis_row[0:1, t * P:(t + 1) * P], one_f[0:1, :], start=True, stop=True)
        a = by_pe.of(mm)
        wait(dve, a)
        turn_free[0] = by_dve.of(dve.tensor_copy(dis1[:], turn_ps[:, 0, 0:NT]))
        wait(act, turn_free[0])
        h_ready += start_pair(1)

        def pair_ahead(t):
            if t % 2 == 0 and t + 4 < NT:
                h_ready.extend(start_pair(t // 2 + 2))
        g_ready = products(h_ready, w_ready, dis1, None, pair_ahead)
        staged = [load_weights("L1_gnn_W2")]

        def sum_out(i):
            nonlocal dis2_done
            wait(dve, looped)
            a = by_dve.of(dve.tensor_reduce(dis2[:, i:i + 1], count[:, i], axis=AX.X, op=ALU.add))
            if i == NT - 1:
                wait(act, a)
                a = by_act.of(act.sqrt(dis2[:], dis2[:]))
                wait(dve, a)
                dis2_done = by_dve.of(dve.reciprocal(dis2[:], dis2[:]))
        dis2_done = None

        def next_weights(split_one, after):
            w_ready.clear()
            aside = {(0, 1 + k): [lambda k=k: w_ready.append(split_one(k, staged[0]))] for k in range(KT)}
            aside[0, 5] = [after]
            return aside

        for layer in range(2):
            marks = [None] * GROUPS

            def to_h_t(c, done):
                cols = slice(c * COLS, (c + 1) * COLS)
                for k in range(KT):
                    wait(dve, done[k], h_t_free)
                    agg_free[k] = by_dve.of(dve.tensor_tensor(h_t[:, k, cols], agg_ps[:, k], dis_row[:, cols], ALU.mult))
                    wait(act, agg_free[k])
                    marks[c] = by_act.of(act.activation(h_t[:, k, cols], h_t[:, k, cols], ACT.Relu, bias=b_col[:, layer, k:k + 1]))

            def stage():
                staged[0] = load_weights("L1_gnn_W3" if layer == 0 else "L2_gnn_W")
            aside = next_weights(split_weights, stage)
            if layer == 0:
                for i in range(NT):
                    aside[1 + i // 6, 1 + i % 6 * 2] = [lambda i=i: sum_out(i)]
            sums(g_ready, True, to_h_t, aside)
            g_ready = products([marks[t // PER] for t in range(NT)], w_ready, dis1, None)

        def sums_into_x(g_ready, split_one, finish_tile, by_graph):
            h_ready = [None] * NT
            relued, normed = [None], [None]

            def finish(c, done):
                ready = []
                for b in range(PER):
                    t = c * PER + b
                    mark = finish_tile(t, b, done[b])
                    ready.append(mark)
                    wait(sp, mark)
                    stored[t] = out_x[b].of(sp.dma_start(x_view[:, t, :], tiles[:, b]), 16)
                    tile_free[b] = [stored[t]]
                normed[0] = norm_scales(0, ready)

            def relu(b):
                relued[0] = relu_tile(b, normed[0])

            def turn(c, b):
                h_ready[c * PER + b] = turn_tile(c * PER + b, relued[0], by_graph)

            def load_group(c):
                for b in range(PER):
                    load_x(c * PER + b, b)
            aside = next_weights(split_one, lambda: load_group(0))
            for c in range(1, GROUPS):
                for b in range(PER):
                    aside[c, 3 + 2 * b] = [lambda b=b: relu(b)]
                    aside[c, 4 + 2 * b] = [lambda c=c, b=b: turn(c - 1, b)]
                aside[c, 10].append(lambda c=c: load_group(c))
            sums(g_ready, False, finish, aside)

            def last(b):
                relu(b)
                turn(GROUPS - 1, b)
            return h_ready, last

        def finish_layer1(t, b, done):
            wait(pool, x_got[b])
            a = by_pool.of(pool.tensor_tensor(tiles[:, b], tiles[:, b], b_row[:], ALU.add))
            wait(dve, done, a)
            agg_free[b] = by_dve.of(dve.scalar_tensor_tensor(tiles[:, b], agg_ps[:, b], dis1[:, t:t + 1], tiles[:, b], ALU.mult, ALU.add))
            return agg_free[b]

        h_ready, last = sums_into_x(g_ready, split_turned_weights, finish_layer1, False)
        wait(sp, agg_free[PER - 1])
        got_b = in_b.of(sp.dma_start(b_row[:], io["L2_gnn_b"].unsqueeze(0).to_broadcast([P, D])), 16)
        wait(dve, got_b)
        wait(act, dis2_done)

        def last_ahead(t):
            if t % 2 == 1 and t // 2 < PER:
                last(t // 2)
        g_ready = products(h_ready, w_ready, dis2, b_row[:], last_ahead)
        staged[0] = load_weights("L3_gnn_weight")

        def finish_layer2(t, b, done):
            wait(act, done)
            a = by_act.of(act.activation(agg_ps[:, b], agg_ps[:, b], ACT.Relu, scale=dis2[:, t:t + 1]))
            wait(dve, a, x_got[b])
            agg_free[b] = by_dve.of(dve.tensor_tensor(tiles[:, b], tiles[:, b], agg_ps[:, b], ALU.add))
            return agg_free[b]

        h_ready, last = sums_into_x(g_ready, split_weights, finish_layer2, True)
        HALF = N // 2
        raw = count[:].rearrange("p t n -> p (t n)").bitcast(F32).rearrange("p (r c) -> p r c", c=HALF)
        in_raw = [Signals(nc, f"in_raw{i}") for i in range(NT)]
        raw_got, raw_free = {}, {i: chunk_read[i] for i in range(NT)}

        def load_raw(n):
            half, q = divmod(n, NT)
            wait(sp, raw_free[q])
            raw_got[n] = in_raw[q].of(sp.dma_start(raw[:, q], io["weight_dram"][q, :, half * HALF:(half + 1) * HALF]), 16)
        wait(sp, g_free)
        for n in range(NT):
            load_raw(n)
        for b in range(PER):
            last(b)
        wait(act, h_free)
        g_ready = products([h_ready[-1]] * NT, w_ready, None, None)
        x_all = h_t[:].rearrange("p k n -> p (k n)").rearrange("p (t d) -> p t d", d=D)
        in_x_all = Signals(nc, "in_x_all")
        wait(sp, h_t_free, *stored)
        x_all_got = in_x_all.of(sp.dma_start(x_all, x_view), 16)

        part = split[:].rearrange("p s (z c) -> p s z c", z=2)
        part_free = [[chunk_free[0], chunk_free[2], w_free]] * 3
        part_ready = {}

        def split_raw(n):
            if n >= 2 * NT:
                return
            q, s = n % NT, n % 3
            wait(act, raw_got[n], part_free[s])
            a = by_act.of(act.copy(part[:, s, 0], raw[:, q]))
            wait(dve, a)
            b = by_dve.of(dve.tensor_tensor(part[:, s, 1], raw[:, q], part[:, s, 0].bitcast(F32), ALU.subtract))
            part_ready[n] = raw_free[q] = b
            if n + NT < 2 * NT:
                load_raw(n + NT)
        for n in range(2):
            split_raw(n)
        acc_free = turn_free + prod_free + agg_free
        outs = [Signals(nc, f"out_y{i}") for i in range(PER)]
        y_free = [tile_free[b] for b in range(PER)]
        out_view = io["out"].rearrange("(t p) d -> p t d", p=P)
        for n in range(2 * NT):
            half, q = divmod(n, NT)
            split_raw(n + 2)
            wait(pe, part_ready[n], g_ready[q])
            for b in range(8):
                if q == 0:
                    wait(pe, acc_free[b])
                for z, gz in ((0, 0), (0, 1), (1, 0)):
                    mm = pe.matmul(banks[:, b], part[:, n % 3, z, b * P:(b + 1) * P], g[:, q, gz],
                                   start=q == 0 and (z, gz) == (0, 0), stop=q == NT - 1 and z == 1)
                if q == NT - 1 or b == 7:
                    done = by_pe.of(mm)
                if q == NT - 1:
                    t = half * 8 + b
                    slot = t % PER
                    wait(dve, done, x_all_got, *y_free[slot])
                    acc_free[b] = by_dve.of(dve.scalar_tensor_tensor(tiles[:, slot], banks[:, b], 0.0, x_all[:, t], ALU.max, ALU.add))
                    wait(sp, acc_free[b])
                    y_free[slot] = [outs[slot].of(sp.dma_start(out_view[:, t, :], tiles[:, slot]), 16)]
            part_free[n % 3] = [done]
        for slot in range(PER):
            wait(sp, *y_free[slot])


INPUTS = ("x", "src", "dst", "edge_attr_16", "edge_weight", "L0_gnn_Wq", "L0_gnn_bq", "L0_gnn_Wk", "L0_gnn_bk",
          "L0_gnn_Wv", "L0_gnn_bv", "L0_gnn_Wo", "L0_gnn_bo", "L0_gnn_We", "L0_gnn_be", "L1_gnn_W1", "L1_gnn_b1",
          "L1_gnn_W2", "L1_gnn_b2", "L1_gnn_W3", "L1_gnn_b3", "L2_gnn_W", "L2_gnn_b", "L3_gnn_weight")


def program(nc, io):
    io = dict(io)
    io["rec_dram"] = nc.dram_tensor("rec_dram", [NBLK + 1, REC], F32, kind="Internal").ap()
    io["weight_dram"] = nc.dram_tensor("weight_dram", [NT, P, N], F32, kind="Internal").ap()
    io["x_dram"] = nc.dram_tensor("x_dram", [N, D], F32, kind="Internal").ap()
    with ExitStack() as mem:
        sb = lambda *a: mem.enter_context(nc.sbuf_tensor(*a))
        keep = {
            "ident": sb("ident", [P, P], F32),
            "blocks": sb("blocks", [P, GTILES, WIN], F32),
            "rounds": sb("rounds", [P, 1], I32),
        }
        make_identity(nc, keep)
        edge_prep(nc, io, keep)
        keep["count"] = sb("count", [P, NT, N], BF16)
        with ExitStack() as edges:
            keep["bias"] = edges.enter_context(nc.sbuf_tensor("bias", [P, SHI, GN], F32))
            keep["x"] = edges.enter_context(nc.sbuf_tensor("x_sb", [P, NT, D], F32))
            build_matrices(nc, io, keep)
            attention(nc, io, keep)
        graph_layers(nc, io, keep)


def kernel(**inputs):
    import concourse.bacc as bacc
    from concourse.bass_utils import run_bass_kernel_spmd

    nc = bacc.Bacc("TRN2", target_bir_lowering=False, num_devices=1)
    arrays, io = {}, {}
    for name in INPUTS:
        a = np.ascontiguousarray(inputs[name])
        arrays[f"in_{name}"] = a
        io[name] = nc.dram_tensor(f"in_{name}", a.shape, mybir.dt.from_np(a.dtype), kind="ExternalInput").ap()
    io["out"] = nc.dram_tensor("out_x", [N, D], F32, kind="ExternalOutput").ap()
    program(nc, io)
    r = run_bass_kernel_spmd(nc, [arrays], core_ids=[0])
    return r.results[0]["out_x"]
```

```python
from contextlib import ExitStack

import numpy as np
import concourse.bass as bass
from concourse import mybir
from concourse.alu_op_type import AluOpType as ALU

F32, F32R, BF16, F16 = mybir.dt.float32, mybir.dt.float32r, mybir.dt.bfloat16, mybir.dt.float16
I32, U32 = mybir.dt.int32, mybir.dt.uint32
ACT = mybir.ActivationFunctionType
AX = mybir.AxisListType

P = 128
N = 2048
D = 512
E = 67584
ED = 16
H = 8
HD = D // H
GN = 64
NT = N // P
KT = D // P
NGRAPH = N // GN

PARTS = 3
WHALF = P // 2
HGRAPH = NGRAPH // 2
NUNIT = N // 2
GTILES = NUNIT // P
CPT = GN // GTILES
BATCH = HGRAPH
NBATCH = P // BATCH
EPP = E // P
HIST = 66
FIELDS = 3 + H
CCOLS = 2 * NT
ROUNDS_MAX = E // WHALF + 1
POOL_HEADS = 1
LN_EPS = 1e-5


class Signals:

    def __init__(self, nc, name):
        self.sem, self.value, self.seen = nc.alloc_semaphore(name), 0, {}

    def of(self, instruction, by=1):
        instruction.then_inc(self.sem, by)
        self.value += by
        return self, self.value


def wait(engine, *marks):
    for mark in marks:
        if mark is None:
            continue
        if isinstance(mark, list):
            wait(engine, *mark)
            continue
        signals, value = mark
        if signals.seen.get(id(engine), 0) < value:
            engine.wait_ge(signals.sem, value)
            signals.seen[id(engine)] = value


def make_constants(nc, keep):
    pool = nc.gpsimd
    made = Signals(nc, "constants")
    a = made.of(pool.memset(keep["ident"][:], 0.0))
    wait(pool, a)
    a = made.of(pool.affine_select(out=keep["ident"][:], in_=keep["ident"][:], compare_op=ALU.not_equal, fill=1.0, base=0,
                                   pattern=[[-1, P]], channel_multiplier=1))
    exact = {"allow_small_or_imprecise_dtypes": True}
    for half in range(2):
        rows = slice(half * WHALF, (half + 1) * WHALF)
        wait(pool, a)
        a = made.of(pool.iota(keep["d0"][rows], pattern=[[1, CPT], [GN, HGRAPH]], base=half * HGRAPH * GN, channel_multiplier=0, **exact))
        wait(pool, a)
        a = made.of(pool.iota(keep["iota_cnt"][rows], pattern=[[1, CCOLS], [0, BATCH]], base=-half * NT, channel_multiplier=0, **exact))
    wait(pool, a)
    keep["constants"] = made.of(pool.iota(keep["iota_rep"][:], pattern=[[1, P], [0, BATCH]], base=0, channel_multiplier=0, **exact))


def scales_from_moments(nc, by_dve, by_act, moments, rstd, shift):
    dve, act = nc.vector, nc.scalar
    wait(dve, (by_dve, by_dve.value))
    mark = by_dve.of(dve.tensor_scalar(rstd[:], moments[:, :, 1], LN_EPS, None, ALU.add))
    wait(act, mark)
    mark = by_act.of(act.sqrt(rstd[:], rstd[:]))
    wait(dve, mark)
    mark = by_dve.of(dve.reciprocal(rstd[:], rstd[:]))
    wait(dve, mark)
    return by_dve.of(dve.scalar_tensor_tensor(shift[:], moments[:, :, 0], -1.0, rstd[:], ALU.mult, ALU.mult))


def edge_prep(nc, io, keep):
    pe, dve, act, pool, sp = nc.tensor, nc.vector, nc.scalar, nc.gpsimd, nc.sync
    by_pe, by_dve, by_act, by_pool = (Signals(nc, f"prep_{x}") for x in ("pe", "dve", "act", "pool"))
    with ExitStack() as mem:
        sb = lambda *a: mem.enter_context(nc.sbuf_tensor(*a))
        ps = lambda *a: mem.enter_context(nc.psum_tensor(*a))
        attr = sb("attr", [P, EPP * ED], F32)
        rec = sb("rec", [P, EPP, FIELDS], F32)
        src_i = sb("src_i", [P, EPP], I32)
        dst_i = sb("dst_i", [P, EPP], I32)
        dst_next = sb("dst_next", [P, EPP], I32)
        step_f = sb("step_f", [P, EPP], F32)
        graph_i = sb("graph_i", [P, EPP], I32)
        class_i = sb("class_i", [P, EPP], I32)
        graph_key = sb("graph_key", [P, EPP], BF16)
        class_key = sb("class_key", [P, EPP], BF16)
        ew = sb("ew", [P, EPP], F32)
        we_diag = sb("we_diag", [P, H, 8], F32)
        be_row = sb("be_row", [P, H], F32)
        attr_t = sb("attr_t", [P, 2, 512], F32)
        iota_hist = sb("iota_hist", [P, GN, HIST], BF16)
        graph_hot = sb("graph_hot", [P, 2, NGRAPH, HIST], BF16)
        class_hot = sb("class_hot", [P, 2, GN, HIST], BF16)
        pad = sb("pad", [1, WHALF * FIELDS], F32)
        small = sb("small", [P, 1024], F32)
        small_i = sb("small_i", [P, 160], I32)
        x_part = sb("x_part", [P, 2, 4, D], F32)
        stats = sb("stats0", [P, 8 * NT], F32)
        turn_ps = ps("turn_ps", [P, 2, 512], F32)
        eb_ps = ps("eb_ps", [P, 2, 512], F32)
        hist_ps = ps("hist_ps", [P, 512], F32)
        misc_ps = ps("misc_ps", [P, 512], F32)
        in_src, in_dst, in_attr, in_w, in_we = (Signals(nc, f"in_{x}") for x in ("src", "dst", "attr", "w", "we"))
        got_dst = in_dst.of(sp.dma_start(dst_i[:], io["dst"].rearrange("(p j) -> p j", p=P)), 16)
        got_src = in_src.of(sp.dma_start(src_i[:], io["src"].rearrange("(p j) -> p j", p=P)), 16)
        got_w = in_w.of(sp.dma_start(ew[:], io["edge_weight"].rearrange("(p j) -> p j", p=P)), 16)
        we_zero = by_dve.of(dve.memset(we_diag[:], 0.0))
        wait(sp, we_zero)
        with nc.allow_non_contiguous_dma(reason="a 16 x 8 matrix"):
            for e in range(8):
                got_we = in_we.of(sp.dma_start(we_diag[e * ED:(e + 1) * ED, :, e], io["L0_gnn_We"]), 16)
        got_we = in_we.of(sp.dma_start(be_row[:], io["L0_gnn_be"].unsqueeze(0).to_broadcast([P, H])), 16)
        got_attr = in_attr.of(act.dma_start(attr[:], io["edge_attr_16"].rearrange("(p j) f -> p (j f)", p=P)), 16)
        filled = by_dve.of(dve.memset(dst_next[:], N))
        wait(sp, filled)
        in_next = Signals(nc, "in_next")
        in_next.of(sp.dma_start(dst_next[0:P - 1, :], io["dst"][1:1 + (P - 1) * EPP].rearrange("(p j) -> p j", p=P - 1)), 16)
        got_next = in_next.of(sp.dma_start(dst_next[P - 1:P, 0:EPP - 1], io["dst"][1 + (P - 1) * EPP:E].unsqueeze(0)), 16)

        x_view = io["x"].rearrange("(t p) d -> p t d", p=P)
        in_x = [Signals(nc, f"in_x_stats{i}") for i in range(2)]
        wait(sp, got_attr)
        x_got = [in_x[i].of(sp.dma_start(x_part[:, i], x_view[:, 4 * i:4 * i + 4, :]), 16) for i in range(2)]
        ident = keep["ident"]
        out_rec = Signals(nc, "out_rec")
        nblk8 = EPP // 8
        per = 4
        turned_free, eb_free, attr_t_free = [None, None], [None, None], [None, None]
        turned = {}
        rec_view = io["rec_dram"][0:E, :].rearrange("(p j) f -> p j f", p=P)

        def turn_attr(i0):
            s = i0 // per % 2
            blocks = range(i0, min(i0 + per, nblk8))
            if not blocks:
                return
            wait(pe, got_attr, keep["constants"], turned_free[s])
            for i in blocks:
                mm = pe.transpose(turn_ps[:, s, (i - i0) * P:(i - i0 + 1) * P], attr[:, i * P:(i + 1) * P], ident[:])
            t = by_pe.of(mm)
            wait(act, t, attr_t_free[s])
            cols = slice(0, len(blocks) * P)
            turned_free[s] = turned[i0] = by_act.of(act.copy(attr_t[:, s, cols], turn_ps[:, s, cols]))

        def edge_bias(i0):
            n = min(8, nblk8 - i0)
            e = (i0 // 8) % 2
            if i0 == 0:
                turn_attr(0)
            wait(pe, got_we, eb_free[e])
            for j0 in range(i0, i0 + n, per):
                s = j0 // per % 2
                turn_attr(j0 + per)
                wait(pe, turned[j0])
                for i in range(j0, min(j0 + per, nblk8)):
                    mm = pe.matmul(eb_ps[:, e, (i - i0) * 64:(i - i0 + 1) * 64], attr_t[:, s, (i - j0) * P:(i - j0 + 1) * P],
                                   we_diag[:].rearrange("p h e -> p (h e)"), start=True, stop=True)
                attr_t_free[s] = by_pe.of(mm)
            wait(dve, attr_t_free[s], got_we)
            eb = eb_ps[:, e, 0:n * 64].rearrange("p (b h e) -> p b e h", h=H, e=8)
            out = rec[:, i0 * 8:(i0 + n) * 8, 3:3 + H].rearrange("p (b e) h -> p b e h", e=8)
            eb_free[e] = by_dve.of(dve.tensor_tensor(out, eb, be_row[:].unsqueeze(1).unsqueeze(1).to_broadcast([P, n, 8, H]), ALU.add))
            wait(sp, eb_free[e], fields_set)
            return out_rec.of(sp.dma_start(rec_view[:, 8 * i0:8 * (i0 + n)], rec[:, 8 * i0:8 * (i0 + n)]), 16)

        moments = stats[:, 6 * NT:8 * NT].rearrange("p (t two) -> p t two", two=2)
        parts_seen = [0]

        def norm_part():
            i = parts_seen[0]
            parts_seen[0] += 1
            wait(dve, x_got[i])
            for t in range(4 * i, 4 * i + 4):
                mark = by_dve.of(dve.bn_stats(stats[:, 6 * t:6 * t + 6], x_part[:, i % 2, t % 4]))
            if i + 2 < NT // 4:
                wait(sp, mark)
                x_got.append(in_x[i % 2].of(sp.dma_start(x_part[:, i % 2], x_view[:, 4 * i + 8:4 * i + 12, :]), 16))
            wait(dve, mark)
            for t in range(4 * i, 4 * i + 4):
                by_dve.of(dve.bn_aggr(moments[:, t, :], stats[:, 6 * t:6 * t + 6]))

        made_iota = by_pool.of(pool.iota(iota_hist[:], pattern=[[1, GN], [0, HIST]], base=0, channel_multiplier=0, allow_small_or_imprecise_dtypes=True))
        make_constants(nc, keep)
        wait(dve, made_iota, got_dst)
        by_dve.of(dve.tensor_scalar(graph_i[:], dst_i[:], 6, None, ALU.logical_shift_right))
        p_i = by_dve.of(dve.tensor_scalar(class_i[:], dst_i[:], GN - 1, None, ALU.bitwise_and))
        wait(dve, p_i)
        by_dve.of(dve.tensor_copy(graph_key[:], graph_i[:]))
        keys = by_dve.of(dve.tensor_copy(class_key[:], class_i[:]))
        wait(dve, keys)
        used, hots = [None, None], {}

        def hist_hots(c):
            wait(dve, used[c % 2])
            cols = slice(c * HIST, (c + 1) * HIST)
            by_dve.of(dve.tensor_tensor(graph_hot[:, c % 2], iota_hist[:, 0:NGRAPH],
                                        graph_key[:, cols].unsqueeze(1).to_broadcast([P, NGRAPH, HIST]), ALU.is_equal))
            hots[c] = by_dve.of(dve.tensor_tensor(class_hot[:, c % 2], iota_hist[:],
                                                  class_key[:, cols].unsqueeze(1).to_broadcast([P, GN, HIST]), ALU.is_equal))
        hist_hots(0)
        HIST_STEPS = EPP // HIST
        for c in range(HIST_STEPS):
            if c + 1 < HIST_STEPS:
                hist_hots(c + 1)
            wait(pe, hots[c])
            for j in range(HIST):
                mm = pe.matmul(hist_ps[0:NGRAPH, 0:GN], graph_hot[:, c % 2, :, j], class_hot[:, c % 2, :, j],
                               start=c == 0 and j == 0, stop=c == HIST_STEPS - 1 and j == HIST - 1)
            used[c % 2] = by_pe.of(mm)
            if c == 2:
                wait(pool, got_src, got_w, got_dst)
                by_pool.of(pool.tensor_copy(rec[:, :, 0], src_i[:]))
                by_pool.of(pool.tensor_copy(rec[:, :, 1], dst_i[:]))
                fields_set = by_pool.of(pool.tensor_copy(rec[:, :, 2], ew[:]))
            if c >= 3:
                edge_bias(8 * (c - 3))
            if c >= 6:
                norm_part()

        cnt, ones, base, end, first = (small[0:NGRAPH, i * GN:(i + 1) * GN] for i in range(5))
        low = small[:, 6 * GN:6 * GN + NGRAPH]
        row, viol, flag, rounds, span_max, viol_all, span_all = (small[:, 7 * GN + i:7 * GN + i + 1] for i in range(7))
        span_i = small_i[0:NGRAPH, 0:GN]
        wait(dve, used[(HIST_STEPS - 1) % 2])
        cnt_set = a = by_dve.of(dve.tensor_copy(cnt, hist_ps[0:NGRAPH, 0:GN]))
        by_dve.of(dve.memset(ones, 1.0))
        b = by_dve.of(dve.memset(low, 1.0))
        wait(dve, a, b)
        a = by_dve.of(dve.tensor_reduce(row[0:NGRAPH], cnt, axis=AX.X, op=ALU.add))
        edge_bias(40)
        wait(pool, b)
        lowered = by_pool.of(pool.affine_select(out=low[0:NGRAPH], in_=low[0:NGRAPH], compare_op=ALU.is_gt, fill=0.0, base=0,
                                                pattern=[[1, NGRAPH]], channel_multiplier=-1))
        wait(pe, a, lowered)
        c0 = by_pe.of(pe.matmul(misc_ps[0:NGRAPH, 0:1], low[0:NGRAPH], row[0:NGRAPH], start=True, stop=True))
        wait(dve, c0)
        a = by_dve.of(dve.tensor_copy(base[:, 0:1], misc_ps[0:NGRAPH, 0:1]))
        wait(dve, a)
        a = by_dve.of(dve.tensor_tensor_scan(end, ones, cnt, base[:, 0:1], ALU.mult, ALU.add))
        wait(dve, a)
        a = by_dve.of(dve.tensor_tensor(first, end, cnt, ALU.subtract))
        wait(dve, a)
        a = by_dve.of(dve.tensor_scalar(span_i, cnt, float(WHALF - 1), None, ALU.add))
        wait(dve, a)
        a = by_dve.of(dve.tensor_scalar(span_i, span_i, 6, None, ALU.logical_shift_right))
        wait(dve, a)
        a = by_dve.of(dve.memset(span_max, 0.0))
        wait(dve, a)
        a = by_dve.of(dve.tensor_reduce(span_max[0:NGRAPH], span_i, axis=AX.X, op=ALU.max))
        wait(dve, got_next)
        b = by_dve.of(dve.tensor_tensor(step_f[:], dst_i[:], dst_next[:], ALU.subtract))
        wait(dve, b)
        b = by_dve.of(dve.tensor_reduce(viol, step_f[:], axis=AX.X, op=ALU.max))
        wait(pool, a, b)
        RMAX = bass.bass_isa.ReduceOp.max
        by_pool.of(pool.partition_all_reduce(viol_all, viol, P, RMAX))
        alls = by_pool.of(pool.partition_all_reduce(span_all, span_max, P, RMAX))
        wait(dve, alls)
        a = by_dve.of(dve.tensor_scalar(flag, viol_all, 0.0, None, ALU.is_le))
        b = by_dve.of(dve.tensor_scalar(rounds, span_all, 1.0, -float(E // WHALF), ALU.max, ALU.add))
        wait(dve, a, b)
        a = by_dve.of(dve.tensor_tensor(rounds, rounds, flag, ALU.mult))
        b = by_dve.of(dve.tensor_scalar(first, first, flag[0:NGRAPH], None, ALU.mult))
        wait(dve, a, b)
        keep["rounds_set"] = by_dve.of(dve.tensor_scalar(keep["rounds"][0:1, :], rounds[0:1], float(E // WHALF), None, ALU.add))
        edge_bias(48)
        wait(pe, b, cnt_set, keep["constants"])
        for z in range(2):
            mm = pe.matmul(misc_ps[z * GN:(z + 1) * GN, 256:256 + NT], cnt, ident[0:NGRAPH, 0:NGRAPH].rearrange("g (t z) -> g z t", z=2)[:, z],
                           start=True, stop=True)
        a = by_pe.of(mm)
        dis1 = keep["dis1"]
        wait(dve, a)
        a = by_dve.of(dve.tensor_scalar(dis1[:], misc_ps[:, 256:256 + NT], 1.0, 1.0, ALU.add, ALU.max))
        wait(act, a)
        a = by_act.of(act.sqrt(dis1[:], dis1[:]))
        wait(dve, a)
        by_dve.of(dve.reciprocal(dis1[:], dis1[:]))
        mask = small[:, 8 * GN:9 * GN]
        chosen = small[:, 9 * GN:10 * GN]
        start_at = keep["starts"][:].rearrange("p (t z) -> p t z", z=2)
        graph_of = small[0:NGRAPH, 11 * GN:11 * GN + 2 * P].rearrange("p (z n) -> p z n", z=2)
        edge_bias(56)
        norm_part()
        m0 = by_pool.of(pool.memset(mask, 1.0))
        wait(pool, m0)
        m0 = by_pool.of(pool.affine_select(out=mask, in_=mask, compare_op=ALU.is_ge, fill=0.0, base=0,
                                           pattern=[[0, GTILES], [-HGRAPH, CPT]], channel_multiplier=1))
        wait(pool, m0)
        masked = by_pool.of(pool.affine_select(out=mask, in_=mask, compare_op=ALU.is_ge, fill=0.0, base=HGRAPH - 1,
                                               pattern=[[0, GTILES], [HGRAPH, CPT]], channel_multiplier=-1))
        wait(dve, keep["constants"])
        for z in range(2):
            a = by_dve.of(dve.tensor_copy(graph_of[:, z].rearrange("p (c b) -> p c b", c=CPT),
                                          ident[0:NGRAPH, z * HGRAPH:(z + 1) * HGRAPH].unsqueeze(1).to_broadcast([NGRAPH, CPT, HGRAPH])))
        wait(pe, a, b)
        for z in range(2):
            mm = pe.matmul(misc_ps[:, 8 + z * GN:8 + (z + 1) * GN], graph_of[:, z], first, start=True, stop=True)
        spread = by_pe.of(mm)
        wait(dve, spread, masked)
        for z in range(2):
            a = by_dve.of(dve.tensor_tensor(chosen, misc_ps[:, 8 + z * GN:8 + (z + 1) * GN], mask, ALU.mult))
            wait(dve, a)
            a = by_dve.of(dve.tensor_reduce(start_at[:, :, z:z + 1], chosen.rearrange("p (t c) -> p t c", t=GTILES), axis=AX.X, op=ALU.add))
            wait(dve, a)

        padded = by_dve.of(dve.memset(pad[:], -1.0))
        wait(sp, padded)
        out_rec.of(sp.dma_start(io["rec_dram"][E:E + WHALF, :].rearrange("e f -> (e f)").unsqueeze(0), pad[:]), 16)
        stored = edge_bias(64)
        norm_part()
        scales_from_moments(nc, by_dve, by_act, moments, keep["rstd"], keep["shift"])
        wait(sp, stored)
        nc.all_engine_barrier()


def build_matrices(nc, io, keep):
    pool = nc.gpsimd
    with ExitStack() as mem:
        sb = lambda *a: mem.enter_context(nc.sbuf_tensor(*a))
        ps = lambda *a: mem.enter_context(nc.psum_tensor(*a))
        place = keep["x"][:].rearrange("p t d -> p (t d)").bitcast(BF16)
        n_src = 2 * P * BATCH
        room = {
            "gathered": sb("gathered", [P, 2, WHALF * FIELDS], F32),
            "fields": sb("fields", [P, FIELDS, P], F32),
            "ints": sb("ints", [P, 3, P], I32),
            "keys": sb("keys", [P, 2, 2, P], BF16),
            "eb_parts": sb("eb_parts", [P, 2, PARTS, H + 1, P], BF16),
            "idx_f": sb("idx_f", [P, GTILES * 2], F32),
            "idx": sb("idx", [P, GTILES * 2], U32),
            "hot_src": place[:, 0:n_src].rearrange("p (z c g) -> p z c g", z=2, g=BATCH),
            "hot_eb": place[:, n_src:n_src + 2 * PARTS * H * NT * BATCH].rearrange("p (z h s g) -> p z h s g", z=2, s=NT, g=BATCH),
            "hot_tile": sb("hot_tile", [P, 2, NT, BATCH], BF16),
            "hot_cnt": sb("hot_cnt", [P, 2, CCOLS, BATCH], BF16),
            "hot_w": sb("hot_w", [P, 2, PARTS, CCOLS, BATCH], BF16),
            "w_slab": sb("w_slab", [P, 2, P, NT], F32),
            "w_old": sb("w_old", [P, 2, 512], F32),
            "w_new": sb("w_new", [P, 2, 512], F32),
            "turn_ps": ps("turn2_ps", [P, 2, 512], F32),
            "cnt_ps": ps("cnt_ps", [P, 2, 512], F32),
            "w_ps": ps("w_ps", [P, 2, 512], F32),
            "bias_ps": ps("bias_ps", [P, 2, 512], F32),
        }
        names = ("pe", "dve", "act", "pool", "gather", "old0", "old1", "store0", "store1")
        first = {n: Signals(nc, f"first_{n}") for n in names}
        later = {n: Signals(nc, f"later_{n}") for n in names}
        nc.all_engine_barrier()
        rounds = nc.values_load(keep["rounds"][0:1, :], min_val=1, max_val=ROUNDS_MAX)
        build_round(nc, io, keep, room, first, True)
        nc.all_engine_barrier()
        nums = [later[n].sem.num for n in names]
        assert nums == list(range(nums[0], nums[0] + len(nums)))
        with nc.If(rounds > 1):
            with nc.Fori(1, rounds):
                build_round(nc, io, keep, room, later, False)
                nc.all_engine_barrier()
                pool.dma_reset(range(nums[0], nums[-1] + 1))
                pool.sem_clear(range(nums[0], nums[-1] + 1))
                nc.all_engine_barrier()


def build_round(nc, io, keep, room, signals, first):
    pe, dve, act, pool, sp = nc.tensor, nc.vector, nc.scalar, nc.gpsimd, nc.sync
    ident, count, bias, starts = keep["ident"], keep["count"], keep["bias"], keep["starts"]
    by_pe, by_dve, by_act, by_pool = (signals[x] for x in ("pe", "dve", "act", "pool"))
    d0, iota_rep, iota_cnt = keep["d0"], keep["iota_rep"], keep["iota_cnt"]
    gathered, fields, ints, keys, eb_parts, idx_f, idx = (
        room[x] for x in ("gathered", "fields", "ints", "keys", "eb_parts", "idx_f", "idx"))
    hot_src, hot_eb, hot_tile, hot_cnt, hot_w = (room[x] for x in ("hot_src", "hot_eb", "hot_tile", "hot_cnt", "hot_w"))
    w_slab, w_old, w_new, turn_ps, cnt_ps, w_ps, bias_ps = (
        room[x] for x in ("w_slab", "w_old", "w_new", "turn_ps", "cnt_ps", "w_ps", "bias_ps"))
    dlocal = fields[:, 1, :]

    a = by_dve.of(dve.tensor_scalar(idx_f[:], starts[:], float(E), float(FIELDS), ALU.min, ALU.mult))
    wait(dve, a)
    indexed = by_dve.of(dve.tensor_copy(idx[:], idx_f[:]))
    by_dve.of(dve.tensor_scalar(starts[:], starts[:], float(WHALF), None, ALU.add))
    records = io["rec_dram"].rearrange("e f -> (e f)").unsqueeze(1)

    gather_read = [None]
    turned_free = [None, None]
    fields_free = evacuated = None
    parts_done = [None, None]
    parts_free = [(), ()]
    got = [None]

    def gather(t):
        wait(pool, indexed, gather_read[0])
        for z in range(2):
            g = pool.indirect_dma_start(gathered[:, z, :], None, records,
                                        bass.IndirectOffsetOnAxis(ap=idx[:, 2 * t + z:2 * t + z + 1], axis=0))
            got[0] = signals["gather"].of(g, 16)

    def prep_fields(t):
        nonlocal evacuated
        wait(pe, got[0])
        view = gathered[:].rearrange("p z (e f) -> p f (z e)", f=FIELDS)
        for f0 in range(0, FIELDS, 4):
            n = min(4, FIELDS - f0)
            bank = (f0 // 4) % 2
            wait(pe, turned_free[bank])
            for f in range(n):
                mm = pe.transpose(turn_ps[:, bank, f * P:(f + 1) * P], view[:, f0 + f], ident[:])
            gather_read[0] = by_pe.of(mm)
            wait(act, gather_read[0], fields_free)
            evacuated = turned_free[bank] = by_act.of(act.copy(
                fields[:, f0:f0 + n, :], turn_ps[:, bank, 0:n * P].rearrange("p (f g) -> p f g", f=n)))

    def prep_keys(t):
        s = t % 2
        wait(dve, evacuated, *parts_free[s])
        a = by_dve.of(dve.tensor_copy(ints[:, 0], fields[:, 0, :]))
        b = by_dve.of(dve.scalar_tensor_tensor(dlocal, fields[:, 1, :], -float(t * CPT), d0[:], ALU.add, ALU.subtract))
        wait(dve, a)
        by_dve.of(dve.tensor_scalar(ints[:, 1], ints[:, 0], P - 1, None, ALU.bitwise_and))
        a = by_dve.of(dve.tensor_scalar(ints[:, 2], ints[:, 0], 7, None, ALU.logical_shift_right))
        wait(dve, a, b)
        by_dve.of(dve.tensor_copy(keys[:, s, 0], ints[:, 1]))
        parts_done[s] = by_dve.of(dve.scalar_tensor_tensor(keys[:, s, 1], dlocal, float(P), ints[:, 2], ALU.mult, ALU.add))

    def part_copy(t, p):
        s = t % 2
        wait(act, evacuated, residual[0], *parts_free[s])
        copied[0] = by_act.of(act.copy(eb_parts[:, s, p], fields[:, 2:FIELDS, :]))

    def part_residual(t, p):
        nonlocal fields_free
        s = t % 2
        source = fields[:, 2:FIELDS, :]
        wait(dve, copied[0])
        residual[0] = by_dve.of(dve.tensor_tensor(source if p == 0 else eb_parts[:, s, 2], source, eb_parts[:, s, p], ALU.subtract))
        if p == 1:
            fields_free = parts_done[s] = residual[0]

    copied, residual = [None], [None]
    hot_free = [None, None]
    ps_free = [(), ()]
    slab_free, slab_done = [None, None], [None, None]
    made = {}

    def hots(n):
        t, i = divmod(n, NBATCH)
        s, ts = n % 2, t % 2
        cols = slice(i * BATCH, (i + 1) * BATCH)

        def key(k, c):
            return keys[:, ts, k, cols].unsqueeze(1).to_broadcast([P, c, BATCH])
        wait(dve, hot_free[s], parts_done[ts])
        in_tile = by_dve.of(dve.tensor_tensor(hot_tile[:, s], iota_rep[:, 0:NT], key(1, NT), ALU.is_equal))
        counted = by_dve.of(dve.tensor_tensor(hot_cnt[:, s], iota_cnt[:], key(1, CCOLS), ALU.is_equal))
        wait(pool, hot_free[s], in_tile, parts_done[ts])

        def product(eng, by, p, h0=0, h1=H):
            wide = [P, h1 - h0, NT, BATCH]
            return by.of(eng.tensor_tensor(
                hot_eb[:, s, p * H + h0:p * H + h1], hot_tile[:, s].unsqueeze(1).to_broadcast(wide),
                eb_parts[:, ts, p, 1 + h0:1 + h1, cols].unsqueeze(2).to_broadcast(wide), ALU.mult))
        product(pool, by_pool, 2)
        e2 = product(pool, by_pool, 1, 0, POOL_HEADS)
        by_dve.of(dve.tensor_tensor(hot_src[:, s], iota_rep[:], key(0, P), ALU.is_equal))
        wait(dve, counted)
        by_dve.of(dve.tensor_tensor(
            hot_w[:, s], hot_cnt[:, s].unsqueeze(1).to_broadcast([P, PARTS, CCOLS, BATCH]),
            eb_parts[:, ts, :, 0, cols].unsqueeze(2).to_broadcast([P, PARTS, CCOLS, BATCH]), ALU.mult))
        product(dve, by_dve, 0)
        e1 = product(dve, by_dve, 1, POOL_HEADS, H)
        made[n] = (e1, e2)
        parts_free[ts] = (e1, e2)

    def products(n, units):
        s = n % 2
        wait(pe, *made[n], *ps_free[s])
        for g in units:
            hs = hot_src[:, s, :, g]
            c = slice(g * CCOLS, (g + 1) * CCOLS)
            pe.matmul(cnt_ps[:, s, c], hs, hot_cnt[:, s, :, g], start=True, stop=True)
            for p in range(PARTS):
                pe.matmul(w_ps[:, s, c], hs, hot_w[:, s, p, :, g], start=p == 0, stop=p == PARTS - 1)
            for p in range(PARTS):
                mm = pe.matmul(bias_ps[:, s, 0:H * NT], hs, hot_eb[:, s, p * H:(p + 1) * H, :, g].rearrange("p h s -> p (h s)"),
                               start=g == 0 and p == 0, stop=g == BATCH - 1 and p == PARTS - 1)
        hot_free[s] = by_pe.of(mm)

    def evacuate(n):
        s, z = n % 2, n // 4 % 2
        done = hot_free[s]
        wait(act, done, slab_free[z])
        slab = w_slab[:, z].rearrange("p (c h b) s -> p c b h s", c=4, h=2)[:, n % 4]
        from_w = w_ps[:, s].rearrange("p (b h s) -> p b h s", b=BATCH, h=2)
        slab_done[z] = by_act.of(act.copy(slab, from_w))
        to_count = count[:].rearrange("p s (h b m) -> p b h s m", h=2, m=GN)[:, :, :, :, n]
        from_count = cnt_ps[:, s].rearrange("p (b h s) -> p b h s", b=BATCH, h=2)
        to_bias, from_bias = bias[:, :, n], bias_ps[:, s, 0:H * NT]
        if first:
            by_act.of(act.copy(to_count, from_count))
            ps_free[s] = (by_act.of(act.copy(to_bias, from_bias)),)
        else:
            wait(dve, done)
            by_dve.of(dve.tensor_tensor(to_count, from_count, to_count, ALU.add))
            ps_free[s] = (slab_done[z], by_dve.of(dve.tensor_tensor(to_bias, from_bias, to_bias, ALU.add)))

    new_free, old_free, old_got = [None, None], [None, None], [None, None]

    def load_old(m):
        if m < NT * 4 and not first:
            wait(sp, old_free[m % 2])
            old_got[m % 2] = signals[f"old{m % 2}"].of(
                sp.dma_start(w_old[:, m % 2], io["weight_dram"][m // 4, :, m % 4 * 512:(m % 4 + 1) * 512]), 16)

    def weight_chunk(m):
        q, c = divmod(m, 4)
        bank = m % 2
        wait(pe, slab_done[q % 2], turned_free[bank])
        for s1 in range(4):
            mm = pe.transpose(turn_ps[:, bank, s1 * P:(s1 + 1) * P], w_slab[:, q % 2, :, c * 4 + s1], ident[:])
        slab_free[q % 2] = by_pe.of(mm)
        if first:
            wait(act, slab_free[q % 2], new_free[bank])
            turned_free[bank] = by_act.of(act.copy(w_new[:, bank], turn_ps[:, bank]))
        else:
            wait(dve, slab_free[q % 2], old_got[bank], new_free[bank])
            old_free[bank] = turned_free[bank] = by_dve.of(dve.tensor_tensor(w_new[:, bank], turn_ps[:, bank], w_old[:, bank], ALU.add))
        load_old(m + 2)
        wait(sp, turned_free[bank])
        new_free[bank] = signals[f"store{bank}"].of(sp.dma_start(io["weight_dram"][q, :, c * 512:(c + 1) * 512], w_new[:, bank]), 16)

    load_old(0)
    load_old(1)
    gather(0)
    prep_fields(0)
    gather(1)
    part_copy(0, 0)
    prep_keys(0)
    part_residual(0, 0)
    part_copy(0, 1)
    part_residual(0, 1)
    hots(0)
    last = GTILES * NBATCH - 1
    for n in range(last + 1):
        t, i = divmod(n, NBATCH)
        if n < last:
            hots(n + 1)
        if t + 1 < GTILES:
            if i == 4:
                prep_fields(t + 1)
                part_copy(t + 1, 0)
            if i == 5:
                if t + 2 < GTILES:
                    gather(t + 2)
                prep_keys(t + 1)
                part_residual(t + 1, 0)
                part_copy(t + 1, 1)
            if i == 6:
                part_residual(t + 1, 1)
        products(n, range(BATCH // 2))
        if n >= 4:
            weight_chunk(n - 4)
        products(n, range(BATCH // 2, BATCH))
        evacuate(n)
    for m in range(NT * 4 - 4, NT * 4):
        weight_chunk(m)
    wait(sp, *((signals[x], signals[x].value) for x in ("old0", "old1", "store0", "store1") if signals[x].value))


def weight_view(w):
    return w.rearrange("(k p) n -> p k n", p=P)


def column_view(v):
    return v.rearrange("(k p) -> p k", p=P)


def attention(nc, io, keep):
    pe, dve, act, pool, sp = nc.tensor, nc.vector, nc.scalar, nc.gpsimd, nc.sync
    ident, x, rstd, shift = keep["ident"], keep["x"], keep["rstd"], keep["shift"]
    bias = keep["bias"][:].rearrange("p (h t) m -> p h t m", h=H)
    by_pe, by_dve, by_act, by_pool = (Signals(nc, f"att_{n}") for n in ("pe", "dve", "act", "pool"))
    with ExitStack() as mem:
        sb = lambda *a: mem.enter_context(nc.sbuf_tensor(*a))
        ps = lambda *a: mem.enter_context(nc.psum_tensor(*a))
        wq = keep["wq"]
        wk, wv, wo = (sb(f"w{n}_sb", [P, KT, D], F32) for n in "kvo")
        bq_col, bk_col, bv_row, bo_row, got_b = (keep[n] for n in ("bq_col", "bk_col", "bv_row", "bo_row", "got_b"))
        h = sb("h0", [P, 2, D], F32)
        h_t = sb("h0_t", [P, KT, 2 * P], F32)
        q_t = sb("q_t", [P, KT, 2 * P], F32)
        k_t = sb("k_t", [P, KT, 2 * P], F32)
        v = sb("v", [P, 2, 2, D], F32)
        prob = sb("prob", [P, 2, D + GN], F32)
        prob_t = sb("prob_t", [P, 2, D], F32)
        att_t = sb("att_t", [P, KT, P], F32)
        stats = sb("stats1", [P, 8 * NT], F32)
        moments = stats[:, 6 * NT:8 * NT].rearrange("p (t two) -> p t two", two=2)
        row_max, row_sum = sb("row_max", [P, 2, H], F32), sb("row_sum", [P, 2, H], F32)
        proj_ps = ps("proj_ps", [P, 2, 512], F32)
        s_ps = ps("s_ps", [P, 2, 2, H // 2 * GN], F32)
        pt_ps = ps("pt_ps", [P, 2, 512], F32)
        av_ps = ps("av_ps", [P, 2, 512], F32)

        SLABS = NT // 2
        x_view = io["x"].rearrange("(t p) d -> p t d", p=P)
        x_got = {}

        def load_x(slab):
            x_got[slab] = Signals(nc, f"in_x{slab}").of(sp.dma_start(x[:, 2 * slab:2 * slab + 2, :], x_view[:, 2 * slab:2 * slab + 2, :]), 16)
        load_x(0)
        in_w = {"q": keep["got_wq"]}
        for n, w in (("k", wk), ("v", wv), ("o", wo)):
            in_w[n] = Signals(nc, f"in_w{n}").of(act.dma_start(w[:], weight_view(io[f"L0_gnn_W{n}"])), 16)
        load_x(1)
        wait(sp, in_w["v"])
        for slab in range(2, SLABS):
            load_x(slab)

        scale = float(HD) ** -0.5
        wait(dve, got_b)
        bq_scaled = by_dve.of(dve.tensor_scalar(bq_col[:], bq_col[:], scale, None, ALU.mult))
        wait(act, bq_scaled)

        h_t_free = att_t_free = prob_t_free = qk_free = s_free = None
        h_free, proj_free, prob_free, v_free = ([None, None] for _ in range(4))
        pt_free, prob_done, av_free, lowered = ([None, None] for _ in range(4))
        proj_n = 0
        slab_done = [[], []]
        x_plus = {}

        def project(slab):
            nonlocal h_t_free, proj_n
            z = slab % 2
            for j in range(2):
                t = 2 * slab + j
                wait(act, x_got[slab], h_free[j])
                relued = by_act.of(act.activation(h[:, j], x[:, t, :], ACT.Relu, bias=shift[:, t:t + 1], scale=rstd[:, t:t + 1]))
                wait(pool, relued, got_b)
                x_plus[t] = by_pool.of(pool.tensor_tensor(x[:, t, :], x[:, t, :], bo_row[:], ALU.add))
                wait(pe, relued, pt_free[j])
                for k in range(KT):
                    mm = pe.transpose(pt_ps[:, j, k * P:(k + 1) * P], h[:, j, k * P:(k + 1) * P], ident[:])
                h_free[j] = by_pe.of(mm)
                wait(act, h_free[j], h_t_free)
                pt_free[j] = turned = by_act.of(act.copy(h_t[:, :, j * P:(j + 1) * P], pt_ps[:, j].rearrange("p (k n) -> p k n", k=KT)))
                yield
            wait(pe, turned)
            done = []
            for w, n in ((wq, "q"), (wk, "k")):
                for m in range(KT):
                    s = proj_n % 2
                    proj_n += 1
                    wait(pe, in_w[n], proj_free[s])
                    for k in range(KT):
                        mm = pe.matmul(proj_ps[:, s, 0:2 * P], w[:, k, m * P:(m + 1) * P], h_t[:, k, :], start=k == 0, stop=k == KT - 1)
                    a = by_pe.of(mm)
                    if n == "q":
                        wait(act, a, qk_free)
                        proj_free[s] = by_act.of(act.activation(q_t[:, m, :], proj_ps[:, s, 0:2 * P], ACT.Identity,
                                                                bias=bq_col[:, m:m + 1], scale=scale))
                    else:
                        wait(dve, a, qk_free)
                        proj_free[s] = by_dve.of(dve.tensor_scalar(k_t[:, m, :], proj_ps[:, s, 0:2 * P], bk_col[:, m:m + 1], None, ALU.add))
                    if m == KT - 1:
                        done.append(proj_free[s])
                    yield
            for j in range(2):
                s = proj_n % 2
                proj_n += 1
                wait(pe, in_w["v"], proj_free[s])
                for k in range(KT):
                    mm = pe.matmul(proj_ps[:, s], h_t[:, k, j * P:(j + 1) * P], wv[:, k, :], start=k == 0, stop=k == KT - 1)
                h_t_free = by_pe.of(mm)
                wait(dve, h_t_free, v_free[z])
                proj_free[s] = by_dve.of(dve.tensor_tensor(v[:, z, j, :], proj_ps[:, s], bv_row[:], ALU.add))
                if j == 1:
                    done.append(proj_free[s])
                yield
            slab_done[z] = done

        def scores(slab, j):
            nonlocal qk_free, s_free
            t = 2 * slab + j
            wait(pe, *slab_done[slab % 2], s_free)
            for g in range(2):
                nodes = slice(j * P + g * GN, j * P + (g + 1) * GN)
                for hd in range(H):
                    rows = slice(hd % 2 * HD, (hd % 2 + 1) * HD)
                    mm = pe.matmul(s_ps[g * GN:(g + 1) * GN, hd % 2, j, hd // 2 * GN:(hd // 2 + 1) * GN], q_t[rows, hd // 2, nodes],
                                   k_t[rows, hd // 2, nodes], start=True, stop=True)
            qk_free = by_pe.of(mm)
            p3 = prob[:, j, 0:D].rearrange("p (h m) -> p h m", h=H)
            wide = [P, H, GN]
            wait(dve, qk_free, prob_free[j])
            for odd in range(2):
                a = s_free = by_dve.of(dve.tensor_tensor(
                    p3.rearrange("p (h o) m -> p o h m", o=2)[:, odd], s_ps[:, odd, j].rearrange("p (h m) -> p h m", m=GN),
                    bias.rearrange("p (h o) t m -> p o h t m", o=2)[:, odd, :, t], ALU.add))
            wait(dve, a)
            a = by_dve.of(dve.tensor_reduce(row_max[:, j], p3, axis=AX.X, op=ALU.max))
            wait(dve, a)
            a = by_dve.of(dve.tensor_tensor(p3, p3, row_max[:, j].unsqueeze(2).to_broadcast(wide), ALU.subtract))
            lowered[j] = a

        def exponentials(j):
            wait(act, lowered[j])
            lowered[j] = by_act.of(act.activation(prob[:, j, 0:D], prob[:, j, 0:D], ACT.Exp))

        def probabilities(j):
            p3 = prob[:, j, 0:D].rearrange("p (h m) -> p h m", h=H)
            wait(dve, lowered[j])
            a = by_dve.of(dve.tensor_reduce(row_sum[:, j], p3, axis=AX.X, op=ALU.add))
            wait(dve, a)
            a = by_dve.of(dve.reciprocal(row_sum[:, j], row_sum[:, j]))
            wait(dve, a)
            a = by_dve.of(dve.tensor_tensor(p3, p3, row_sum[:, j].unsqueeze(2).to_broadcast([P, H, GN]), ALU.mult))
            wait(dve, a)
            prob_done[j] = by_dve.of(dve.tensor_copy(prob[:, j, D:D + GN], prob[:, j, 0:GN]))

        def mix(slab, j):
            nonlocal prob_t_free, att_t_free, proj_n
            t, z = 2 * slab + j, slab % 2
            for odd in range(2):
                wait(pe, prob_done[j], pt_free[odd])
                for i in range(KT):
                    c = i * P + odd * GN
                    mm = pe.transpose(pt_ps[:, odd, i * P:(i + 1) * P], prob[:, j, c:c + P], ident[:])
                a = prob_free[j] = by_pe.of(mm)
                wait(act, a, prob_t_free)
                pt_free[odd] = by_act.of(act.copy(prob_t[:, odd], pt_ps[:, odd]))
                yield
            wait(pe, *pt_free, *av_free)
            for g in range(2):
                rows = slice(g * GN, (g + 1) * GN)
                for hd in range(H):
                    odd = (hd + g) % 2
                    block = (hd - odd) % H // 2
                    if g == 1:
                        block = (hd - 1 - odd) % H // 2
                    mm = pe.matmul(av_ps[hd % 2 * HD:(hd % 2 + 1) * HD, g, hd // 2 * GN:(hd // 2 + 1) * GN],
                                   v[rows, z, j, hd * HD:(hd + 1) * HD],
                                   prob_t[rows, odd, block * P + g * GN:block * P + (g + 1) * GN], start=True, stop=True)
                prob_t_free = v_free[z] = by_pe.of(mm)
                wait(act, prob_t_free, att_t_free)
                av_free[g] = by_act.of(act.copy(att_t[:, :, g * GN:(g + 1) * GN], av_ps[:, g, 0:KT * GN].rearrange("p (k n) -> p k n", k=KT)))
            yield
            s = proj_n % 2
            proj_n += 1
            wait(pe, *av_free, proj_free[s], in_w["o"])
            for k in range(KT):
                mm = pe.matmul(proj_ps[:, s], att_t[:, k, :], wo[:, k, :], start=k == 0, stop=k == KT - 1)
            att_t_free = by_pe.of(mm)
            wait(dve, att_t_free, x_plus[t])
            proj_free[s] = by_dve.of(dve.tensor_tensor(x[:, t, :], x[:, t, :], proj_ps[:, s], ALU.add))
            wait(dve, proj_free[s])
            a = by_dve.of(dve.bn_stats(stats[:, 6 * t:6 * t + 6], x[:, t, :]))
            wait(dve, a)
            by_dve.of(dve.bn_aggr(moments[:, t, :], stats[:, 6 * t:6 * t + 6]))
            wait(sp, proj_free[s])
            stored[0] = out_x.of(sp.dma_start(io["x_dram"][t * P:(t + 1) * P, :], x[:, t, :]), 16)
            yield

        out_x, stored = Signals(nc, "out_x0"), [None]
        for _ in project(0):
            pass
        count = keep["count"]
        for t in range(NT):
            diag = count[:, t, t * P:(t + 1) * P]
            by_dve.of(dve.tensor_tensor(diag, diag, ident[:], ALU.add))
        ending = iter(())
        for slab in range(SLABS):
            following = project(slab + 1) if slab + 1 < SLABS else iter(())
            next(ending, None)
            next(following, None)
            scores(slab, 0)
            next(following, None)
            scores(slab, 1)
            next(following, None)
            exponentials(0)
            next(following, None)
            exponentials(1)
            probabilities(0)
            next(following, None)
            probabilities(1)
            next(following, None)
            for _ in mix(slab, 0):
                next(following, None)
            ending = mix(slab, 1)
            for _ in range(3):
                next(ending)
                next(following, None)
        next(ending)
        scales_from_moments(nc, by_dve, by_act, moments, rstd, shift)
        wait(sp, stored[0])
        nc.all_engine_barrier()


def graph_layers(nc, io, keep):
    pe, dve, act, pool, sp = nc.tensor, nc.vector, nc.scalar, nc.gpsimd, nc.sync
    ident, count = keep["ident"], keep["count"]
    by_pe, by_dve, by_act, by_pool = (Signals(nc, f"gcn_{n}") for n in ("pe", "dve", "act", "pool"))
    GROUPS, PER = 4, NT // 4
    COLS = PER * P
    with ExitStack() as mem:
        sb = lambda *a: mem.enter_context(nc.sbuf_tensor(*a))
        ps = lambda *a: mem.enter_context(nc.psum_tensor(*a))
        g = sb("g", [P, NT, 2, D], F32R)
        h_t = sb("h_gcn_t", [P, KT, N], F32)
        split = sb("split", [P, 3, KT * D], F32R)
        dis_row = sb("dis_row", [P, N], F32)
        tiles = sb("tiles", [P, PER, D], F32)
        h = sb("h_gcn", [P, 2, D], F32)
        dis1, dis2 = keep["dis1"], sb("dis2", [P, NT], F32)
        b_col = sb("b_col", [P, 2, KT], F32)
        b_row = sb("b_row", [P, D], F32)
        stats = sb("stats2", [P, 8 * PER], F32)
        rstd, shift = sb("rstd1", [P, PER], F32), sb("shift1", [P, PER], F32)
        banks = ps("banks", [P, 8, 512], F32)
        turn_ps, prod_ps, agg_ps = banks[:, 0:2], banks[:, 2:4], banks[:, 4:8]
        chunk = split[:, 0].rearrange("p (r c) -> p r c", r=4)
        h_parts = split[:, 0].rearrange("p (r z k n) -> p r z k n", r=2, z=2, k=KT)
        w_parts = split[:, 1:3].rearrange("p z (k d) -> p z k d", k=KT)
        x_view = io["x_dram"].rearrange("(t p) d -> p t d", p=P)

        in_w, in_b = Signals(nc, "in_gcn_w"), Signals(nc, "in_gcn_b")
        in_x, out_x = ([Signals(nc, f"{n}_x1_{i}") for i in range(PER)] for n in ("in", "out"))
        turn_free, prod_free, agg_free = [None] * 2, [None] * 2, [None] * PER
        chunk_free = [None] * 4
        tile_free = [[] for _ in range(PER)]
        h_free = [None, None]
        w_free = h_t_free = g_free = scales_free = None
        stored = [None] * NT
        x_got = [None] * PER

        def load_weights(name):
            for b in range(PER):
                wait(sp, *tile_free[b])
            return in_w.of(sp.dma_start(tiles[:], weight_view(io[name])), 16)

        def split_weights(k, got, place=tiles):
            wait(act, got, w_free)
            a = by_act.of(act.copy(w_parts[:, 0, k], place[:, k]))
            wait(dve, a)
            b = by_dve.of(dve.tensor_tensor(w_parts[:, 1, k], place[:, k], w_parts[:, 0, k].bitcast(F32), ALU.subtract))
            tile_free[k] = [b]
            return b

        def split_turned_weights(o, got):
            bank = o % 2
            wait(pe, got, turn_free[bank])
            for i in range(KT):
                mm = pe.transpose(turn_ps[:, bank, i * P:(i + 1) * P], tiles[:, o, i * P:(i + 1) * P], ident[:])
            turned = by_pe.of(mm)
            source = turn_ps[:, bank].rearrange("p (i o) -> p i o", i=KT)
            hi, lo = (w_parts[:, z, :, o * P:(o + 1) * P] for z in range(2))
            wait(act, turned, w_free)
            a = by_act.of(act.copy(hi, source))
            wait(dve, a)
            turn_free[bank] = by_dve.of(dve.tensor_tensor(lo, source, hi.bitcast(F32), ALU.subtract))
            tile_free[o] = [turned]
            return turn_free[bank]

        def load_x(t, b):
            wait(sp, stored[t], *tile_free[b])
            x_got[b] = in_x[b].of(sp.dma_start(tiles[:, b], x_view[:, t, :]), 16)

        def norm_scales(first, ready):
            slots = slice(first, first + len(ready))
            moments = stats[:, 6 * PER:].rearrange("p (t two) -> p t two", two=2)
            for b, mark in zip(range(first, PER), ready):
                wait(dve, mark)
                a = by_dve.of(dve.bn_stats(stats[:, 6 * b:6 * b + 6], tiles[:, b]))
            wait(dve, a)
            for b in range(slots.start, slots.stop):
                a = by_dve.of(dve.bn_aggr(moments[:, b], stats[:, 6 * b:6 * b + 6]))
            wait(dve, a, scales_free)
            a = by_dve.of(dve.tensor_scalar(rstd[:, slots], moments[:, slots, 1], LN_EPS, None, ALU.add))
            wait(act, a)
            a = by_act.of(act.sqrt(rstd[:, slots], rstd[:, slots]))
            wait(dve, a)
            a = by_dve.of(dve.reciprocal(rstd[:, slots], rstd[:, slots]))
            wait(dve, a)
            return by_dve.of(dve.scalar_tensor_tensor(shift[:, slots], moments[:, slots, 0], -1.0, rstd[:, slots], ALU.mult, ALU.mult))

        def relu_tile(b, normed, rstd_col=None, shift_col=None):
            nonlocal scales_free
            if rstd_col is None:
                rstd_col, shift_col = rstd[:, b:b + 1], shift[:, b:b + 1]
            wait(act, normed, h_free[b % 2])
            a = scales_free = by_act.of(act.activation(h[:, b % 2], tiles[:, b], ACT.Relu, bias=shift_col, scale=rstd_col))
            tile_free[b] = tile_free[b] + [a]
            return a

        def turn_tile(t, relued, by_graph):
            bank = t % 2
            wait(pe, relued, turn_free[bank])
            for k in range(KT):
                mm = pe.transpose(turn_ps[:, bank, k * P:(k + 1) * P], h[:, bank, k * P:(k + 1) * P], ident[:])
            h_free[bank] = by_pe.of(mm)
            wait(act, h_free[bank], h_t_free)
            source = turn_ps[:, bank].rearrange("p (k n) -> p k n", k=KT)
            if by_graph:
                for k in range(KT):
                    out = h_t[:, k].rearrange("p (v b) -> p v b", b=NGRAPH)[:, :, 2 * t:2 * t + 2]
                    a = by_act.of(act.copy(out, source[:, k].rearrange("p (b v) -> p v b", b=2)))
            else:
                a = by_act.of(act.copy(h_t[:, :, t * P:(t + 1) * P], source))
            turn_free[bank] = a
            return a

        split_n = 0

        def split_h(t, h_ready):
            nonlocal split_n, h_t_free
            s = split_n % 2
            split_n += 1
            hi, lo = h_parts[:, s, 0], h_parts[:, s, 1]
            source = h_t[:, :, t * P:(t + 1) * P]
            wait(act, h_ready, chunk_free[2 * s], chunk_free[2 * s + 1])
            a = by_act.of(act.copy(hi, source))
            wait(dve, a)
            h_t_free = by_dve.of(dve.tensor_tensor(lo, source, hi.bitcast(F32), ALU.subtract))
            return s, h_t_free

        def product(t, h_split, w_ready, scale, bias_row, meanwhile=lambda: None):
            nonlocal w_free
            s, split_done = h_split
            hi, lo = h_parts[:, s, 0], h_parts[:, s, 1]
            wait(pe, split_done, w_ready, prod_free[s])
            passes = [(hi, k, 0) for k in range(KT)] + [(hi, k, 1) for k in range(KT)] + [(lo, k, 0) for k in range(KT)]
            for n, (part, k, z) in enumerate(passes):
                mm = pe.matmul(prod_ps[:, s], part[:, k], w_parts[:, z, k], start=n == 0, stop=n == len(passes) - 1)
            done = by_pe.of(mm)
            w_free = chunk_free[2 * s] = chunk_free[2 * s + 1] = done
            meanwhile()
            result = prod_ps[:, s]
            if bias_row is not None:
                wait(dve, done)
                done = by_dve.of(dve.tensor_tensor(result, result, bias_row, ALU.add))
            wait(act, done, g_free)
            hi, lo = g[:, t, 0], g[:, t, 1]
            if scale is None:
                a = by_act.of(act.copy(hi, result))
                wait(dve, a)
                b = by_dve.of(dve.tensor_tensor(lo, result, hi.bitcast(F32), ALU.subtract))
            else:
                a = by_act.of(act.activation(hi, result, ACT.Copy, scale=scale[:, t:t + 1]))
                wait(dve, a)
                b = by_dve.of(dve.scalar_tensor_tensor(lo, result, scale[:, t:t + 1], hi.bitcast(F32), ALU.mult, ALU.subtract))
            prod_free[s] = b
            return b

        def products(h_ready, w_ready, scale, bias_row, before=lambda t: None, early=(), following=lambda: None):
            ready, splits = [], list(early)
            for t in range(NT + 1):
                if t < NT:
                    before(t)
                    if t >= len(early):
                        splits.append(split_h(t, h_ready[t]))
                if t > 0:
                    ready.append(product(t - 1, splits[t - 1], w_ready, scale, bias_row, *([following] if t == NT else [])))
            return ready

        chunk_read = [None] * NT

        steps = [(c, i) for c in range(GROUPS) for i in range(NT)]
        copied = {}

        def copy_chunk(n):
            if n < len(steps):
                c, i = steps[n]
                wait(dve, chunk_free[n % 4])
                copied[n] = chunk_read[i] = by_dve.of(dve.tensor_copy(chunk[:, n % 4], count[:, i, c * COLS:(c + 1) * COLS]))

        def first_chunks():
            copy_chunk(0)
            copy_chunk(1)

        def sums(g_ready, turned, finish, aside, split_next=lambda t: None):
            nonlocal g_free
            copy_chunk(2)
            for n, (c, i) in enumerate(steps):
                copy_chunk(n + 3)
                wait(pe, copied[n], g_ready[i])
                done = []
                for b in range(4):
                    if i == 0:
                        wait(pe, agg_free[b])
                    block = slice(b * P, (b + 1) * P)
                    for z in range(2):
                        lhs, rhs = (g[:, i, z, block], chunk[:, n % 4]) if turned else (chunk[:, n % 4, block], g[:, i, z])
                        mm = pe.matmul(agg_ps[:, b], lhs, rhs, start=i == 0 and z == 0, stop=i == NT - 1 and z == 1)
                    if i == NT - 1 or b == 3:
                        done.append(by_pe.of(mm))
                chunk_free[n % 4] = g_free = done[-1]
                if c == GROUPS - 1 and i == NT - 3:
                    split_next(0)
                if c == GROUPS - 1 and i == NT - 1:
                    split_next(1)
                if i == NT - 1:
                    finish(c, done)
                for f in aside.get((c, i), ()):
                    f()

        for b in range(2):
            load_x(b, b)
        w_place = h_t[:, :, N - D:N]
        got = in_w.of(sp.dma_start(w_place, weight_view(io["L1_gnn_W1"])), 16)
        for b in range(2, PER):
            load_x(b, b)
        w_ready = [split_weights(k, got, w_place) for k in range(KT)]
        h_t_free = w_ready[-1]
        for b in range(PER):
            tile_free[b] = []
        with nc.allow_non_contiguous_dma(reason="a bias by partitions"):
            in_b.of(sp.dma_start(b_col[:, 0, :], column_view(io["L1_gnn_b1"])), 16)
            in_b.of(sp.dma_start(b_col[:, 1, :], column_view(io["L1_gnn_b2"])), 16)
        got_b = in_b.of(sp.dma_start(b_row[:], io["L1_gnn_b3"].unsqueeze(0).to_broadcast([P, D])), 16)
        pair_relued = {}

        def relu_pair(pair):
            first = pair % 2 * 2
            for b in range(first, first + 2):
                t = 2 * pair + b - first
                tile_free[b] = []
                pair_relued[t] = relu_tile(b, x_got[b], keep["rstd"][:, t:t + 1], keep["shift"][:, t:t + 1])
                if t + 4 < NT:
                    load_x(t + 4, b)

        def turn_pair(pair):
            return [turn_tile(t, pair_relued[t], False) for t in (2 * pair, 2 * pair + 1)]
        relu_pair(0)
        h_ready = turn_pair(0)
        relu_pair(1)
        for c in range(GROUPS):
            for b in range(PER):
                t = c * PER + b
                mm = pe.matmul(agg_ps[:, c, b * P:(b + 1) * P], dis1[:, t:t + 1].to_broadcast([P, P]), ident[:], start=True, stop=True)
            a = by_pe.of(mm)
            wait(act, a)
            agg_free[c] = by_act.of(act.copy(dis_row[:, c * COLS:(c + 1) * COLS], agg_ps[:, c]))
        dis_row_set = agg_free[GROUPS - 1]
        h_ready += turn_pair(1)
        relu_pair(2)

        def pair_ahead(t):
            pair = t // 2 + 2
            if t % 2 == 0 and pair < NT // 2:
                h_ready.extend(turn_pair(pair))
            if t % 2 == 1 and pair + 1 < NT // 2:
                relu_pair(pair + 1)
        g_ready = products(h_ready, w_ready, dis1, None, pair_ahead, following=first_chunks)
        staged = [load_weights("L1_gnn_W2")]

        def sum_out(i):
            nonlocal dis2_done
            a = by_dve.of(dve.tensor_reduce(dis2[:, i:i + 1], count[:, i], axis=AX.X, op=ALU.add))
            if i == NT - 1:
                wait(act, a)
                a = by_act.of(act.sqrt(dis2[:], dis2[:]))
                wait(dve, a)
                dis2_done = by_dve.of(dve.reciprocal(dis2[:], dis2[:]))
        dis2_done = None

        def next_weights(split_one, after):
            w_ready.clear()
            aside = {(0, 1 + k): [lambda k=k: w_ready.append(split_one(k, staged[0]))] for k in range(KT)}
            aside[0, 5] = [after]
            return aside

        for layer in range(2):
            marks = [None] * GROUPS

            def to_h_t(c, done):
                cols = slice(c * COLS, (c + 1) * COLS)
                for k in range(KT):
                    wait(dve, done[k], h_t_free, dis_row_set)
                    wait(act, got_b)
                    agg_free[k] = by_dve.of(dve.tensor_tensor(h_t[:, k, cols], agg_ps[:, k], dis_row[:, cols], ALU.mult))
                    wait(act, agg_free[k])
                    marks[c] = by_act.of(act.activation(h_t[:, k, cols], h_t[:, k, cols], ACT.Relu, bias=b_col[:, layer, k:k + 1]))

            def stage():
                staged[0] = load_weights("L1_gnn_W3" if layer == 0 else "L2_gnn_W")
            aside = next_weights(split_weights, stage)
            if layer == 0:
                for i in range(NT):
                    aside[1 + i // 6, 1 + i % 6 * 2] = [lambda i=i: sum_out(i)]
            early = []
            sums(g_ready, True, to_h_t, aside, lambda t: early.append(split_h(t, marks[0])))
            g_ready = products([marks[t // PER] for t in range(NT)], w_ready, dis1, None, early=early, following=first_chunks)

        def sums_into_x(g_ready, split_one, finish_tile, by_graph):
            h_ready = [None] * NT
            relued, normed = {}, [None]

            def finish(c, done):
                ready = []
                for b in range(PER):
                    t = c * PER + b
                    mark = finish_tile(t, b, done[b])
                    ready.append(mark)
                    wait(sp, mark)
                    stored[t] = out_x[b].of(sp.dma_start(x_view[:, t, :], tiles[:, b]), 16)
                    tile_free[b] = [stored[t]]
                normed[0] = norm_scales(0, ready)

            def relu(b):
                relued[b] = relu_tile(b, normed[0])

            def turn(c, b):
                h_ready[c * PER + b] = turn_tile(c * PER + b, relued[b], by_graph)

            def load_group(c):
                for b in range(PER):
                    load_x(c * PER + b, b)
            aside = next_weights(split_one, lambda: load_group(0))
            for c in range(1, GROUPS):
                for b in range(PER):
                    aside[c, 3 + 2 * b] = [lambda b=b: relu(b)]
                    aside[c, 4 + 2 * b] = [lambda c=c, b=b: turn(c - 1, b)]
                aside[c, 10].append(lambda c=c: load_group(c))
            early = []
            sums(g_ready, False, finish, aside, lambda t: by_graph or early.append(split_h(t, h_ready[t])))

            def last(b):
                turn(GROUPS - 1, b)
            return h_ready, last, relu, early

        def finish_layer1(t, b, done):
            wait(pool, x_got[b], got_b)
            a = by_pool.of(pool.tensor_tensor(tiles[:, b], tiles[:, b], b_row[:], ALU.add))
            wait(dve, done, a)
            agg_free[b] = by_dve.of(dve.scalar_tensor_tensor(tiles[:, b], agg_ps[:, b], dis1[:, t:t + 1], tiles[:, b], ALU.mult, ALU.add))
            return agg_free[b]

        h_ready, last, relu_last, early = sums_into_x(g_ready, split_turned_weights, finish_layer1, False)
        wait(sp, agg_free[PER - 1])
        got_b = in_b.of(sp.dma_start(b_row[:], io["L2_gnn_b"].unsqueeze(0).to_broadcast([P, D])), 16)
        wait(dve, got_b)
        wait(act, dis2_done)

        def last_ahead(t):
            b, odd = divmod(t - 3, 2)
            if 0 <= b < PER:
                last(b) if odd else relu_last(b)
        g_ready = products(h_ready, w_ready, dis2, b_row[:], last_ahead, early, first_chunks)
        staged[0] = load_weights("L3_gnn_weight")

        def finish_layer2(t, b, done):
            wait(act, done)
            a = by_act.of(act.activation(agg_ps[:, b], agg_ps[:, b], ACT.Relu, scale=dis2[:, t:t + 1]))
            wait(dve, a, x_got[b])
            agg_free[b] = by_dve.of(dve.tensor_tensor(tiles[:, b], tiles[:, b], agg_ps[:, b], ALU.add))
            return agg_free[b]

        h_ready, last, relu_last, early = sums_into_x(g_ready, split_weights, finish_layer2, True)
        HALF = N // 2
        raw = count[:].rearrange("p t n -> p (t n)").bitcast(F32).rearrange("p (r c) -> p r c", c=HALF)
        in_raw = [Signals(nc, f"in_raw{i}") for i in range(NT)]
        raw_got, raw_free = {}, {i: chunk_read[i] for i in range(NT)}

        def load_raw(n):
            half, q = divmod(n, NT)
            wait(sp, raw_free[q])
            raw_got[n] = in_raw[q].of(sp.dma_start(raw[:, q], io["weight_dram"][q, :, half * HALF:(half + 1) * HALF]), 16)
        wait(sp, g_free)
        for n in range(NT):
            load_raw(n)
        relu_last(0)
        for b in range(PER):
            if b + 1 < PER:
                relu_last(b + 1)
            last(b)
        wait(act, *h_free)
        g_ready = products([h_ready[-1]] * NT, w_ready, None, None)
        x_all = h_t[:].rearrange("p k n -> p (k n)").rearrange("p (t d) -> p t d", d=D)
        in_x_all = Signals(nc, "in_x_all")
        wait(sp, h_t_free, *stored)
        x_all_got = in_x_all.of(sp.dma_start(x_all, x_view), 16)

        part = split[:].rearrange("p s (z c) -> p s z c", z=2)
        part_free = [[chunk_free[0], chunk_free[2], w_free]] * 3
        part_ready = {}

        def split_raw(n):
            if n >= 2 * NT:
                return
            q, s = n % NT, n % 3
            wait(act, raw_got[n], part_free[s])
            a = by_act.of(act.copy(part[:, s, 0], raw[:, q]))
            wait(dve, a)
            b = by_dve.of(dve.tensor_tensor(part[:, s, 1], raw[:, q], part[:, s, 0].bitcast(F32), ALU.subtract))
            part_ready[n] = raw_free[q] = b
            if n + NT < 2 * NT:
                load_raw(n + NT)
        for n in range(2):
            split_raw(n)
        acc_free = turn_free + prod_free + agg_free
        outs = [Signals(nc, f"out_y{i}") for i in range(PER)]
        y_free = [tile_free[b] for b in range(PER)]
        out_view = io["out"].rearrange("(t p) d -> p t d", p=P)
        for n in range(2 * NT):
            half, q = divmod(n, NT)
            split_raw(n + 2)
            wait(pe, part_ready[n], g_ready[q])
            for b in range(8):
                if q == 0:
                    wait(pe, acc_free[b])
                for z, gz in ((0, 0), (0, 1), (1, 0)):
                    mm = pe.matmul(banks[:, b], part[:, n % 3, z, b * P:(b + 1) * P], g[:, q, gz],
                                   start=q == 0 and (z, gz) == (0, 0), stop=q == NT - 1 and z == 1)
                if q == NT - 1 or b == 7:
                    done = by_pe.of(mm)
                if q == NT - 1:
                    t = half * 8 + b
                    slot = t % PER
                    wait(dve, done, x_all_got, *y_free[slot])
                    acc_free[b] = by_dve.of(dve.scalar_tensor_tensor(tiles[:, slot], banks[:, b], 0.0, x_all[:, t], ALU.max, ALU.add))
                    wait(sp, acc_free[b])
                    y_free[slot] = [outs[slot].of(sp.dma_start(out_view[:, t, :], tiles[:, slot]), 16)]
            part_free[n % 3] = [done]
        for slot in range(PER):
            wait(sp, *y_free[slot])


INPUTS = ("x", "src", "dst", "edge_attr_16", "edge_weight", "L0_gnn_Wq", "L0_gnn_bq", "L0_gnn_Wk", "L0_gnn_bk",
          "L0_gnn_Wv", "L0_gnn_bv", "L0_gnn_Wo", "L0_gnn_bo", "L0_gnn_We", "L0_gnn_be", "L1_gnn_W1", "L1_gnn_b1",
          "L1_gnn_W2", "L1_gnn_b2", "L1_gnn_W3", "L1_gnn_b3", "L2_gnn_W", "L2_gnn_b", "L3_gnn_weight")


def program(nc, io):
    io = dict(io)
    io["rec_dram"] = nc.dram_tensor("rec_dram", [E + WHALF, FIELDS], F32, kind="Internal").ap()
    io["weight_dram"] = nc.dram_tensor("weight_dram", [NT, P, N], F32, kind="Internal").ap()
    io["x_dram"] = nc.dram_tensor("x_dram", [N, D], F32, kind="Internal").ap()
    with ExitStack() as mem:
        sb = lambda *a: mem.enter_context(nc.sbuf_tensor(*a))
        keep = {
            "ident": sb("ident", [P, P], F32),
            "starts": sb("starts", [P, GTILES * 2], F32),
            "rounds": sb("rounds", [P, 1], I32),
            "rstd": sb("rstd0", [P, NT], F32),
            "shift": sb("shift0", [P, NT], F32),
            "dis1": sb("dis1", [P, NT], F32),
        }
        keep["count"] = sb("count", [P, NT, N], F16)
        with ExitStack() as edges:
            build = lambda *a: edges.enter_context(nc.sbuf_tensor(*a))
            keep["d0"] = build("d0", [P, P], F32)
            keep["iota_rep"] = build("iota_rep", [P, P, BATCH], BF16)
            keep["iota_cnt"] = build("iota_cnt", [P, CCOLS, BATCH], BF16)
            edge_prep(nc, io, keep)
            keep["bias"] = build("bias", [P, H * NT, GN], F32)
            keep["x"] = build("x_sb", [P, NT, D], F32)
            keep["wq"] = build("wq_sb", [P, KT, D], F32)
            keep["got_wq"] = Signals(nc, "in_wq").of(nc.sync.dma_start(keep["wq"][:], weight_view(io["L0_gnn_Wq"])), 16)
            keep["bq_col"], keep["bk_col"] = build("bq_col", [P, KT], F32), build("bk_col", [P, KT], F32)
            keep["bv_row"], keep["bo_row"] = build("bv_row", [P, D], F32), build("bo_row", [P, D], F32)
            in_b = Signals(nc, "in_b")
            with nc.allow_non_contiguous_dma(reason="a bias by partitions"):
                for n in "qk":
                    in_b.of(nc.sync.dma_start(keep[f"b{n}_col"][:], column_view(io[f"L0_gnn_b{n}"])), 16)
            for n in "vo":
                keep["got_b"] = in_b.of(nc.sync.dma_start(keep[f"b{n}_row"][:], io[f"L0_gnn_b{n}"].unsqueeze(0).to_broadcast([P, D])), 16)
            build_matrices(nc, io, keep)
            attention(nc, io, keep)
        graph_layers(nc, io, keep)


def kernel(**inputs):
    import concourse.bacc as bacc
    from concourse.bass_utils import run_bass_kernel_spmd

    nc = bacc.Bacc("TRN2", target_bir_lowering=False, num_devices=1)
    arrays, io = {}, {}
    for name in INPUTS:
        a = np.ascontiguousarray(inputs[name])
        arrays[f"in_{name}"] = a
        io[name] = nc.dram_tensor(f"in_{name}", a.shape, mybir.dt.from_np(a.dtype), kind="ExternalInput").ap()
    io["out"] = nc.dram_tensor("out_x", [N, D], F32, kind="ExternalOutput").ap()
    program(nc, io)
    r = run_bass_kernel_spmd(nc, [arrays], core_ids=[0])
    return r.results[0]["out_x"]
```
